# Optimizing a Trainium2 kernel written in Bass

```python
import numpy as np
import jax
import jax.numpy as jnp

def _softmax(x, axis=-1):
    return jax.nn.softmax(x, axis=axis)

def _gelu(x):
    return jax.nn.gelu(x, approximate=True)

def _silu(x):
    return jax.nn.silu(x)

def _sigmoid(x):
    return jax.nn.sigmoid(x)

def _layernorm(x, axis=-1, eps=1e-05):
    m = jnp.mean(x, axis=axis, keepdims=True)
    v = jnp.var(x, axis=axis, keepdims=True)
    return (x - m) / jnp.sqrt(v + eps)

def _scatter_add(tgt, idx, src, axis=0):
    return tgt.at[idx].add(src)

def _segment_sum(src, seg, n):
    return jax.ops.segment_sum(src, seg, n)
kernel_name = 'mk_audio_tower_d1_tok_audfeat768_r4_d96351'

def setup_inputs(seed: int=0):
    np.random.seed(seed)
    _w = jnp.asarray

    def _rec_inputs():
        import jax
        import jax.numpy as jnp
        _rk = jax.random.key(seed)
        x = 0.000106427 + 1.00001 * jax.random.normal(jax.random.fold_in(_rk, 1), (32, 750, 192), jnp.float32)
        return x
    x = _rec_inputs()

    def _L0_tok_setup():
        import jax, jax.numpy as jnp
        import numpy as np
        D_MODEL = 192
        SEGMENT_SIZE = 128
        DILATION_RATE = 2
        key = jax.random.key(seed)
        x = jax.random.normal(key, (4, 4096, D_MODEL), dtype=jnp.float32)
        return {'x': x}
    _L0_tok_all = _L0_tok_setup()
    _L0_tok_in = {k: v for k, v in _L0_tok_all.items() if k in ()}
    del _L0_tok_all

    def _L0_attn_setup():
        import math
        import jax, jax.numpy as jnp
        import numpy as np
        H, D_MODEL, D_K, D_V, SEQ, BATCH = (12, 192, 64, 64, 512, 4)
        key = jax.random.key(seed)
        k1, k2, k3, k4, k5 = jax.random.split(key, 5)
        s = math.sqrt(0.02)
        return {'residual': jax.random.normal(k1, (BATCH, SEQ, D_MODEL), dtype=jnp.float32), 'W_Q': jax.random.normal(k2, (H, D_MODEL, D_K), dtype=jnp.float32) * s, 'W_K': jax.random.normal(k3, (H, D_MODEL, D_K), dtype=jnp.float32) * s, 'W_V': jax.random.normal(k4, (H, D_MODEL, D_V), dtype=jnp.float32) * s, 'W_O': jax.random.normal(k5, (H * D_V, D_MODEL), dtype=jnp.float32) * s}
    _L0_attn_all = _L0_attn_setup()
    _L0_attn_in = {k: v for k, v in _L0_attn_all.items() if k in ('W_Q', 'W_K', 'W_V', 'W_O')}
    del _L0_attn_all

    def _L0_ffn_setup():
        import jax, jax.numpy as jnp
        import numpy as np
        DIM = 192
        NUM_EXPERTS = 8
        TOP_K = 2
        MLP_RATIO = 4
        CAPACITY_RATIO = 1.25
        key = jax.random.key(seed)
        ks = jax.random.split(key, 6)
        B, N, C = (16, 256, DIM)
        H = MLP_RATIO * C
        s_in = 1.0 / np.sqrt(C)
        s_h = 1.0 / np.sqrt(H)
        return {'x': jax.random.normal(ks[0], (B, N, C), dtype=jnp.float32), 'Wg': jax.random.normal(ks[1], (C, NUM_EXPERTS), dtype=jnp.float32) * s_in, 'W1': jax.random.normal(ks[2], (NUM_EXPERTS, C, H), dtype=jnp.float32) * s_in, 'b1': jnp.zeros((NUM_EXPERTS, H), dtype=jnp.float32), 'W2': jax.random.normal(ks[3], (NUM_EXPERTS, H, C), dtype=jnp.float32) * s_h, 'b2': jnp.zeros((NUM_EXPERTS, C), dtype=jnp.float32)}
    _L0_ffn_all = _L0_ffn_setup()
    _L0_ffn_in = {k: v for k, v in _L0_ffn_all.items() if k in ('Wg', 'W1', 'b1', 'W2', 'b2')}
    del _L0_ffn_all
    return {'x': x, 'L0_attn_W_Q': _L0_attn_in['W_Q'], 'L0_attn_W_K': _L0_attn_in['W_K'], 'L0_attn_W_V': _L0_attn_in['W_V'], 'L0_attn_W_O': _L0_attn_in['W_O'], 'L0_ffn_Wg': _L0_ffn_in['Wg'], 'L0_ffn_W1': _L0_ffn_in['W1'], 'L0_ffn_b1': _L0_ffn_in['b1'], 'L0_ffn_W2': _L0_ffn_in['W2'], 'L0_ffn_b2': _L0_ffn_in['b2']}

def reference(x, L0_attn_W_Q, L0_attn_W_K, L0_attn_W_V, L0_attn_W_O, L0_ffn_Wg, L0_ffn_W1, L0_ffn_b1, L0_ffn_W2, L0_ffn_b2):
    import jax
    import jax.numpy as jnp

    def _L0_tok_ref(x):
        import jax, jax.numpy as jnp
        import numpy as np
        D_MODEL = 192
        SEGMENT_SIZE = 128
        DILATION_RATE = 2
        B, S, D = x.shape
        pad = -S % SEGMENT_SIZE
        if pad:
            x = jnp.pad(x, ((0, 0), (0, pad), (0, 0)))
        xs = x.reshape(B, -1, SEGMENT_SIZE, D)[:, :, ::DILATION_RATE, :]
        scale = 1.0 / jnp.sqrt(jnp.asarray(D, dtype=x.dtype))
        scores = jnp.einsum('bnqd,bnkd->bnqk', xs, xs) * scale
        attn = jax.nn.softmax(scores, axis=-1)
        out = jnp.einsum('bnqk,bnkd->bnqd', attn, xs)
        return out.reshape(B, -1, D)

    def _L0_attn_ref(residual, W_Q, W_K, W_V, W_O):
        import math
        import jax, jax.numpy as jnp
        import numpy as np
        H, D_MODEL, D_K, D_V, SEQ, BATCH = (12, 192, 64, 64, 512, 4)
        B, S, _ = residual.shape
        Q = jnp.einsum('hmk,bsm->hbsk', W_Q, residual)
        K = jnp.einsum('hmk,bsm->hbsk', W_K, residual)
        V = jnp.einsum('hmv,bsm->hbsv', W_V, residual)
        QK = jnp.einsum('hbqk,hbsk->hbqs', Q, K)
        causal = jnp.triu(jnp.ones((S, S), dtype=bool), k=1)
        mask = jnp.where(causal, -jnp.inf, 0.0).astype(QK.dtype)
        soft = jax.nn.softmax((QK + mask) / math.sqrt(D_K), axis=-1)
        attn = jnp.einsum('hbqs,hbsv->hbqv', soft, V)
        multi_head = jnp.transpose(attn, (1, 2, 0, 3)).reshape(B, S, -1)
        return jnp.einsum('nd,bqn->bqd', W_O, multi_head)

    def _L0_ffn_ref(x, Wg, W1, b1, W2, b2):
        import jax, jax.numpy as jnp
        import numpy as np
        DIM = 192
        NUM_EXPERTS = 8
        TOP_K = 2
        MLP_RATIO = 4
        CAPACITY_RATIO = 1.25
        B, N, C = x.shape
        E = W1.shape[0]
        K = TOP_K
        T = B * N
        cap = int(CAPACITY_RATIO * T * K / E)
        xf = x.reshape(T, C)
        logits = xf @ Wg
        topv, topi = jax.lax.top_k(logits, K)
        w = jax.nn.softmax(topv, axis=-1)
        priority = w[:, 0]
        order = jnp.argsort(-priority)
        e_ids = topi[order].reshape(T * K)
        w_ord = w[order].reshape(T * K)
        tok_rep = jnp.repeat(order, K)
        oh = jax.nn.one_hot(e_ids, E, dtype=jnp.int32)
        pos = (jnp.cumsum(oh, axis=0) * oh).sum(-1) - 1
        keep = pos < cap
        slot = jnp.where(keep, e_ids * cap + pos, E * cap)
        buf = jnp.zeros((E * cap + 1, C), xf.dtype).at[slot].set(xf[tok_rep])
        buf_e = buf[:E * cap].reshape(E, cap, C)
        h = jax.nn.gelu(jnp.einsum('ecd,edh->ech', buf_e, W1) + b1[:, None, :], approximate=False)
        out = jnp.einsum('ech,ehd->ecd', h, W2) + b2[:, None, :]
        out_flat = jnp.concatenate([out.reshape(E * cap, C), jnp.zeros((1, C), xf.dtype)], axis=0)
        y_assign = out_flat[slot] * (w_ord * keep.astype(xf.dtype))[:, None]
        y = jnp.zeros((T, C), xf.dtype).at[tok_rep].add(y_assign)
        return y.reshape(B, N, C)
    h = _L0_tok_ref(x)
    h = h + _L0_attn_ref(_layernorm(h, axis=-1), L0_attn_W_Q, L0_attn_W_K, L0_attn_W_V, L0_attn_W_O)
    h = h + _L0_ffn_ref(_layernorm(h, axis=-1), L0_ffn_Wg, L0_ffn_W1, L0_ffn_b1, L0_ffn_W2, L0_ffn_b2)
    return h

_drawn_inputs = setup_inputs


def setup_inputs(seed=0):
    import zlib

    import numpy as np

    out = dict(_drawn_inputs(seed))
    spreads = {'L0_ffn_b1': (0.0, 0.774), 'L0_ffn_b2': (0.0, 0.524)}
    factors = {}
    for name, (base, spread) in spreads.items():
        noise = np.random.default_rng([zlib.crc32(name.encode()), seed]).standard_normal(out[name].shape)
        drawn = base * np.exp(spread * noise) if base else spread * noise
        out[name] = jnp.asarray(drawn.astype(out[name].dtype))
    for name, factor in factors.items():
        out[name] = (out[name] * factor).astype(out[name].dtype)
    return out
```

```python
import concourse.bass as bass
from concourse import mybir
from contextlib import ExitStack

FP32 = mybir.dt.float32
BF16 = mybir.dt.bfloat16
U32 = mybir.dt.uint32
I32 = mybir.dt.int32
ALU = mybir.AluOpType
ACT = mybir.ActivationFunctionType
AX = mybir.AxisListType.X

P = 128
SEG = 64
DILATION = 2
LN_EPS = 1e-5
RSQRT_SEED = float(0x5F3759DF)
NEWTON_STEPS = 3
MASKED = -1e30
OUT_OF_BOUNDS = float(1 << 20)
CAPACITY_RATIO = 1.25
TOP_K = 2
SEARCH_STEPS = 26


def after(eng, sem, count):
    if not (isinstance(count, int) and count <= 0):
        eng.wait_ge(sem, count)


def alone(eng, sem):
    eng.sem_inc(sem, 1)


def over_rows(ap, shape):
    return ap.rearrange("p (t o) -> p t o", o=1).to_broadcast(shape)


def over_tiles(ap, shape):
    return ap.rearrange("p (o n) -> p o n", o=1).to_broadcast(shape)


class Chain:

    def __init__(self, eng, sem, base):
        self.eng, self.sem, self.base, self.n = eng, sem, base, 0

    def step(self, ins):
        self.n += 1
        ins.then_inc(self.sem, 1)
        self.eng.wait_ge(self.sem, self.base + self.n)


def audio_tower_kernel(nc, x, wq, wk, wv, wo, wg, w1, b1, w2, b2, out):
    B, S_IN, D = x.shape
    H, _, DK = wq.shape
    E, _, HID = w1.shape
    S = -(-S_IN // (SEG * DILATION)) * SEG
    REAL = -(-S_IN // DILATION)
    NT = S // P
    TILES = B * NT
    T = B * S
    CAP = int(CAPACITY_RATIO * T * TOP_K / E)
    GROUP = NT * P
    GPE = -(-CAP // (2 * GROUP)) * 2
    CAPP = GPE * GROUP
    D1 = D - P
    PAIRS = H // 2
    HT = HID // P
    UNITS = H * NT
    PROJ = 2 * PAIRS + 2 * NT
    VH = H * DK // 2
    TOK_SCALE = float(D) ** -0.5
    Q_SCALE = float(DK) ** -0.5
    REC = 2 * E + 4
    assert S == NT * P and D1 == 64 and DK == 64 and B % 2 == 0 and UNITS % 4 == 0

    slots_dram = nc.dram_tensor("slots_dram", (E * CAPP + GROUP, D), FP32).ap()
    expert_dram = nc.dram_tensor("expert_dram", (E * CAPP, D), FP32).ap()

    top = ExitStack()
    with top:
        def sb(name, shape, dt=FP32, ctx=top):
            return ctx.enter_context(nc.sbuf_tensor(name, shape, dt))

        def sem(name):
            return top.enter_context(nc.semaphore(name))

        tokens = sb("tokens", [P, TILES, D])
        record = sb("record", [P, TILES, REC])
        ident = sb("ident", [P, P])
        ident_bf = sb("ident_bf", [P, P], BF16)
        before = sb("before", [P, P], BF16)
        ones_bf = sb("ones_bf", [P, P], BF16)
        running = sb("running", [P, 2, E])
        expert_base = sb("expert_base", [P, E])
        first_wins = sb("first_wins", [P, E])
        most = sb("most", [P, 1], I32)
        spare = sem("spare")

        def layer_norm(chain, src, dst, st, mv, half_var, y, yy, n):
            alone(chain.eng, spare)
            for t in range(n):
                ins = nc.vector.bn_stats(st[:, t, :], src[:, t, :])
            chain.step(ins)
            alone(chain.eng, spare)
            for t in range(n):
                ins = nc.vector.bn_aggr(mv[:, t, :], st[:, t, :])
            chain.step(ins)
            var = mv[:, 0:n, 1]
            chain.step(nc.vector.tensor_scalar(half_var[:, 0:n], var, LN_EPS, None, ALU.add))
            chain.step(nc.vector.tensor_scalar(yy[:, 0:n].bitcast(I32), half_var[:, 0:n].bitcast(I32), 1, None,
                                               ALU.logical_shift_right))
            chain.step(nc.vector.tensor_scalar(y[:, 0:n].bitcast(I32), yy[:, 0:n].bitcast(I32), -1.0, RSQRT_SEED,
                                               ALU.mult, ALU.add))
            chain.step(nc.vector.tensor_scalar(half_var[:, 0:n], half_var[:, 0:n], -0.5, None, ALU.mult))
            for _ in range(NEWTON_STEPS):
                chain.step(nc.vector.tensor_tensor(yy[:, 0:n], y[:, 0:n], y[:, 0:n], ALU.mult))
                chain.step(nc.vector.tensor_tensor(yy[:, 0:n], yy[:, 0:n], half_var[:, 0:n], ALU.mult))
                chain.step(nc.vector.scalar_tensor_tensor(y[:, 0:n], yy[:, 0:n], 1.5, y[:, 0:n], ALU.add, ALU.mult))
            for t in range(n):
                ins = nc.vector.tensor_scalar(dst[:, t, :], src[:, t, :], mv[:, t, 0:1], y[:, t:t + 1],
                                              ALU.subtract, ALU.mult)
            return ins

        part = ExitStack()
        with part:
            def sa(name, shape, dt=FP32):
                return sb(name, shape, dt, part)

            def ps(name, shape, dt=FP32):
                return part.enter_context(nc.psum_tensor(name, shape, dt))

            wqk_hi = [sa("wq_hi", [P, H, DK]), sa("wk_hi", [P, H, DK])]
            wqk_lo = [sa("wq_lo", [D1, H, DK]), sa("wk_lo", [D1, H, DK])]
            wv_hi, wv_lo = sa("wv_hi", [P, H, DK]), sa("wv_lo", [D1, H, DK])
            wo_sb = sa("wo_sb", [P, PAIRS, D])
            wg_hi, wg_lo = sa("wg_hi", [P, E]), sa("wg_lo", [D1, E])
            causal = sa("causal", [P, P], BF16)
            own_segment = sa("own_segment", [P, P])
            zeros = sa("zeros", [P, D])

            xin = [sa(f"xin{i}", [P, NT, D]) for i in range(2)]
            xsT_hi, xsT_lo = sa("xsT_hi", [P, S]), sa("xsT_lo", [D1, S])
            tok_s, tok_p, tok_pT = sa("tok_s", [P, NT, P]), sa("tok_p", [P, NT, P]), sa("tok_pT", [P, NT, P])
            tok_max, tok_sum, tok_inv = sa("tok_max", [P, NT]), sa("tok_sum", [P, NT]), sa("tok_inv", [P, NT])
            st, mv = sa("st", [P, NT, 6]), sa("mv", [P, NT, 2])
            ln_h, ln_y, ln_yy = sa("ln_h", [P, NT]), sa("ln_y", [P, NT]), sa("ln_yy", [P, NT])
            xn = sa("xn", [P, NT, D])
            xnT_hi, xnT_lo = xsT_hi, xsT_lo
            QT = [sa(f"QT{i}", [P, PAIRS, S]) for i in range(2)]
            KT = [sa(f"KT{i}", [P, PAIRS, S]) for i in range(2)]
            V = [sa(f"V{i}", [P, NT, H * DK]) for i in range(2)]
            NR = 4
            neg_max = sa("neg_max", [P, NR])
            prob = sa("prob", [P, NR, S])
            probT = sa("probT", [P, NR, S])
            row_sum = sa("row_sum", [P, H, NT])
            row_inv = sa("row_inv", [P, H, NT])
            O_sb = sa("O_sb", [P, 2, NT, P])
            OT = sa("OT", [P, PAIRS, S])
            st2, mv2 = sa("st2", [P, NT, 6]), sa("mv2", [P, NT, 2])
            ln_h2, ln_y2, ln_yy2 = sa("ln_h2", [P, NT]), sa("ln_y2", [P, NT]), sa("ln_yy2", [P, NT])
            xn2 = [sa(f"xn2_{i}", [P, NT, D]) for i in range(2)]
            x2T_hi = tok_p[:, :, :].rearrange("p t k -> p (t k)")
            x2T_lo = tok_s[0:D1, :, :].rearrange("p t k -> p (t k)")
            lg, lg2 = sa("lg", [P, NT, E]), sa("lg2", [P, NT, E])
            key = sa("key", [P, NT, E])
            top1, top2, key_max = sa("top1", [P, NT]), sa("top2", [P, NT]), sa("key_max", [P, NT])
            gap, gap_exp, gap_sum = sa("gap", [P, NT]), sa("gap_exp", [P, NT]), sa("gap_sum", [P, NT])
            rec = sa("rec", [P, NT, REC])
            sel2 = sa("sel2", [P, NT, E])
            chosen_bf = sa("chosen_bf", [P, NT, E], BF16)
            pos, late = sa("pos", [P, NT, E]), sa("late", [P, NT, E])
            picked = sa("picked", [P, NT, E])
            slot_idx = [sa(f"slot_idx{i}", [P, NT, 2], U32) for i in range(2)]

            S_ps = [ps(f"S_ps{i}", [P, 512]) for i in range(2)]
            T_ps = [ps(f"T_ps{i}", [P, 512]) for i in range(2)]
            O_ps = ps("O_ps", [P, 512])
            FA, FB = ps("FA", [P, 512]), ps("FB", [P, 512])
            TA = ps("TA", [P, 512])
            O_view = O_ps[:, 0:NT * P].rearrange("p (t c) -> p t c", t=NT)

            zero_ready, const_pool, consts = sem("zero_ready"), sem("const_pool"), sem("consts")
            weights_in = sem("weights_in")
            x_in = [sem("x_in0"), sem("x_in1")]
            rows_zeroed = sem("rows_zeroed")
            xsT_ps, xsT_hi_sb, xsT_lo_sb = sem("xsT_ps"), sem("xsT_hi_sb"), sem("xsT_lo_sb")
            tok_scores, tok_max_ready, tok_exp = sem("tok_scores"), sem("tok_max_ready"), sem("tok_exp")
            tok_pT_ps, tok_pT_sb, tok_mixed = sem("tok_pT_ps"), sem("tok_pT_sb"), sem("tok_mixed")
            xn_ready, xnT_ps, xnT_hi_sb, xnT_lo_sb = sem("xn_ready"), sem("xnT_ps"), sem("xnT_hi_sb"), sem("xnT_lo_sb")
            proj_ps = sem("proj_ps")
            proj_sb = [sem("proj_sb_act"), sem("proj_sb_dve")]
            scores, max_ready, exp_done = sem("scores"), sem("max_ready"), sem("exp_done")
            probT_ps = sem("probT_ps")
            probT_sb = [sem("probT_sb_dve"), sem("probT_sb_act")]
            attended, normed = sem("attended"), sem("normed")
            OT_ps, OT_sb = sem("OT_ps"), sem("OT_sb")
            wo_ps, wo_added = sem("wo_ps"), sem("wo_added")
            xn2_ready, x2T_ps, x2T_sb = sem("xn2_ready"), sem("x2T_ps"), sem("x2T_sb")
            totals_ready = sem("totals_ready")
            logits_ps, logits_sb, ranks_sb = sem("logits_ps"), sem("logits_sb"), sem("ranks_sb")
            gap_ready, gap_exped = sem("gap_ready"), sem("gap_exped")
            chosen_ready, ranks_ps, slots_ready = sem("chosen_ready"), sem("ranks_ps"), sem("slots_ready")
            xn2_free = sem("xn2_free")
            scattered = [sem("scattered0"), sem("scattered1")]
            front_chain, tail_chain, norm_chain = sem("front_chain"), sem("tail_chain"), sem("norm_chain")

            LN_STEPS = 6 + 3 * NEWTON_STEPS
            FRONT_STEPS = 3 + LN_STEPS
            TAIL_STEPS = LN_STEPS + 5 + 1 + 5 + 2 + 4 + 4

            F_XT, F_SCORE, F_PT, F_MIX, F_XNT, F_PROJ = 1, 3, 6, 8, 13, UNITS - PROJ
            T_WO, T_X2T, T_LOGIT, T_RANK = 4, 9, 12, 16
            PAIR = 2 * NT

            def alternate(b, par, first, last, unit, front, tail):
                for n in range(UNITS):
                    unit(b, par, n, first, last)
                    if not last:
                        front(b + 1, 1 - par, n)
                    if not first:
                        tail(b - 1, 1 - par, n)

            def run(eng, unit, front, tail):
                for n in range(UNITS):
                    front(0, 0, n)
                alternate(0, 0, True, False, unit, front, tail)
                if B > 2:
                    with eng.Fori(0, B // 2 - 1) as j:
                        for u in range(2):
                            alternate(2 * j + 1 + u, (1 + u) % 2, False, False, unit, front, tail)
                alternate(B - 1, 1, False, True, unit, front, tail)

            block = part.enter_context(nc.Block())

            @block.sync
            def _(sp):
                for w, hi, lo in ((wq, wqk_hi[0], wqk_lo[0]), (wk, wqk_hi[1], wqk_lo[1]), (wv, wv_hi, wv_lo)):
                    sp.dma_start(hi[:, :, :], w[:, 0:P, :].rearrange("h m k -> m h k")).then_inc(weights_in, 16)
                    sp.dma_start(lo[:, :, :], w[:, P:D, :].rearrange("h m k -> m h k")).then_inc(weights_in, 16)
                sp.dma_start(wo_sb[:, :, :], wo.rearrange("(c p) d -> p c d", p=P)).then_inc(weights_in, 16)
                sp.dma_start(wg_hi[:, :], wg[0:P, :]).then_inc(weights_in, 16)
                sp.dma_start(wg_lo[:, :], wg[P:D, :]).then_inc(weights_in, 16)
                sp.wait_ge(zero_ready, 1)

                LAST = REAL - (NT - 1) * P

                def load(b, par):
                    xb = x[bass.ds(b, 1), :, :].rearrange("o (s two) d -> (o s) two d", two=DILATION)
                    full = (NT - 1) * P
                    sp.dma_start(xin[par][:, 0:NT - 1, :],
                                 xb[0:full, 0, :].rearrange("(t p) d -> p t d", p=P)).then_inc(x_in[par], 16)
                    sp.dma_start(xin[par][0:LAST, NT - 1, :], xb[full:REAL, 0, :]).then_inc(x_in[par], 16)

                def zero_rows(k):
                    for e in range(E):
                        sp.dma_start(slots_dram[bass.ds(k * GROUP + e * CAPP, GROUP), :]
                                     .rearrange("(p r) d -> p r d", p=P), over_tiles(zeros[:, :], [P, NT, D])
                                     ).then_inc(rows_zeroed, 16)

                load(0, 0)
                load(1, 1)
                sp.dma_start(slots_dram[E * CAPP:E * CAPP + GROUP, :].rearrange("(p r) d -> p r d", p=P),
                             over_tiles(zeros[:, :], [P, NT, D])).then_inc(rows_zeroed, 16)
                for turns, fill in ((range(1, GPE // 2 + 1), True), (range(GPE // 2 + 1, B // 2), False)):
                    if not len(turns):
                        continue
                    with sp.Fori(turns.start, turns.stop) as j:
                        for par in range(2):
                            if fill:
                                zero_rows(2 * j - 2 + par)
                            sp.wait_ge(tok_mixed, 2 * j - 1 + par)
                            load(2 * j + par, par)

            @block.gpsimd
            def _(pool):
                nc.gpsimd.memset(ident[:, :], 0.0).then_inc(const_pool, 1)
                nc.gpsimd.memset(ident_bf[:, :], 0.0).then_inc(const_pool, 1)
                nc.gpsimd.memset(before[:, :], 1.0).then_inc(const_pool, 1)
                nc.gpsimd.memset(causal[:, :], 0.0).then_inc(const_pool, 1)
                pool.wait_ge(const_pool, 4)
                for m in (ident, ident_bf):
                    nc.gpsimd.affine_select(out=m[:, :], in_=m[:, :], compare_op=ALU.not_equal, fill=1.0, base=0,
                                            pattern=[[-1, P]], channel_multiplier=1).then_inc(consts, 1)
                nc.gpsimd.affine_select(out=before[:, :], in_=before[:, :], compare_op=ALU.is_gt, fill=0.0, base=0,
                                        pattern=[[1, P]], channel_multiplier=-1).then_inc(consts, 1)
                nc.gpsimd.affine_select(out=causal[:, :], in_=causal[:, :], compare_op=ALU.is_ge, fill=MASKED, base=0,
                                        pattern=[[-1, P]], channel_multiplier=1).then_inc(consts, 1)

                pool.sem_inc(xn2_free, 2)

                def scatter(b, par, zeroed):
                    pool.wait_ge(slots_ready, b + 1)
                    if zeroed is not None:
                        pool.wait_ge(rows_zeroed, zeroed)
                    alone(pool, spare)
                    for t in range(NT):
                        for k in range(2):
                            pool.indirect_dma_start(
                                slots_dram[:, :], bass.IndirectOffsetOnAxis(slot_idx[par][:, t, k:k + 1], 0),
                                xn2[par][:, t, :], None, bounds_check=E * CAPP - 1, oob_is_err=False
                            ).then_inc(scattered[par], 16)
                    pool.wait_ge(scattered[par], NT * 16 * (b - par) + 2 * NT * 16)
                    pool.sem_inc(xn2_free, 1)

                with pool.Fori(0, GPE // 2) as j:
                    for par in range(2):
                        scatter(2 * j + par, par, 16 + 16 * E * (2 * j + par + 1))
                if B > GPE:
                    with pool.Fori(GPE // 2, B // 2) as j:
                        for par in range(2):
                            scatter(2 * j + par, par, None)
                pool.wait_ge(rows_zeroed, 16 + 16 * E * GPE)

            @block.scalar
            def _(act):
                def front(b, par, n):
                    if n == F_XT:
                        act.wait_ge(xsT_ps, b + 1)
                        nc.scalar.activation(xsT_hi[:, :], FA[:, 0:S], ACT.Copy).then_inc(xsT_hi_sb, 1)
                    if n == F_SCORE:
                        act.wait_ge(tok_max_ready, b + 1)
                        for t in range(NT):
                            nc.scalar.activation(tok_p[:, t, :], tok_s[:, t, :], ACT.Exp, bias=tok_max[:, t:t + 1],
                                                 accum_out=tok_sum[:, t:t + 1]).then_inc(tok_exp, 1)
                    if n == F_XNT:
                        act.wait_ge(xnT_ps, b + 1)
                        nc.scalar.activation(xnT_hi[:, :], FA[:, 0:S], ACT.Copy).then_inc(xnT_hi_sb, 1)
                    q = n - F_PROJ
                    if q >= 0 and q % 2 == 0:
                        act.wait_ge(proj_ps, PROJ * b + q + 1)
                        if q == 0:
                            after(act, attended, UNITS * (b - 1))
                        if q < PAIRS:
                            ins = nc.scalar.activation(QT[par][:, q, :], FA[:, 0:S], ACT.Copy, scale=Q_SCALE)
                        elif q < 2 * PAIRS:
                            ins = nc.scalar.activation(KT[par][:, q - PAIRS, :], FA[:, 0:S], ACT.Copy)
                        else:
                            t, half = divmod(q - 2 * PAIRS, 2)
                            ins = nc.scalar.activation(V[par][:, t, half * VH:half * VH + VH], FA[:, 0:VH], ACT.Copy)
                        ins.then_inc(proj_sb[0], 1)

                def exp_unit(b, par, n):
                    g = UNITS * b + n
                    h, t = divmod(n, NT)
                    w = P * (t + 1)
                    act.wait_ge(max_ready, g + 1)
                    after(act, probT_ps, g - NR + 1)
                    nc.scalar.activation(prob[:, n % NR, 0:w], S_ps[n % 2][:, 0:w], ACT.Exp,
                                         bias=neg_max[:, n % NR:n % NR + 1],
                                         accum_out=row_sum[:, h, t:t + 1]).then_inc(exp_done, 1)

                def unit(b, par, n, first, last):
                    g = UNITS * b + n
                    w = P * (n % NT + 1)
                    if first and n == 0:
                        exp_unit(b, par, 0)
                        exp_unit(b, par, 1)
                    if n % 2 == 1:
                        act.wait_ge(probT_ps, g + 1)
                        after(act, attended, g - NR + 1)
                        nc.scalar.activation(probT[:, n % NR, 0:w], T_ps[1][:, 0:w], ACT.Copy).then_inc(probT_sb[1], 1)
                    if n + 2 < UNITS:
                        exp_unit(b, par, n + 2)
                    elif not last:
                        exp_unit(b + 1, 1 - par, n + 2 - UNITS)

                def tail(b, par, n):
                    if n == T_LOGIT + 1:
                        act.wait_ge(gap_ready, b + 1)
                        nc.scalar.activation(gap_exp[:, :], gap[:, :], ACT.Exp).then_inc(gap_exped, 1)

                run(act, unit, front, tail)
                for n in range(UNITS):
                    tail(B - 1, 1, n)

            @block.vector
            def _(dve):
                nc.vector.memset(zeros[:, :], 0.0)
                nc.vector.memset(running[:, :, :], 0.0)
                nc.vector.memset(ones_bf[:, :], 1.0)
                nc.vector.memset(own_segment[:, :], 0.0)
                nc.vector.memset(xin[0][:, :, :], 0.0)
                nc.vector.memset(xin[1][:, :, :], 0.0).then_inc(zero_ready, 1)
                for e in range(E):
                    nc.vector.memset(expert_base[:, e:e + 1], float(e * CAPP))
                    nc.vector.memset(first_wins[:, e:e + 1], float(E - e))
                dve.wait_ge(zero_ready, 1)
                nc.vector.memset(own_segment[0:SEG, SEG:P], MASKED)
                nc.vector.memset(own_segment[SEG:P, 0:SEG], MASKED).then_inc(zero_ready, 1)
                dve.wait_ge(zero_ready, 2)

                chains = {}

                def front(b, par, n):
                    if n == 0:
                        chains["front"] = Chain(dve, front_chain, FRONT_STEPS * b)
                    chain = chains["front"]
                    if n == F_XT:
                        dve.wait_ge(xsT_ps, b + 1)
                        nc.vector.tensor_copy(xsT_lo[:, :], FB[0:D1, 0:S]).then_inc(xsT_lo_sb, 1)
                    if n == F_SCORE:
                        dve.wait_ge(tok_scores, b + 1)
                        chain.step(nc.vector.scalar_tensor_tensor(
                            tok_s[:, :, :], FA[:, 0:S].rearrange("p (t k) -> p t k", t=NT), TOK_SCALE,
                            over_tiles(own_segment[:, :], [P, NT, P]), ALU.mult, ALU.add))
                        nc.vector.tensor_reduce(tok_max[:, :], tok_s[:, :, :], AX, ALU.max,
                                                negate=True).then_inc(tok_max_ready, 1)
                    if n == F_PT:
                        dve.wait_ge(tok_pT_ps, b + 1)
                        nc.vector.tensor_copy(tok_pT[:, :, :], FB[:, 0:S].rearrange("p (t k) -> p t k", t=NT)
                                              ).then_inc(tok_pT_sb, 1)
                        dve.wait_ge(tok_exp, NT * (b + 1))
                        chain.step(nc.vector.reciprocal(tok_inv[:, :], tok_sum[:, :]))
                    if n == F_MIX:
                        dve.wait_ge(tok_mixed, b + 1)
                        for t in range(NT):
                            src = FA[:, t * D:t * D + D] if t < 2 else FB[:, 0:D]
                            ins = nc.vector.tensor_scalar(tokens[:, bass.ds(NT * b + t, 1), :],
                                                          src.rearrange("p (o d) -> p o d", o=1),
                                                          tok_inv[:, t:t + 1], None, ALU.mult)
                        chain.step(ins)
                        layer_norm(chain, tokens[:, bass.ds(NT * b, NT), :], xn, st, mv, ln_h, ln_y, ln_yy, NT
                                   ).then_inc(xn_ready, 1)
                    if n == F_XNT:
                        dve.wait_ge(xnT_ps, b + 1)
                        nc.vector.tensor_copy(xnT_lo[:, :], FB[0:D1, 0:S]).then_inc(xnT_lo_sb, 1)
                    q = n - F_PROJ
                    if q >= 0 and q % 2 == 1:
                        dve.wait_ge(proj_ps, PROJ * b + q + 1)
                        if q == 1:
                            after(dve, attended, UNITS * (b - 1))
                        if q < PAIRS:
                            ins = nc.vector.tensor_scalar(QT[par][:, q, :], FB[:, 0:S], Q_SCALE, None, ALU.mult)
                        elif q < 2 * PAIRS:
                            ins = nc.vector.tensor_copy(KT[par][:, q - PAIRS, :], FB[:, 0:S])
                        else:
                            t, half = divmod(q - 2 * PAIRS, 2)
                            ins = nc.vector.tensor_copy(V[par][:, t, half * VH:half * VH + VH], FB[:, 0:VH])
                        ins.then_inc(proj_sb[1], 1)
                    if n == UNITS - 1:
                        assert chain.n == FRONT_STEPS, chain.n

                def max_unit(b, par, n):
                    g = UNITS * b + n
                    w = P * (n % NT + 1)
                    dve.wait_ge(scores, g + 1)
                    after(dve, exp_done, g - NR + 1)
                    nc.vector.tensor_reduce(neg_max[:, n % NR:n % NR + 1], S_ps[n % 2][:, 0:w], AX, ALU.max,
                                            negate=True).then_inc(max_ready, 1)

                def norm_pair(b, m):
                    k = PAIRS * b + m
                    dve.wait_ge(attended, UNITS * b + 2 * NT * (m + 1))
                    nc.vector.reciprocal(row_inv[:, 2 * m:2 * m + 2, :], row_sum[:, 2 * m:2 * m + 2, :]
                                         ).then_inc(norm_chain, 1)
                    dve.wait_ge(norm_chain, k + 1)
                    after(dve, OT_ps, k - 1)
                    for t in range(NT):
                        ins = nc.vector.tensor_tensor(
                            O_sb[:, m % 2, t, :].rearrange("p (h c) -> p h c", h=2),
                            O_view[:, t, :].rearrange("p (h c) -> p h c", h=2),
                            row_inv[:, 2 * m:2 * m + 2, t:t + 1].to_broadcast([P, 2, DK]), ALU.mult)
                    ins.then_inc(normed, 1)

                def copy_OT(b, m):
                    k = PAIRS * b + m
                    dve.wait_ge(OT_ps, k + 1)
                    if m == 0:
                        after(dve, wo_ps, 2 * b)
                    nc.vector.tensor_copy(OT[:, m, :], TA[:, 0:S]).then_inc(OT_sb, 1)

                def pair_steps(b, n):
                    if n % (2 * NT) == 0 and n:
                        norm_pair(b, n // (2 * NT) - 1)
                    if n % (2 * NT) == 2 and n > 2:
                        copy_OT(b, n // (2 * NT) - 1)

                def unit(b, par, n, first, last):
                    g = UNITS * b + n
                    w = P * (n % NT + 1)
                    if first and n == 0:
                        max_unit(b, par, 0)
                        max_unit(b, par, 1)
                    if n % 2 == 0:
                        dve.wait_ge(probT_ps, g + 1)
                        after(dve, attended, g - NR + 1)
                        nc.vector.tensor_copy(probT[:, n % NR, 0:w], T_ps[0][:, 0:w]).then_inc(probT_sb[0], 1)
                    if n + 2 < UNITS:
                        max_unit(b, par, n + 2)
                    elif not last:
                        max_unit(b + 1, 1 - par, n + 2 - UNITS)
                    if n <= 2 and not first:
                        pair_steps(b - 1, UNITS + n)
                    pair_steps(b, n)

                def tail(b, par, n):
                    if n == 0:
                        chains["tail"] = Chain(dve, tail_chain, TAIL_STEPS * b)
                    chain = chains["tail"]
                    for use, (lo, hi) in enumerate(((0, 2), (2, NT))):
                        if n == T_WO + use:
                            dve.wait_ge(wo_ps, 2 * b + use + 1)
                            h = tokens[:, bass.ds(NT * b + lo, hi - lo), :]
                            nc.vector.tensor_tensor(h, TA[:, 0:(hi - lo) * D].rearrange("p (t d) -> p t d", d=D), h,
                                                    ALU.add).then_inc(wo_added, 1)
                    if n == T_WO + 1:
                        dve.wait_ge(wo_added, 2 * b + 2)
                        dve.wait_ge(xn2_free, b + 1)
                        layer_norm(chain, tokens[:, bass.ds(NT * b, NT), :], xn2[par], st2, mv2, ln_h2, ln_y2, ln_yy2,
                                   NT).then_inc(xn2_ready, 1)
                    if n == T_X2T:
                        dve.wait_ge(x2T_ps, 2 * b + 1)
                        nc.vector.tensor_copy(x2T_hi[:, :], TA[:, 0:S]).then_inc(x2T_sb, 1)
                    if n == T_X2T + 1:
                        dve.wait_ge(x2T_ps, 2 * b + 2)
                        nc.vector.tensor_copy(x2T_lo[:, :], TA[0:D1, 0:S]).then_inc(x2T_sb, 1)
                    if n == T_LOGIT:
                        whole = [P, NT, E]
                        sel1, chosen = rec[:, :, 0:E], rec[:, :, E:2 * E]
                        dve.wait_ge(logits_ps, b + 1)
                        nc.vector.tensor_copy(lg[:, :, :], TA[:, 0:NT * E].rearrange("p (t e) -> p t e", t=NT)
                                              ).then_inc(logits_sb, 1)
                        dve.wait_ge(logits_sb, b + 1)

                        def pick(src, best, sel):
                            chain.step(nc.vector.tensor_reduce(best[:, :], src, AX, ALU.max))
                            chain.step(nc.vector.tensor_tensor(key[:, :, :], src, over_rows(best[:, :], whole), ALU.is_equal))
                            chain.step(nc.vector.tensor_tensor(key[:, :, :], key[:, :, :], over_tiles(first_wins[:, :], whole),
                                                               ALU.mult))
                            chain.step(nc.vector.tensor_reduce(key_max[:, :], key[:, :, :], AX, ALU.max))
                            chain.step(nc.vector.tensor_tensor(sel, key[:, :, :], over_rows(key_max[:, :], whole), ALU.is_equal))

                        pick(lg[:, :, :], top1, sel1)
                        chain.step(nc.vector.scalar_tensor_tensor(lg2[:, :, :], sel1, MASKED, lg[:, :, :], ALU.mult, ALU.add))
                        pick(lg2[:, :, :], top2, sel2[:, :, :])
                        nc.vector.tensor_tensor(gap[:, :], top2[:, :], top1[:, :], ALU.subtract).then_inc(gap_ready, 1)
                        nc.vector.tensor_tensor(chosen_bf[:, :, :], sel1, sel2[:, :, :], ALU.add).then_inc(chosen_ready, 1)
                        nc.vector.tensor_tensor(chosen, sel1, sel2[:, :, :], ALU.add)
                    if n == T_LOGIT + 2:
                        dve.wait_ge(gap_exped, b + 1)
                        chain.step(nc.vector.tensor_scalar(gap_sum[:, :], gap_exp[:, :], 1.0, None, ALU.add))
                        chain.step(nc.vector.reciprocal(rec[:, :, 2 * E], gap_sum[:, :]))
                        nc.vector.tensor_tensor(rec[:, :, 2 * E + 1], rec[:, :, 2 * E], gap_exp[:, :], ALU.mult)
                    if n == T_RANK:
                        whole = [P, NT, E]
                        old, new = running[:, par, :], running[:, 1 - par, :]
                        dve.wait_ge(ranks_ps, b + 1)
                        nc.vector.tensor_tensor(new, TA[:, NT * E:(NT + 1) * E], old, ALU.add)
                        nc.vector.tensor_tensor(pos[:, :, :], TA[:, 0:NT * E].rearrange("p (t e) -> p t e", t=NT),
                                                over_tiles(old, whole), ALU.add).then_inc(ranks_sb, 1)
                        dve.wait_ge(ranks_sb, b + 1)
                        chain.step(nc.vector.tensor_scalar(late[:, :, :], pos[:, :, :], float(CAP), OUT_OF_BOUNDS,
                                                           ALU.is_ge, ALU.mult))
                        chain.step(nc.vector.tensor_tensor(pos[:, :, :], pos[:, :, :], late[:, :, :], ALU.add))
                        chain.step(nc.vector.tensor_tensor(pos[:, :, :], pos[:, :, :],
                                                           over_tiles(expert_base[:, :], whole), ALU.add))
                        for k, sel in enumerate((rec[:, :, 0:E], sel2[:, :, :])):
                            chain.step(nc.vector.tensor_tensor(picked[:, :, :], pos[:, :, :], sel, ALU.mult))
                            chain.step(nc.vector.tensor_reduce(rec[:, :, 2 * E + 2 + k:2 * E + 3 + k], picked[:, :, :],
                                                               AX, ALU.add))
                        nc.vector.tensor_copy(slot_idx[par][:, :, :], rec[:, :, 2 * E + 2:REC]).then_inc(slots_ready, 1)
                        chain.step(nc.vector.tensor_copy(record[:, bass.ds(NT * b, NT), :], rec[:, :, :]))
                    if n == UNITS - 1:
                        assert chain.n == TAIL_STEPS, chain.n

                run(dve, unit, front, tail)
                norm_pair(B - 1, PAIRS - 1)
                copy_OT(B - 1, PAIRS - 1)
                for n in range(UNITS):
                    tail(B - 1, 1, n)
                nc.vector.tensor_reduce(most[:, :], running[:, B % 2, :], AX, ALU.max).then_inc(totals_ready, 1)
                dve.wait_ge(totals_ready, 1)

            @block.tensor
            def _(pe):
                pe.wait_ge(weights_in, 16 * 9)
                pe.wait_ge(consts, 4)
                pe.wait_ge(zero_ready, 2)

                def transposes(dst, src, lo, hi):
                    for t in range(NT):
                        ins = nc.tensor.transpose(dst[0:hi - lo, t * P:t * P + P], src[:, t, lo:hi], ident[:, :])
                    return ins

                def front(b, par, n):
                    if n == F_XT:
                        if isinstance(b, int):
                            pe.wait_ge(x_in[par], 32 * (b // 2 + 1))
                        else:
                            pe.wait_ge(x_in[par], 16 * (b - par) + 32)
                        after(pe, proj_sb[0], PROJ // 2 * b)
                        after(pe, proj_sb[1], PROJ // 2 * b)
                        transposes(FA, xin[par], 0, P)
                        transposes(FB, xin[par], P, D).then_inc(xsT_ps, 1)
                    if n == F_SCORE:
                        pe.wait_ge(xsT_hi_sb, b + 1)
                        pe.wait_ge(xsT_lo_sb, b + 1)
                        for t in range(NT):
                            c = slice(t * P, t * P + P)
                            nc.tensor.matmul(FA[:, c], xsT_hi[:, c], xsT_hi[:, c], start=True, stop=False)
                            ins = nc.tensor.matmul(FA[:, c], xsT_lo[:, c], xsT_lo[:, c], start=False, stop=True)
                        ins.then_inc(tok_scores, 1)
                    if n == F_PT:
                        pe.wait_ge(tok_exp, NT * (b + 1))
                        transposes(FB, tok_p, 0, P).then_inc(tok_pT_ps, 1)
                    if n == F_MIX:
                        pe.wait_ge(tok_pT_sb, b + 1)
                        for t in range(NT):
                            dst = FA[:, t * D:t * D + D] if t < 2 else FB[:, 0:D]
                            ins = nc.tensor.matmul(dst, tok_pT[:, t, :], xin[par][:, t, :], start=True, stop=True)
                        ins.then_inc(tok_mixed, 1)
                    if n == F_XNT:
                        pe.wait_ge(xn_ready, b + 1)
                        transposes(FA, xn, 0, P)
                        transposes(FB, xn, P, D).then_inc(xnT_ps, 1)
                    q = n - F_PROJ
                    if q >= 0:
                        dst = (FA, FB)[q % 2]
                        if q < 2:
                            pe.wait_ge(xnT_hi_sb, b + 1)
                            pe.wait_ge(xnT_lo_sb, b + 1)
                        else:
                            pe.wait_ge(proj_sb[q % 2], PROJ // 2 * b + q // 2)
                        if q < 2 * PAIRS:
                            k, m = divmod(q, PAIRS)
                            w = slice(2 * m, 2 * m + 2)
                            nc.tensor.matmul(dst[:, 0:S], wqk_hi[k][:, w, :].rearrange("p h k -> p (h k)"), xnT_hi[:, :],
                                             start=True, stop=False)
                            ins = nc.tensor.matmul(dst[:, 0:S], wqk_lo[k][:, w, :].rearrange("p h k -> p (h k)"),
                                                   xnT_lo[:, :], start=False, stop=True)
                        else:
                            t, half = divmod(q - 2 * PAIRS, 2)
                            c = slice(t * P, t * P + P)
                            w = slice(half * H // 2, (half + 1) * H // 2)
                            nc.tensor.matmul(dst[:, 0:VH], xnT_hi[:, c], wv_hi[:, w, :].rearrange("p h k -> p (h k)"),
                                             start=True, stop=False)
                            ins = nc.tensor.matmul(dst[:, 0:VH], xnT_lo[:, c],
                                                   wv_lo[:, w, :].rearrange("p h k -> p (h k)"), start=False, stop=True)
                        ins.then_inc(proj_ps, 1)

                def score_unit(b, par, n):
                    h, t = divmod(n, NT)
                    m, rows = h // 2, slice(DK * (h % 2), DK * (h % 2) + DK)
                    g = UNITS * b + n
                    if n % PAIR == 0:
                        pe.wait_ge(proj_sb[m % 2], PROJ // 2 * b + (PAIRS + m) // 2 + 1)
                    after(pe, exp_done, g - 1)
                    dst = S_ps[n % 2]
                    nc.tensor.matmul(dst[:, 0:P * (t + 1)], QT[par][rows, m, t * P:t * P + P],
                                     KT[par][rows, m, 0:P * (t + 1)], start=True, stop=False)
                    nc.tensor.matmul(dst[:, t * P:t * P + P], ident_bf[:, :], causal[:, :], start=False,
                                     stop=True).then_inc(scores, 1)

                def attend_unit(b, par, n):
                    h, t = divmod(n, NT)
                    g = UNITS * b + n
                    if n == 0:
                        for k in range(2):
                            pe.wait_ge(proj_sb[k], PROJ // 2 * (b + 1))
                    if n % PAIR == 0:
                        after(pe, normed, PAIRS * b + n // PAIR)
                    pe.wait_ge(probT_sb[n % 2], UNITS // 2 * b + n // 2 + 1)
                    for j in range(t + 1):
                        ins = nc.tensor.matmul(O_view[:, t, DK * (h % 2):DK * (h % 2) + DK],
                                               probT[:, n % NR, j * P:j * P + P], V[par][:, j, h * DK:h * DK + DK],
                                               start=(j == 0), stop=(j == t))
                    ins.then_inc(attended, 1)

                def transpose_O(b, m):
                    k = PAIRS * b + m
                    pe.wait_ge(normed, k + 1)
                    after(pe, OT_sb, k)
                    if m == 0:
                        after(pe, wo_added, 2 * b)
                    if m == 1:
                        after(pe, logits_sb, b)
                    if m == 2:
                        after(pe, ranks_sb, b)
                    for t in range(NT):
                        ins = nc.tensor.transpose(TA[:, t * P:t * P + P], O_sb[:, m % 2, t, :], ident[:, :])
                    ins.then_inc(OT_ps, 1)

                def unit(b, par, n, first, last):
                    g = UNITS * b + n
                    t = n % NT
                    if first and n == 0:
                        score_unit(b, par, 0)
                        score_unit(b, par, 1)
                    pe.wait_ge(exp_done, g + 1)
                    if n >= 2 or not first:
                        pe.wait_ge(probT_sb[n % 2], UNITS // 2 * b + n // 2)
                    for j in range(t + 1):
                        ins = nc.tensor.transpose(T_ps[n % 2][:, j * P:j * P + P], prob[:, n % NR, j * P:j * P + P],
                                                  ident[:, :])
                    ins.then_inc(probT_ps, 1)
                    if n + 2 < UNITS:
                        score_unit(b, par, n + 2)
                    elif not last:
                        score_unit(b + 1, 1 - par, n + 2 - UNITS)
                    if n:
                        attend_unit(b, par, n - 1)
                    elif not first:
                        attend_unit(b - 1, 1 - par, UNITS - 1)
                    if n % PAIR == 1:
                        if n > 1:
                            transpose_O(b, n // PAIR - 1)
                        elif not first:
                            transpose_O(b - 1, PAIRS - 1)

                def tail(b, par, n, final=False):
                    for use, tiles in enumerate((range(0, 2), range(2, NT))):
                        if n == T_WO + use:
                            pe.wait_ge(OT_sb, PAIRS * (b + 1))
                            if use:
                                pe.wait_ge(wo_added, 2 * b + use)
                            for i, t in enumerate(tiles):
                                for m in range(PAIRS):
                                    ins = nc.tensor.matmul(TA[:, i * D:i * D + D], OT[:, m, t * P:t * P + P],
                                                           wo_sb[:, m, :], start=(m == 0), stop=(m == PAIRS - 1))
                            ins.then_inc(wo_ps, 1)
                    if n == T_X2T:
                        pe.wait_ge(xn2_ready, b + 1)
                        if not final:
                            pe.wait_ge(OT_sb, PAIRS * (b + 1) + 1)
                        transposes(TA, xn2[par], 0, P).then_inc(x2T_ps, 1)
                    if n == T_X2T + 1:
                        pe.wait_ge(x2T_sb, 2 * b + 1)
                        alone(pe, spare)
                        transposes(TA, xn2[par], P, D).then_inc(x2T_ps, 1)
                    if n == T_LOGIT:
                        pe.wait_ge(x2T_sb, 2 * b + 2)
                        for t in range(NT):
                            c = slice(t * P, t * P + P)
                            nc.tensor.matmul(TA[:, t * E:t * E + E], x2T_hi[:, c], wg_hi[:, :], start=True, stop=False)
                            ins = nc.tensor.matmul(TA[:, t * E:t * E + E], x2T_lo[:, c], wg_lo[:, :], start=False,
                                                   stop=True)
                        ins.then_inc(logits_ps, 1)
                    if n == T_RANK:
                        pe.wait_ge(chosen_ready, b + 1)
                        if not final:
                            pe.wait_ge(OT_sb, PAIRS * (b + 1) + 2)
                        for t in range(NT + 1):
                            dst = TA[:, t * E:t * E + E]
                            for k in range(t):
                                ins = nc.tensor.matmul(dst, ones_bf[:, :], chosen_bf[:, k, :], start=(k == 0),
                                                       stop=(t == NT and k == t - 1))
                            if t < NT:
                                ins = nc.tensor.matmul(dst, before[:, :], chosen_bf[:, t, :], start=(t == 0), stop=True)
                        ins.then_inc(ranks_ps, 1)

                run(pe, unit, front, tail)
                attend_unit(B - 1, 1, UNITS - 1)
                transpose_O(B - 1, PAIRS - 1)
                for n in range(UNITS):
                    tail(B - 1, 1, n, final=True)

        part = ExitStack()
        with part:
            def sa(name, shape, dt=FP32):
                return sb(name, shape, dt, part)

            def ps(name, shape, dt=FP32):
                return part.enter_context(nc.psum_tensor(name, shape, dt))

            HALF = TILES // 2
            assert HALF * E <= 512 and TILES <= 256
            priority = sa("priority", [P, TILES])
            threshold, candidate = sa("threshold", [P, E]), sa("candidate", [P, E])
            step_size = sa("step_size", [P, 1])
            hits = sa("hits", [P, TILES, E])
            hits_f = sa("hits_f", [P, E])
            hits_bf = sa("hits_bf", [P, E], BF16)
            raised = sa("raised", [P, E])
            above, ties = sa("above", [P, TILES, E]), sa("ties", [P, TILES, E])
            marked = sa("marked", [P, TILES, E], BF16)
            column, rank = sa("column", [P, TILES, E]), sa("rank", [P, TILES, E])
            ones_row = sa("ones_row", [P, TILES])
            places = sa("places", [P, TILES])
            second = sa("second", [P, TILES, E])
            scatter_to = sa("scatter_to", [P, TILES, 2])
            r_st, r_mv = sa("r_st", [P, 1, 6]), sa("r_mv", [P, 1, 2])
            r_h, r_y, r_yy = sa("r_h", [P, 1]), sa("r_y", [P, 1]), sa("r_yy", [P, 1])
            r_tok, r_rows = sa("r_tok", [P, 1, D]), sa("r_rows", [P, 1, D])
            r_idx = sa("r_idx", [P, 1, 2], U32)
            total_ps = ps("total_ps", [P, 512])
            before_ps = [ps(f"before_ps{i}", [P, 512]) for i in range(2)]
            column_ps = [ps(f"column_ps{i}", [P, 512]) for i in range(2)]
            r_chain, l_chain = sem("r_chain"), sem("l_chain")
            counted, totals, marks, ranked = sem("counted"), sem("totals"), sem("marks"), sem("ranked")
            r_ready, r_free, rescattered = sem("r_ready"), sem("r_free"), sem("rescattered")
            LOOP_CHAIN = 8
            TILE_CHAIN = 1 + 6 + 3 * NEWTON_STEPS

            block = part.enter_context(nc.Block())

            @block.vector
            def _(dve):
                with dve.If(dve.value_load(most[0:1, 0:1], min_val=0, max_val=T) > CAP):
                    whole = [P, TILES, E]
                    sel1, chosen = record[:, :, 0:E], record[:, :, E:2 * E]
                    chain = Chain(dve, r_chain, 0)
                    nc.vector.memset(threshold[:, :], 0.0)
                    nc.vector.memset(ones_row[:, :], 1.0)
                    chain.step(nc.vector.memset(step_size[:, :], float(1 << 24)))
                    chain.step(nc.vector.tensor_scalar(priority[:, :], record[:, :, 2 * E], float(1 << 24), None, ALU.mult))
                    with dve.Fori(0, SEARCH_STEPS) as k:
                        loop = Chain(dve, l_chain, LOOP_CHAIN * k)
                        loop.step(nc.vector.tensor_scalar(candidate[:, :], threshold[:, :], step_size[:, 0:1], None, ALU.add))
                        loop.step(nc.vector.tensor_tensor(hits[:, :, :], over_rows(priority[:, :], whole),
                                                          over_tiles(candidate[:, :], whole), ALU.is_ge))
                        loop.step(nc.vector.tensor_tensor(hits[:, :, :], hits[:, :, :], chosen, ALU.mult))
                        loop.step(nc.vector.tensor_reduce(hits_f[:, :], hits[:, :, :].rearrange("p t e -> p e t"), AX,
                                                          ALU.add))
                        nc.vector.tensor_copy(hits_bf[:, :], hits_f[:, :]).then_inc(counted, 1)
                        dve.wait_ge(totals, k + 1)
                        loop.step(nc.vector.tensor_scalar(raised[:, :], total_ps[:, 0:E], float(CAP), None, ALU.is_ge))
                        loop.step(nc.vector.tensor_scalar(raised[:, :], raised[:, :], step_size[:, 0:1], None, ALU.mult))
                        loop.step(nc.vector.tensor_tensor(threshold[:, :], threshold[:, :], raised[:, :], ALU.add))
                        loop.step(nc.vector.tensor_scalar(step_size[:, :], step_size[:, :], 0.5, None, ALU.mult))
                        assert loop.n == LOOP_CHAIN
                    for dst, op in ((above, ALU.is_gt), (ties, ALU.is_equal)):
                        chain.step(nc.vector.tensor_tensor(dst[:, :, :], over_rows(priority[:, :], whole),
                                                           over_tiles(threshold[:, :], whole), op))
                        chain.step(nc.vector.tensor_tensor(dst[:, :, :], dst[:, :, :], chosen, ALU.mult))
                    chain.step(nc.vector.tensor_reduce(hits_f[:, :], above[:, :, :].rearrange("p t e -> p e t"), AX, ALU.add))
                    nc.vector.tensor_copy(hits_bf[:, :], hits_f[:, :]).then_inc(counted, 1)
                    dve.wait_ge(totals, SEARCH_STEPS + 1)
                    chain.step(nc.vector.tensor_scalar(candidate[:, :], total_ps[:, 0:E], -1.0, float(CAP), ALU.mult, ALU.add))

                    def rank_of(marks_f, n):
                        nc.vector.tensor_copy(marked[:, :, :], marks_f).then_inc(marks, 1)
                        dve.wait_ge(ranked, n)
                        for i in range(2):
                            c = slice(i * HALF, (i + 1) * HALF)
                            nc.vector.tensor_copy(column[:, c, :], column_ps[i][:, 0:HALF * E]
                                                  .rearrange("p (t e) -> p t e", e=E))
                            ins = nc.vector.tensor_copy(rank[:, c, :], before_ps[i][:, 0:HALF * E]
                                                        .rearrange("p (t e) -> p t e", e=E))
                        chain.step(ins)
                        chain.step(nc.vector.tensor_tensor(rank[:, :, :], rank[:, :, :], column[:, :, :], ALU.subtract))
                        for e in range(E):
                            ins = nc.vector.tensor_tensor_scan(hits[:, :, e], ones_row[:, :], column[:, :, e], 0.0,
                                                               ALU.mult, ALU.add)
                        chain.step(ins)
                        chain.step(nc.vector.tensor_tensor(rank[:, :, :], rank[:, :, :], hits[:, :, :], ALU.add))

                    rank_of(ties[:, :, :], 1)
                    chain.step(nc.vector.tensor_tensor(rank[:, :, :], rank[:, :, :], over_tiles(candidate[:, :], whole),
                                                       ALU.is_lt))
                    chain.step(nc.vector.tensor_tensor(ties[:, :, :], ties[:, :, :], rank[:, :, :], ALU.mult))
                    chain.step(nc.vector.tensor_tensor(above[:, :, :], above[:, :, :], ties[:, :, :], ALU.add))
                    rank_of(above[:, :, :], 2)
                    chain.step(nc.vector.tensor_tensor(rank[:, :, :], rank[:, :, :], over_tiles(expert_base[:, :], whole),
                                                       ALU.add))
                    chain.step(nc.vector.tensor_tensor(second[:, :, :], chosen, sel1, ALU.subtract))
                    for k, sel in enumerate((sel1, second[:, :, :])):
                        slot, weight = record[:, :, 2 * E + 2 + k], record[:, :, 2 * E + k]
                        chain.step(nc.vector.tensor_tensor(hits[:, :, :], sel, above[:, :, :], ALU.mult))
                        chain.step(nc.vector.tensor_reduce(places[:, :], hits[:, :, :], AX, ALU.add))
                        chain.step(nc.vector.tensor_tensor(weight, weight, places[:, :], ALU.mult))
                        chain.step(nc.vector.tensor_tensor(hits[:, :, :], hits[:, :, :], rank[:, :, :], ALU.mult))
                        chain.step(nc.vector.tensor_reduce(slot, hits[:, :, :], AX, ALU.add))
                        chain.step(nc.vector.tensor_scalar(places[:, :], places[:, :], -OUT_OF_BOUNDS, OUT_OF_BOUNDS,
                                                           ALU.mult, ALU.add))
                        chain.step(nc.vector.tensor_tensor(scatter_to[:, :, k], slot, places[:, :], ALU.add))
                    with dve.Fori(0, TILES) as c:
                        tile_chain = Chain(dve, l_chain, LOOP_CHAIN * SEARCH_STEPS + TILE_CHAIN * c)
                        dve.wait_ge(r_free, c + 1)
                        tile_chain.step(nc.vector.tensor_copy(r_tok[:, :, :], tokens[:, bass.ds(c, 1), :]))
                        nc.vector.tensor_copy(r_idx[:, :, :], scatter_to[:, bass.ds(c, 1), :])
                        layer_norm(tile_chain, r_tok, r_rows, r_st, r_mv, r_h, r_y, r_yy, 1).then_inc(r_ready, 1)
                        assert tile_chain.n == TILE_CHAIN

            @block.tensor
            def _(pe):
                with pe.If(pe.value_load(most[0:1, 0:1], min_val=0, max_val=T) > CAP):
                    with pe.Fori(0, SEARCH_STEPS + 1) as k:
                        pe.wait_ge(counted, k + 1)
                        nc.tensor.matmul(total_ps[:, 0:E], ones_bf[:, :], hits_bf[:, :], start=True, stop=True
                                         ).then_inc(totals, 1)
                    with pe.Fori(0, 2) as n:
                        pe.wait_ge(marks, n + 1)
                        for i in range(2):
                            src = marked[:, i * HALF:(i + 1) * HALF, :].rearrange("p t e -> p (t e)")
                            nc.tensor.matmul(before_ps[i][:, 0:HALF * E], before[:, :], src, start=True, stop=True)
                            ins = nc.tensor.matmul(column_ps[i][:, 0:HALF * E], ones_bf[:, :], src, start=True, stop=True)
                        ins.then_inc(ranked, 1)

            @block.gpsimd
            def _(pool):
                with pool.If(pool.value_load(most[0:1, 0:1], min_val=0, max_val=T) > CAP):
                    pool.sem_inc(r_free, 1)
                    with pool.Fori(0, TILES) as c:
                        pool.wait_ge(r_ready, c + 1)
                        alone(pool, spare)
                        for k in range(2):
                            pool.indirect_dma_start(slots_dram[:, :], bass.IndirectOffsetOnAxis(r_idx[:, 0, k:k + 1], 0),
                                                    r_rows[:, 0, :], None, bounds_check=E * CAPP - 1, oob_is_err=False
                                                    ).then_inc(rescattered, 16)
                        pool.wait_ge(rescattered, 32 * c + 32)
                        pool.sem_inc(r_free, 1)

        part = ExitStack()
        with part:
            def sa(name, shape, dt=FP32):
                return sb(name, shape, dt, part)

            def ps(name, shape, dt=FP32):
                return part.enter_context(nc.psum_tensor(name, shape, dt))

            w1_hi = [sa(f"w1_hi{i}", [P, HID]) for i in range(2)]
            w1_lo = [sa(f"w1_lo{i}", [D1, HID]) for i in range(2)]
            w2_sb = [sa(f"w2_sb{i}", [P, HT, D]) for i in range(2)]
            b1_sb = [sa(f"b1_sb{i}", [P, HT]) for i in range(2)]
            b2_sb = [sa(f"b2_sb{i}", [P, D]) for i in range(2)]
            rows = [sa(f"rows{i}", [P, NT, D]) for i in range(2)]
            rT_hi = [sa(f"rT_hi{i}", [P, GROUP]) for i in range(2)]
            rT_lo = [sa(f"rT_lo{i}", [D1, GROUP]) for i in range(2)]
            hT = sa("hT", [P, HT, GROUP])
            ex_out = [sa(f"ex_out{i}", [P, NT, D]) for i in range(2)]
            RG = 4
            assert TILES % RG == 0
            pick_w = sa("pick_w", [P, RG, 2])
            picks = [[sa(f"pick{k}_{i}", [P, D]) for i in range(RG)] for k in range(2)]
            pick_idx = sa("pick_idx", [P, RG, 2], U32)
            half = sa("half", [P, RG, D])
            result = [sa(f"result{i}", [P, D]) for i in range(RG)]

            HB = 3
            h_ps = [ps(f"h_ps{i}", [P, 512]) for i in range(HB)]
            rT_ps = [ps(f"rT_ps{i}", [P, 512]) for i in range(2)]
            ex_ps = [ps(f"ex_ps{i}", [P, 512]) for i in range(2)]

            w_in = [sem("w_in0"), sem("w_in1")]
            rows_in = [sem("rows_in0"), sem("rows_in1")]
            rT_ready, rT_sb = sem("rT_ready"), [sem("rT_sb_dve"), sem("rT_sb_act")]
            hidden_ps, hidden_sb = sem("hidden_ps"), sem("hidden_sb")
            ex_ready, ex_added = sem("ex_ready"), sem("ex_added")
            stored = [sem("stored0"), sem("stored1")]
            idx_ready = sem("idx_ready")
            pick_in = [sem(f"pick_in{i}") for i in range(RG)]
            half_sum, result_ready = sem("half_sum"), sem("result_ready")
            out_stored = [sem(f"out_stored{i}") for i in range(RG)]

            def each_step(eng, step, per_expert=None):
                with eng.Fori(0, E // 2) as pair:
                    for ep in range(2):
                        if per_expert:
                            per_expert(pair, ep)
                        with eng.Fori(0, GPE // 2) as j:
                            for par in range(2):
                                step(GPE * (2 * pair + ep) + 2 * j + par, par, ep)

            block = part.enter_context(nc.Block())

            def slot_rows(table, g):
                return table[bass.ds(g * GROUP, GROUP), :].rearrange("(p r) d -> p r d", p=P)

            @block.sync
            def _(sp):
                for s in stored + out_stored:
                    sp.sem_inc(s, 1)
                sp.dma_start(rows[0][:, :, :], slot_rows(slots_dram, 0)).then_inc(rows_in[0], 16)

                def step(g, par, ep):
                    sp.wait_ge(rT_ready, g + 1)
                    sp.dma_start(rows[1 - par][:, :, :], slot_rows(slots_dram, g + 1)).then_inc(rows_in[1 - par], 16)
                    sp.wait_ge(ex_added, g + 2)
                    sp.dma_start(slot_rows(expert_dram, g), ex_out[par][:, :, :]).then_inc(stored[par], 16)

                each_step(sp, step)
                sp.wait_ge(rows_in[0], 16 * (E * GPE // 2 + 1))
                out_rows = out.rearrange("b s d -> (b s) d")
                with sp.Fori(0, TILES // RG) as k:
                    for i in range(RG):
                        sp.wait_ge(result_ready, RG * k + i + 1)
                        sp.dma_start(out_rows[bass.ds((RG * k + i) * P, P), :], result[i][:, :]
                                     ).then_inc(out_stored[i], 16)
                for i in range(RG):
                    sp.wait_ge(out_stored[i], 16 * (TILES // RG) + 1)

            @block.gpsimd
            def _(pool):
                def weights(e, ep):
                    for dst, src in (
                        (w1_hi[ep][:, :], w1[bass.ds(e, 1), 0:P, :].rearrange("o m k -> (o m) k")),
                        (w1_lo[ep][:, :], w1[bass.ds(e, 1), P:D, :].rearrange("o m k -> (o m) k")),
                        (w2_sb[ep][:, :, :], w2[bass.ds(e, 1), :, :].rearrange("o (c p) d -> (o p) c d", p=P)),
                        (b1_sb[ep][:, :], b1[bass.ds(e, 1), :].rearrange("o (c p) -> (o p) c", p=P)),
                        (b2_sb[ep][:, :], b2[bass.ds(e, 1), :].to_broadcast([P, D])),
                    ):
                        pool.dma_start(dst, src, allow_slow_non_contiguous=True).then_inc(w_in[ep], 16)

                weights(0, 0)
                weights(1, 1)
                with pool.Fori(1, E // 2) as pair:
                    for ep in range(2):
                        pool.wait_ge(ex_added, GPE * (2 * pair + ep - 1) + 1)
                        alone(pool, spare)
                        weights(2 * pair + ep, ep)
                for par in range(2):
                    pool.wait_ge(stored[par], 16 * (E * GPE // 2) + 1)
                with pool.Fori(0, TILES // RG) as k:
                    for i in range(RG):
                        pool.wait_ge(idx_ready, RG * k + i + 1)
                        alone(pool, spare)
                        for c in range(2):
                            pool.indirect_dma_start(picks[c][i][:, :], None, expert_dram[:, :],
                                                    bass.IndirectOffsetOnAxis(pick_idx[:, i, c:c + 1], 0),
                                                    bounds_check=E * CAPP - 1, oob_is_err=False
                                                    ).then_inc(pick_in[i], 16)

            @block.scalar
            def _(act):
                def move_lo(src_par):
                    nc.scalar.activation(rT_lo[src_par][:, :], rT_ps[1][0:D1, 0:GROUP], ACT.Copy).then_inc(rT_sb[1], 1)

                act.wait_ge(rT_ready, 1)
                move_lo(0)

                def weights_there(pair, ep):
                    act.wait_ge(w_in[ep], 80 * pair + 80)
                    alone(act, spare)

                def step(g, par, ep):
                    for m in range(HT):
                        act.wait_ge(hidden_ps, HT * g + m + 1)
                        nc.scalar.activation(hT[:, m, :], h_ps[m % HB][:, 0:GROUP], ACT.Gelu, bias=b1_sb[ep][:, m:m + 1]
                                             ).then_inc(hidden_sb, 1)
                    act.wait_ge(rT_ready, g + 2)
                    move_lo(1 - par)

                each_step(act, step, weights_there)

            @block.vector
            def _(dve):
                dve.sem_inc(hidden_sb, HB)
                dve.sem_inc(ex_added, 1)

                def move_hi(par):
                    nc.vector.tensor_copy(rT_hi[par][:, :], rT_ps[0][:, 0:GROUP]).then_inc(rT_sb[0], 1)

                dve.wait_ge(rT_ready, 1)
                move_hi(0)

                def weights_there(pair, ep):
                    dve.wait_ge(w_in[ep], 80 * pair + 80)
                    alone(dve, spare)

                def step(g, par, ep):
                    dve.wait_ge(rT_ready, g + 2)
                    move_hi(1 - par)
                    dve.wait_ge(ex_ready, g + 1)
                    dve.wait_ge(stored[par], 8 * (g - par) + 1)
                    for lo, hi in ((0, 2), (2, NT)):
                        ins = nc.vector.tensor_tensor(
                            ex_out[par][:, lo:hi, :], ex_ps[lo // 2][:, 0:(hi - lo) * D].rearrange("p (t d) -> p t d", d=D),
                            over_tiles(b2_sb[ep][:, :], [P, hi - lo, D]), ALU.add)
                    ins.then_inc(ex_added, 1)

                each_step(dve, step, weights_there)

                def fetch(c, i):
                    nc.vector.tensor_copy(pick_w[:, i:i + 1, :], record[:, bass.ds(c, 1), 2 * E:2 * E + 2])
                    nc.vector.tensor_copy(pick_idx[:, i:i + 1, :], record[:, bass.ds(c, 1), 2 * E + 2:REC]
                                          ).then_inc(idx_ready, 1)

                def combine(k, i):
                    c = RG * k + i
                    dve.wait_ge(pick_in[i], 32 * k + 32)
                    dve.wait_ge(idx_ready, c + 1)
                    nc.vector.scalar_tensor_tensor(half[:, i:i + 1, :], picks[0][i][:, :].rearrange("p (o d) -> p o d", o=1),
                                                   pick_w[:, i, 0:1], tokens[:, bass.ds(c, 1), :], ALU.mult, ALU.add
                                                   ).then_inc(half_sum, 1)
                    dve.wait_ge(half_sum, c + 1)
                    dve.wait_ge(out_stored[i], 16 * k + 1)
                    nc.vector.scalar_tensor_tensor(result[i][:, :], picks[1][i][:, :], pick_w[:, i, 1:2], half[:, i, :],
                                                   ALU.mult, ALU.add).then_inc(result_ready, 1)

                for i in range(RG):
                    fetch(i, i)
                with dve.Fori(0, TILES // RG - 1) as k:
                    for i in range(RG):
                        combine(k, i)
                        dve.wait_ge(result_ready, RG * k + i + 1)
                        fetch(RG * k + i + RG, i)
                for i in range(RG):
                    combine(TILES // RG - 1, i)

            @block.tensor
            def _(pe):
                def transposes(par):
                    for r in range(NT):
                        nc.tensor.transpose(rT_ps[0][:, r * P:r * P + P], rows[par][:, r, 0:P], ident[:, :])
                    for r in range(NT):
                        ins = nc.tensor.transpose(rT_ps[1][0:D1, r * P:r * P + P], rows[par][:, r, P:D], ident[:, :])
                    ins.then_inc(rT_ready, 1)

                pe.wait_ge(rows_in[0], 16)
                transposes(0)

                def weights_there(pair, ep):
                    pe.wait_ge(w_in[ep], 80 * pair + 80)
                    alone(pe, spare)

                def step(g, par, ep):
                    for k in range(2):
                        pe.wait_ge(rT_sb[k], g + 1)
                    for m in range(HT):
                        c = slice(m * P, m * P + P)
                        dst = h_ps[m % HB][:, 0:GROUP]
                        pe.wait_ge(hidden_sb, HT * g + m + 1)
                        nc.tensor.matmul(dst, w1_hi[ep][:, c], rT_hi[par][:, :], start=True, stop=False)
                        nc.tensor.matmul(dst, w1_lo[ep][:, c], rT_lo[par][:, :], start=False, stop=True
                                         ).then_inc(hidden_ps, 1)
                    pe.wait_ge(rows_in[1 - par], 8 * (g - par) + 16 + 16 * par)
                    transposes(1 - par)
                    pe.wait_ge(ex_added, g + 1)
                    for r in range(NT):
                        dst = ex_ps[r // 2][:, (r % 2) * D:(r % 2) * D + D]
                        for m in range(HT):
                            if r == 0:
                                pe.wait_ge(hidden_sb, HB + HT * g + m + 1)
                            ins = nc.tensor.matmul(dst, hT[:, m, r * P:r * P + P], w2_sb[ep][:, m, :],
                                                   start=(m == 0), stop=(m == HT - 1))
                    ins.then_inc(ex_ready, 1)

                each_step(pe, step, weights_there)


_INS = ["x", "L0_attn_W_Q", "L0_attn_W_K", "L0_attn_W_V", "L0_attn_W_O", "L0_ffn_Wg", "L0_ffn_W1", "L0_ffn_b1",
        "L0_ffn_W2", "L0_ffn_b2"]


def kernel(**inputs):
    import numpy as np
    import concourse.bacc as bacc
    from concourse.bass_utils import run_bass_kernel_spmd

    nc = bacc.Bacc("TRN2", target_bir_lowering=False, num_devices=1)
    arrays, args = {}, []
    for name in _INS:
        a = np.ascontiguousarray(inputs[name])
        arrays[f"in_{name}"] = a
        args.append(nc.dram_tensor(f"in_{name}", a.shape, mybir.dt.from_np(a.dtype), kind="ExternalInput").ap())
    batches, rows, width = inputs["x"].shape
    span = SEG * DILATION
    shape = (batches, -(-rows // span) * SEG, width)
    out = nc.dram_tensor("out_dram", shape, FP32, kind="ExternalOutput").ap()
    audio_tower_kernel(nc, *args, out)
    r = run_bass_kernel_spmd(nc, [arrays], core_ids=[0])
    return r.results[0]["out_dram"]
```

```python
import concourse.bass as bass
from concourse import mybir
from contextlib import ExitStack

FP32 = mybir.dt.float32
BF16 = mybir.dt.bfloat16
FP16 = mybir.dt.float16
U32 = mybir.dt.uint32
I32 = mybir.dt.int32
ALU = mybir.AluOpType
ACT = mybir.ActivationFunctionType
AX = mybir.AxisListType.X

P = 128
SEG = 64
DILATION = 2
LN_EPS = 1e-5
RSQRT_SEED = float(0x5F3759DF)
NEWTON_STEPS = 3
MASKED = -1e30
X_SCALE = 2.0 ** 8
W_SCALE = 2.0 ** 8
QK_SCALE = 2.0 ** 5
H_SCALE = 2.0 ** 6
OUT_OF_BOUNDS = float(1 << 20)
CAPACITY_RATIO = 1.25
TOP_K = 2
SEARCH_STEPS = 26


def after(eng, sem, count):
    if not (isinstance(count, int) and count <= 0):
        eng.wait_ge(sem, count)


def alone(eng, sem):
    eng.sem_inc(sem, 1)


def over_rows(ap, shape):
    return ap.rearrange("p (t o) -> p t o", o=1).to_broadcast(shape)


def over_tiles(ap, shape):
    return ap.rearrange("p (o n) -> p o n", o=1).to_broadcast(shape)


class Chain:

    def __init__(self, eng, sem, base):
        self.eng, self.sem, self.base, self.n = eng, sem, base, 0

    def step(self, ins):
        self.n += 1
        ins.then_inc(self.sem, 1)
        self.eng.wait_ge(self.sem, self.base + self.n)


def audio_tower_kernel(nc, x, wq, wk, wv, wo, wg, w1, b1, w2, b2, out):
    B, S_IN, D = x.shape
    H, _, DK = wq.shape
    E, _, HID = w1.shape
    S = -(-S_IN // (SEG * DILATION)) * SEG
    REAL = -(-S_IN // DILATION)
    NT = S // P
    TILES = B * NT
    T = B * S
    CAP = int(CAPACITY_RATIO * T * TOP_K / E)
    GROUP = NT * P
    GPE = -(-CAP // (2 * GROUP)) * 2
    CAPP = GPE * GROUP
    D1 = D - P
    PAIRS = H // 2
    HT = HID // P
    UNITS = H * NT
    PROJ = 2 * PAIRS + 2 * NT
    VH = H * DK // 2
    TOK_SCALE = float(D) ** -0.5
    QK_OUT = QK_SCALE / (X_SCALE * W_SCALE)
    V_OUT = 1 / (X_SCALE * W_SCALE)
    S_OUT = float(DK) ** -0.5 / QK_SCALE ** 2
    H_OUT = 1 / (X_SCALE * W_SCALE)
    EX_OUT = 1 / (H_SCALE * W_SCALE)
    REC = 2 * E + 4
    assert S == NT * P and D1 == 64 and DK == 64 and B % 2 == 0 and UNITS % 4 == 0

    slots_dram = nc.dram_tensor("slots_dram", (E * CAPP + GROUP, 2 * D), FP16).ap()
    expert_dram = nc.dram_tensor("expert_dram", (E * CAPP, D), FP32).ap()

    top = ExitStack()
    with top:
        def sb(name, shape, dt=FP32, ctx=top):
            return ctx.enter_context(nc.sbuf_tensor(name, shape, dt))

        def sem(name):
            return top.enter_context(nc.semaphore(name))

        tokens = sb("tokens", [P, TILES, D])
        record = sb("record", [P, TILES, REC])
        ident = sb("ident", [P, P])
        ident_bf = sb("ident_bf", [P, P], BF16)
        ident16 = sb("ident16", [P, P], FP16)
        before = sb("before", [P, P], BF16)
        ones_bf = sb("ones_bf", [P, P], BF16)
        running = sb("running", [P, 2, E])
        expert_base = sb("expert_base", [P, E])
        first_wins = sb("first_wins", [P, E])
        most = sb("most", [P, 1], I32)
        spare = sem("spare")

        def layer_norm(chain, src, dst, st, mv, half_var, y, yy, n):
            alone(chain.eng, spare)
            for t in range(n):
                ins = nc.vector.bn_stats(st[:, t, :], src[:, t, :])
            chain.step(ins)
            alone(chain.eng, spare)
            for t in range(n):
                ins = nc.vector.bn_aggr(mv[:, t, :], st[:, t, :])
            chain.step(ins)
            var = mv[:, 0:n, 1]
            chain.step(nc.vector.tensor_scalar(half_var[:, 0:n], var, LN_EPS, X_SCALE ** -2, ALU.add, ALU.mult))
            chain.step(nc.vector.tensor_scalar(yy[:, 0:n].bitcast(I32), half_var[:, 0:n].bitcast(I32), 1, None,
                                               ALU.logical_shift_right))
            chain.step(nc.vector.tensor_scalar(y[:, 0:n].bitcast(I32), yy[:, 0:n].bitcast(I32), -1.0, RSQRT_SEED,
                                               ALU.mult, ALU.add))
            chain.step(nc.vector.tensor_scalar(half_var[:, 0:n], half_var[:, 0:n], -0.5, None, ALU.mult))
            for _ in range(NEWTON_STEPS):
                chain.step(nc.vector.tensor_tensor(yy[:, 0:n], y[:, 0:n], y[:, 0:n], ALU.mult))
                chain.step(nc.vector.tensor_tensor(yy[:, 0:n], yy[:, 0:n], half_var[:, 0:n], ALU.mult))
                chain.step(nc.vector.scalar_tensor_tensor(y[:, 0:n], yy[:, 0:n], 1.5, y[:, 0:n], ALU.add, ALU.mult))
            for t in range(n):
                ins = nc.vector.tensor_scalar(dst[:, t, :], src[:, t, :], mv[:, t, 0:1], y[:, t:t + 1],
                                              ALU.subtract, ALU.mult)
            return ins

        def split_tokens(chain, src, dst):
            chain.step(nc.vector.tensor_copy(dst[:, :, 0:D], src[:, :, :]))
            nc.vector.tensor_tensor(dst[:, :, D:2 * P], src[:, :, P:D], dst[:, :, P:D], ALU.subtract)
            return nc.vector.tensor_tensor(dst[:, :, 2 * P:2 * D], src[:, :, 0:P], dst[:, :, 0:P], ALU.subtract)

        def split_weights(chain, first, last, hi, lo, hi_twice, lo_last):
            nc.vector.tensor_scalar(hi_twice, last, W_SCALE, None, ALU.mult)
            chain.step(nc.vector.tensor_scalar(hi, first, W_SCALE, None, ALU.mult))
            nc.vector.scalar_tensor_tensor(lo, first, W_SCALE, hi, ALU.mult, ALU.subtract)
            return nc.vector.scalar_tensor_tensor(lo_last, last[0:D1], W_SCALE, hi_twice[0:D1], ALU.mult, ALU.subtract)

        def product(w, wc, xT, xc, dst, weights_move):
            w_hi, w_lo, w_twice, w_last = w
            terms = ((w_hi[:, wc], xT[:, 0, xc]), (w_lo[:, wc], xT[:, 0, xc]), (w_hi[:, wc], xT[:, 2, xc]),
                     (w_twice[:, wc], xT[:, 1, xc]), (w_last[:, wc], xT[0:D1, 1, xc]))
            for i, (a, b) in enumerate(terms):
                if weights_move:
                    a, b = b, a
                ins = nc.tensor.matmul(dst, a, b, start=(i == 0), stop=(i == len(terms) - 1))
            return ins

        part = ExitStack()
        with part:
            def sa(name, shape, dt=FP32):
                return sb(name, shape, dt, part)

            def ps(name, shape, dt=FP32):
                return part.enter_context(nc.psum_tensor(name, shape, dt))

            def w16(name, n, own_last=True):
                return [sa(name + "_hi", [P, n], FP16), sa(name + "_lo", [P, n], FP16),
                        sa(name + "_twice", [P, n], FP16), sa(name + "_last", [D1, n], FP16) if own_last else None]

            w_q, w_k, w_v, w_g = w16("w_q", H * DK, False), w16("w_k", H * DK), w16("w_v", H * DK), w16("w_g", E)
            wo_sb = sa("wo_sb", [P, PAIRS, D])
            wg_raw = sa("wg_raw", [P, 2, E])
            causal = sa("causal", [P, P], BF16)
            own_segment = sa("own_segment", [P, P])
            zeros = sa("zeros", [P, 2 * D], FP16)

            xin = [sa(f"xin{i}", [P, NT, D]) for i in range(2)]
            both_last = sa("both_last", [P, H * DK], FP16)
            xsT_first, xsT_last = sa("xsT_first", [P, S]), both_last[D1:P, :].bitcast(FP32)[:, 0:S]
            w_q[3] = both_last[0:D1, :]
            tok_max, tok_sum, tok_inv = sa("tok_max", [P, NT]), sa("tok_sum", [P, NT]), sa("tok_inv", [P, NT])
            st, mv = sa("st", [P, NT, 6]), sa("mv", [P, NT, 2])
            ln_h, ln_y, ln_yy = sa("ln_h", [P, NT]), sa("ln_y", [P, NT]), sa("ln_yy", [P, NT])
            xn = sa("xn", [P, NT, D])
            xs = sa("xs", [P, NT, 2 * D], FP16)
            xT = sa("xT", [P, 3, S], FP16)
            QT = [[sa(f"QT_{k}{i}", [P, PAIRS, S], FP16) for k in ("hi", "lo")] for i in range(2)]
            KT = [[sa(f"KT_{k}{i}", [P, PAIRS, S], FP16) for k in ("hi", "lo")] for i in range(2)]
            V = [sa(f"V{i}", [P, NT, H * DK]) for i in range(2)]
            NR = 4
            neg_max = sa("neg_max", [P, NR])
            unread = sa("unread", [P, 2, S], BF16)
            prob = sa("prob", [P, NR, S])
            probT = sa("probT", [P, NR, S])
            row_sum = sa("row_sum", [P, H, NT])
            row_inv = sa("row_inv", [P, H, NT])
            O_sb = sa("O_sb", [P, 2, NT, P])
            OT = sa("OT", [P, PAIRS, S])
            st2, mv2 = sa("st2", [P, NT, 6]), sa("mv2", [P, NT, 2])
            ln_h2, ln_y2, ln_yy2 = sa("ln_h2", [P, NT]), sa("ln_y2", [P, NT]), sa("ln_yy2", [P, NT])
            xs2 = [sa(f"xs2_{i}", [P, NT, 2 * D], FP16) for i in range(2)]
            x2T = sa("x2T", [P, 3, S], FP16)
            tok_s, tok_p, tok_pT = (big[:, :, :].rearrange("p k s -> p (k s)").bitcast(FP32)[:, 0:NT * P]
                                    .rearrange("p (t k) -> p t k", t=NT) for big in (xs, xT, x2T))
            lg, lg2 = sa("lg", [P, NT, E]), sa("lg2", [P, NT, E])
            key = sa("key", [P, NT, E])
            top1, top2, key_max = sa("top1", [P, NT]), sa("top2", [P, NT]), sa("key_max", [P, NT])
            gap, gap_exp, gap_sum = sa("gap", [P, NT]), sa("gap_exp", [P, NT]), sa("gap_sum", [P, NT])
            rec = sa("rec", [P, NT, REC])
            sel2 = sa("sel2", [P, NT, E])
            chosen_bf = sa("chosen_bf", [P, NT, E], BF16)
            pos, late = sa("pos", [P, NT, E]), sa("late", [P, NT, E])
            picked = sa("picked", [P, NT, E])
            slot_idx = [sa(f"slot_idx{i}", [P, NT, 2], U32) for i in range(2)]

            S_ps = [ps(f"S_ps{i}", [P, 512]) for i in range(2)]
            T_ps = [ps(f"T_ps{i}", [P, 512]) for i in range(2)]
            O_ps = ps("O_ps", [P, 512])
            FA, FB = ps("FA", [P, 512]), ps("FB", [P, 512])
            TA = ps("TA", [P, 512])
            O_view = O_ps[:, 0:NT * P].rearrange("p (t c) -> p t c", t=NT)

            zero_ready, const_pool, consts = sem("zero_ready"), sem("const_pool"), sem("consts")
            weights_in = sem("weights_in")
            x_in = [sem("x_in0"), sem("x_in1")]
            rows_zeroed = sem("rows_zeroed")
            xsT_ps, xsT_first_sb, xsT_last_sb = sem("xsT_ps"), sem("xsT_first_sb"), sem("xsT_last_sb")
            tok_scores, tok_max_ready, tok_exp = sem("tok_scores"), sem("tok_max_ready"), sem("tok_exp")
            tok_pT_ps, tok_pT_sb, tok_mixed = sem("tok_pT_ps"), sem("tok_pT_sb"), sem("tok_mixed")
            raw_in, split = sem("raw_in"), sem("split")
            xn_ready, xnT_ps, xT_sb = sem("xn_ready"), sem("xnT_ps"), [sem("xT_sb_act"), sem("xT_sb_dve")]
            proj_ps, qk_hi, qk_sb = sem("proj_ps"), sem("qk_hi"), sem("qk_sb")
            v_sb = [sem("v_sb_act"), sem("v_sb_dve")]
            scores, max_ready, exp_done = sem("scores"), sem("max_ready"), sem("exp_done")
            probT_ps = sem("probT_ps")
            probT_sb = [sem("probT_sb_dve"), sem("probT_sb_act")]
            attended, normed = sem("attended"), sem("normed")
            OT_ps, OT_sb = sem("OT_ps"), sem("OT_sb")
            wo_ps, wo_added = sem("wo_ps"), sem("wo_added")
            xn2_ready, x2T_ps, x2T_sb = sem("xn2_ready"), sem("x2T_ps"), sem("x2T_sb")
            totals_ready = sem("totals_ready")
            logits_ps, logits_sb, ranks_sb = sem("logits_ps"), sem("logits_sb"), sem("ranks_sb")
            gap_ready, gap_exped = sem("gap_ready"), sem("gap_exped")
            chosen_ready, ranks_ps, slots_ready = sem("chosen_ready"), sem("ranks_ps"), sem("slots_ready")
            xn2_free = sem("xn2_free")
            scattered = [sem("scattered0"), sem("scattered1")]
            front_chain, tail_chain, norm_chain = sem("front_chain"), sem("tail_chain"), sem("norm_chain")

            LN_STEPS = 6 + 3 * NEWTON_STEPS
            FRONT_STEPS = 3 + LN_STEPS + 2
            TAIL_STEPS = LN_STEPS + 2 + 5 + 1 + 5 + 2 + 4 + 4

            F_XT, F_SCORE, F_PT, F_MIX, F_XNT, F_PROJ = 1, 3, 6, 8, 13, UNITS - PROJ
            T_WO, T_X2T, T_LOGIT, T_RANK = 4, 9, 12, 16
            PAIR = 2 * NT

            def alternate(b, par, first, last, unit, front, tail):
                for n in range(UNITS):
                    unit(b, par, n, first, last)
                    if not last:
                        front(b + 1, 1 - par, n)
                    if not first:
                        tail(b - 1, 1 - par, n)

            def run(eng, unit, front, tail):
                for n in range(UNITS):
                    front(0, 0, n)
                alternate(0, 0, True, False, unit, front, tail)
                if B > 2:
                    with eng.Fori(0, B // 2 - 1) as j:
                        for u in range(2):
                            alternate(2 * j + 1 + u, (1 + u) % 2, False, False, unit, front, tail)
                alternate(B - 1, 1, False, True, unit, front, tail)

            block = part.enter_context(nc.Block())

            @block.sync
            def _(sp):
                for i, w in enumerate((wq, wk, wv)):
                    for k, (lo, hi, rows) in enumerate(((0, P, slice(0, P)), (P, D, slice(0, D1)), (P, D, slice(D1, P)))):
                        n = (2 * i + min(k, 1))
                        sp.dma_start((V[0], V[1])[n // 3][rows, n % 3, :].rearrange("p (h k) -> p h k", h=H),
                                     w[:, lo:hi, :].rearrange("h m k -> m h k")).then_inc(raw_in, 16)
                for k, (lo, hi, rows) in enumerate(((0, P, slice(0, P)), (P, D, slice(0, D1)), (P, D, slice(D1, P)))):
                    sp.dma_start(wg_raw[rows, min(k, 1), :], wg[lo:hi, :]).then_inc(raw_in, 16)
                sp.dma_start(wo_sb[:, :, :], wo.rearrange("(c p) d -> p c d", p=P)).then_inc(weights_in, 16)
                sp.wait_ge(zero_ready, 1)

                LAST = REAL - (NT - 1) * P

                def load(b, par):
                    xb = x[bass.ds(b, 1), :, :].rearrange("o (s two) d -> (o s) two d", two=DILATION)
                    full = (NT - 1) * P
                    sp.dma_start(xin[par][:, 0:NT - 1, :],
                                 xb[0:full, 0, :].rearrange("(t p) d -> p t d", p=P)).then_inc(x_in[par], 16)
                    sp.dma_start(xin[par][0:LAST, NT - 1, :], xb[full:REAL, 0, :]).then_inc(x_in[par], 16)

                def zero_rows(k):
                    for e in range(E):
                        sp.dma_start(slots_dram[bass.ds(k * GROUP + e * CAPP, GROUP), :]
                                     .rearrange("(p r) d -> p r d", p=P), over_tiles(zeros[:, :], [P, NT, 2 * D])
                                     ).then_inc(rows_zeroed, 16)

                load(0, 0)
                load(1, 1)
                sp.dma_start(slots_dram[E * CAPP:E * CAPP + GROUP, :].rearrange("(p r) d -> p r d", p=P),
                             over_tiles(zeros[:, :], [P, NT, 2 * D])).then_inc(rows_zeroed, 16)
                for turns, fill in ((range(1, GPE // 2 + 1), True), (range(GPE // 2 + 1, B // 2), False)):
                    if not len(turns):
                        continue
                    with sp.Fori(turns.start, turns.stop) as j:
                        for par in range(2):
                            if fill:
                                zero_rows(2 * j - 2 + par)
                            sp.wait_ge(tok_mixed, 2 * j - 1 + par)
                            load(2 * j + par, par)

            @block.gpsimd
            def _(pool):
                nc.gpsimd.memset(ident[:, :], 0.0).then_inc(const_pool, 1)
                nc.gpsimd.memset(ident_bf[:, :], 0.0).then_inc(const_pool, 1)
                nc.gpsimd.memset(ident16[:, :], 0.0).then_inc(const_pool, 1)
                nc.gpsimd.memset(before[:, :], 1.0).then_inc(const_pool, 1)
                nc.gpsimd.memset(causal[:, :], 0.0).then_inc(const_pool, 1)
                pool.wait_ge(const_pool, 5)
                for m in (ident, ident_bf, ident16):
                    nc.gpsimd.affine_select(out=m[:, :], in_=m[:, :], compare_op=ALU.not_equal, fill=1.0, base=0,
                                            pattern=[[-1, P]], channel_multiplier=1).then_inc(consts, 1)
                nc.gpsimd.affine_select(out=before[:, :], in_=before[:, :], compare_op=ALU.is_gt, fill=0.0, base=0,
                                        pattern=[[1, P]], channel_multiplier=-1).then_inc(consts, 1)
                nc.gpsimd.affine_select(out=causal[:, :], in_=causal[:, :], compare_op=ALU.is_ge, fill=MASKED, base=0,
                                        pattern=[[-1, P]], channel_multiplier=1).then_inc(consts, 1)

                pool.sem_inc(xn2_free, 2)

                def scatter(b, par, zeroed):
                    pool.wait_ge(slots_ready, b + 1)
                    if zeroed is not None:
                        pool.wait_ge(rows_zeroed, zeroed)
                    alone(pool, spare)
                    for t in range(NT):
                        for k in range(2):
                            pool.indirect_dma_start(
                                slots_dram[:, :], bass.IndirectOffsetOnAxis(slot_idx[par][:, t, k:k + 1], 0),
                                xs2[par][:, t, :], None, bounds_check=E * CAPP - 1, oob_is_err=False
                            ).then_inc(scattered[par], 16)
                    pool.wait_ge(scattered[par], NT * 16 * (b - par) + 2 * NT * 16)
                    pool.sem_inc(xn2_free, 1)

                with pool.Fori(0, GPE // 2) as j:
                    for par in range(2):
                        scatter(2 * j + par, par, 16 + 16 * E * (2 * j + par + 1))
                if B > GPE:
                    with pool.Fori(GPE // 2, B // 2) as j:
                        for par in range(2):
                            scatter(2 * j + par, par, None)
                pool.wait_ge(rows_zeroed, 16 + 16 * E * GPE)

            @block.scalar
            def _(act):
                def front(b, par, n):
                    if n == F_XT:
                        act.wait_ge(xsT_ps, b + 1)
                        nc.scalar.activation(xsT_first[:, :], FA[:, 0:S], ACT.Copy).then_inc(xsT_first_sb, 1)
                    if n == F_SCORE:
                        act.wait_ge(tok_max_ready, b + 1)
                        for t in range(NT):
                            nc.scalar.activation(tok_p[:, t, :], tok_s[:, t, :], ACT.Exp, bias=tok_max[:, t:t + 1],
                                                 accum_out=tok_sum[:, t:t + 1]).then_inc(tok_exp, 1)
                    if n == F_XNT:
                        act.wait_ge(xnT_ps, b + 1)
                        nc.scalar.activation(xT[:, 0:2, :], FA[:, 0:S].bitcast(FP16).rearrange("p (k s) -> p k s", k=2),
                                             ACT.Copy).then_inc(xT_sb[0], 1)
                    q = n - F_PROJ
                    if 0 <= q and (q < 2 * PAIRS or q % 2 == 0):
                        act.wait_ge(proj_ps, PROJ * b + q + 1)
                        if q == 0:
                            after(act, attended, UNITS * (b - 1))
                        src = (FA, FB)[q % 2]
                        if q < 2 * PAIRS:
                            dst = (QT, KT)[q // PAIRS][par][0][:, q % PAIRS, :]
                            nc.scalar.activation(dst, src[:, 0:S], ACT.Copy, scale=QK_OUT).then_inc(qk_hi, 1)
                        else:
                            t, half = divmod(q - 2 * PAIRS, 2)
                            nc.scalar.activation(V[par][:, t, half * VH:half * VH + VH], src[:, 0:VH], ACT.Copy,
                                                 scale=V_OUT).then_inc(v_sb[0], 1)

                def exp_unit(b, par, n):
                    g = UNITS * b + n
                    h, t = divmod(n, NT)
                    w = P * (t + 1)
                    act.wait_ge(max_ready, g + 1)
                    after(act, probT_ps, g - NR + 1)
                    nc.scalar.activation(prob[:, n % NR, 0:w], S_ps[n % 2][:, 0:w], ACT.Exp,
                                         bias=neg_max[:, n % NR:n % NR + 1], scale=S_OUT,
                                         accum_out=row_sum[:, h, t:t + 1]).then_inc(exp_done, 1)

                def unit(b, par, n, first, last):
                    g = UNITS * b + n
                    w = P * (n % NT + 1)
                    if first and n == 0:
                        exp_unit(b, par, 0)
                        exp_unit(b, par, 1)
                    if n % 2 == 1:
                        act.wait_ge(probT_ps, g + 1)
                        after(act, attended, g - NR + 1)
                        nc.scalar.activation(probT[:, n % NR, 0:w], T_ps[1][:, 0:w], ACT.Copy).then_inc(probT_sb[1], 1)
                    if n + 2 < UNITS:
                        exp_unit(b, par, n + 2)
                    elif not last:
                        exp_unit(b + 1, 1 - par, n + 2 - UNITS)

                def tail(b, par, n):
                    if n == T_LOGIT + 1:
                        act.wait_ge(gap_ready, b + 1)
                        nc.scalar.activation(gap_exp[:, :], gap[:, :], ACT.Exp).then_inc(gap_exped, 1)

                run(act, unit, front, tail)
                for n in range(UNITS):
                    tail(B - 1, 1, n)

            @block.vector
            def _(dve):
                nc.vector.memset(zeros[:, :], 0.0)
                nc.vector.memset(running[:, :, :], 0.0)
                nc.vector.memset(ones_bf[:, :], 1.0)
                nc.vector.memset(own_segment[:, :], 0.0)
                nc.vector.memset(xin[0][:, :, :], 0.0)
                nc.vector.memset(xin[1][:, :, :], 0.0).then_inc(zero_ready, 1)
                for e in range(E):
                    nc.vector.memset(expert_base[:, e:e + 1], float(e * CAPP))
                    nc.vector.memset(first_wins[:, e:e + 1], float(E - e))
                dve.wait_ge(zero_ready, 1)
                nc.vector.memset(own_segment[0:SEG, SEG:P], MASKED)
                nc.vector.memset(own_segment[SEG:P, 0:SEG], MASKED).then_inc(zero_ready, 1)
                dve.wait_ge(zero_ready, 2)

                split_chain = Chain(dve, split, 0)
                dve.wait_ge(raw_in, 16 * 12)
                for i, w in enumerate((w_q, w_k, w_v)):
                    raw = [(V[0], V[1])[n // 3][:, n % 3, :] for n in (2 * i, 2 * i + 1)]
                    split_weights(split_chain, raw[0], raw[1], *(t[:, :] for t in w))
                split_chain.step(split_weights(split_chain, wg_raw[:, 0, :], wg_raw[:, 1, :], *(t[:, :] for t in w_g)))

                chains = {}

                def front(b, par, n):
                    if n == 0:
                        chains["front"] = Chain(dve, front_chain, FRONT_STEPS * b)
                    chain = chains["front"]
                    if n == F_XT:
                        dve.wait_ge(xsT_ps, b + 1)
                        nc.vector.tensor_copy(xsT_last[:, :], FB[0:D1, 0:S]).then_inc(xsT_last_sb, 1)
                    if n == F_SCORE:
                        dve.wait_ge(tok_scores, b + 1)
                        chain.step(nc.vector.scalar_tensor_tensor(
                            tok_s[:, :, :], FA[:, 0:S].rearrange("p (t k) -> p t k", t=NT), TOK_SCALE,
                            over_tiles(own_segment[:, :], [P, NT, P]), ALU.mult, ALU.add))
                        nc.vector.tensor_reduce(tok_max[:, :], tok_s[:, :, :], AX, ALU.max,
                                                negate=True).then_inc(tok_max_ready, 1)
                    if n == F_PT:
                        dve.wait_ge(tok_pT_ps, b + 1)
                        nc.vector.tensor_copy(tok_pT[:, :, :], FB[:, 0:S].rearrange("p (t k) -> p t k", t=NT)
                                              ).then_inc(tok_pT_sb, 1)
                        dve.wait_ge(tok_exp, NT * (b + 1))
                        chain.step(nc.vector.reciprocal(tok_inv[:, :], tok_sum[:, :]))
                    if n == F_MIX:
                        dve.wait_ge(tok_mixed, b + 1)
                        for t in range(NT):
                            src = FA[:, t * D:t * D + D] if t < 2 else FB[:, 0:D]
                            ins = nc.vector.tensor_scalar(tokens[:, bass.ds(NT * b + t, 1), :],
                                                          src.rearrange("p (o d) -> p o d", o=1),
                                                          tok_inv[:, t:t + 1], None, ALU.mult)
                        chain.step(ins)
                        chain.step(layer_norm(chain, tokens[:, bass.ds(NT * b, NT), :], xn, st, mv, ln_h, ln_y, ln_yy, NT))
                        split_tokens(chain, xn, xs).then_inc(xn_ready, 1)
                        dve.wait_ge(xn_ready, b + 1)
                    if n == F_XNT:
                        dve.wait_ge(xnT_ps, b + 1)
                        nc.vector.tensor_copy(xT[:, 2, :], FB[:, 0:S // 2].bitcast(FP16)).then_inc(xT_sb[1], 1)
                    q = n - F_PROJ
                    if 0 <= q < 2 * PAIRS:
                        src = (FA, FB)[q % 2]
                        hi, lo = ((QT, KT)[q // PAIRS][par][k][:, q % PAIRS, :] for k in range(2))
                        dve.wait_ge(qk_hi, 2 * PAIRS * b + q + 1)
                        nc.vector.scalar_tensor_tensor(lo, src[:, 0:S], QK_OUT, hi, ALU.mult, ALU.subtract
                                                       ).then_inc(qk_sb, 1)
                    elif q >= 0 and q % 2:
                        t, half = divmod(q - 2 * PAIRS, 2)
                        dve.wait_ge(proj_ps, PROJ * b + q + 1)
                        nc.vector.tensor_scalar(V[par][:, t, half * VH:half * VH + VH], FB[:, 0:VH], V_OUT, None, ALU.mult
                                                ).then_inc(v_sb[1], 1)
                    if n == UNITS - 1:
                        assert chain.n == FRONT_STEPS, chain.n

                def max_unit(b, par, n):
                    g = UNITS * b + n
                    w = P * (n % NT + 1)
                    dve.wait_ge(scores, g + 1)
                    after(dve, exp_done, g - NR + 1)
                    nc.vector.tensor_scalar(unread[:, n % 2, 0:w], S_ps[n % 2][:, 0:w], -S_OUT, None, ALU.mult, ALU.min,
                                            accum_out=neg_max[:, n % NR:n % NR + 1]).then_inc(max_ready, 1)

                def norm_pair(b, m):
                    k = PAIRS * b + m
                    dve.wait_ge(attended, UNITS * b + 2 * NT * (m + 1))
                    nc.vector.reciprocal(row_inv[:, 2 * m:2 * m + 2, :], row_sum[:, 2 * m:2 * m + 2, :]
                                         ).then_inc(norm_chain, 1)
                    dve.wait_ge(norm_chain, k + 1)
                    after(dve, OT_ps, k - 1)
                    for t in range(NT):
                        ins = nc.vector.tensor_tensor(
                            O_sb[:, m % 2, t, :].rearrange("p (h c) -> p h c", h=2),
                            O_view[:, t, :].rearrange("p (h c) -> p h c", h=2),
                            row_inv[:, 2 * m:2 * m + 2, t:t + 1].to_broadcast([P, 2, DK]), ALU.mult)
                    ins.then_inc(normed, 1)

                def copy_OT(b, m):
                    k = PAIRS * b + m
                    dve.wait_ge(OT_ps, k + 1)
                    if m == 0:
                        after(dve, wo_ps, 2 * b)
                    nc.vector.tensor_copy(OT[:, m, :], TA[:, 0:S]).then_inc(OT_sb, 1)

                def pair_steps(b, n):
                    if n % (2 * NT) == 0 and n:
                        norm_pair(b, n // (2 * NT) - 1)
                    if n % (2 * NT) == 2 and n > 2:
                        copy_OT(b, n // (2 * NT) - 1)

                def unit(b, par, n, first, last):
                    g = UNITS * b + n
                    w = P * (n % NT + 1)
                    if first and n == 0:
                        max_unit(b, par, 0)
                        max_unit(b, par, 1)
                    if n % 2 == 0:
                        dve.wait_ge(probT_ps, g + 1)
                        after(dve, attended, g - NR + 1)
                        nc.vector.tensor_copy(probT[:, n % NR, 0:w], T_ps[0][:, 0:w]).then_inc(probT_sb[0], 1)
                    if n + 2 < UNITS:
                        max_unit(b, par, n + 2)
                    elif not last:
                        max_unit(b + 1, 1 - par, n + 2 - UNITS)
                    if n <= 2 and not first:
                        pair_steps(b - 1, UNITS + n)
                    pair_steps(b, n)

                def tail(b, par, n):
                    if n == 0:
                        chains["tail"] = Chain(dve, tail_chain, TAIL_STEPS * b)
                    chain = chains["tail"]
                    for use, (lo, hi) in enumerate(((0, 2), (2, NT))):
                        if n == T_WO + use:
                            dve.wait_ge(wo_ps, 2 * b + use + 1)
                            h = tokens[:, bass.ds(NT * b + lo, hi - lo), :]
                            nc.vector.tensor_tensor(h, TA[:, 0:(hi - lo) * D].rearrange("p (t d) -> p t d", d=D), h,
                                                    ALU.add).then_inc(wo_added, 1)
                    if n == T_WO + 1:
                        dve.wait_ge(wo_added, 2 * b + 2)
                        dve.wait_ge(xn2_free, b + 1)
                        chain.step(layer_norm(chain, tokens[:, bass.ds(NT * b, NT), :], xn, st2, mv2, ln_h2, ln_y2, ln_yy2,
                                              NT))
                        split_tokens(chain, xn, xs2[par]).then_inc(xn2_ready, 1)
                        dve.wait_ge(xn2_ready, b + 1)
                    if n == T_X2T:
                        dve.wait_ge(x2T_ps, 2 * b + 1)
                        nc.vector.tensor_copy(x2T[:, 0:2, :], TA[:, 0:S].bitcast(FP16).rearrange("p (k s) -> p k s", k=2)
                                              ).then_inc(x2T_sb, 1)
                    if n == T_X2T + 1:
                        dve.wait_ge(x2T_ps, 2 * b + 2)
                        nc.vector.tensor_copy(x2T[:, 2, :], TA[:, 0:S // 2].bitcast(FP16)).then_inc(x2T_sb, 1)
                    if n == T_LOGIT:
                        whole = [P, NT, E]
                        sel1, chosen = rec[:, :, 0:E], rec[:, :, E:2 * E]
                        dve.wait_ge(logits_ps, b + 1)
                        nc.vector.tensor_scalar(lg[:, :, :], TA[:, 0:NT * E].rearrange("p (t e) -> p t e", t=NT),
                                                V_OUT, None, ALU.mult).then_inc(logits_sb, 1)
                        dve.wait_ge(logits_sb, b + 1)

                        def pick(src, best, sel):
                            chain.step(nc.vector.tensor_reduce(best[:, :], src, AX, ALU.max))
                            chain.step(nc.vector.tensor_tensor(key[:, :, :], src, over_rows(best[:, :], whole), ALU.is_equal))
                            chain.step(nc.vector.tensor_tensor(key[:, :, :], key[:, :, :], over_tiles(first_wins[:, :], whole),
                                                               ALU.mult))
                            chain.step(nc.vector.tensor_reduce(key_max[:, :], key[:, :, :], AX, ALU.max))
                            chain.step(nc.vector.tensor_tensor(sel, key[:, :, :], over_rows(key_max[:, :], whole), ALU.is_equal))

                        pick(lg[:, :, :], top1, sel1)
                        chain.step(nc.vector.scalar_tensor_tensor(lg2[:, :, :], sel1, MASKED, lg[:, :, :], ALU.mult, ALU.add))
                        pick(lg2[:, :, :], top2, sel2[:, :, :])
                        nc.vector.tensor_tensor(gap[:, :], top2[:, :], top1[:, :], ALU.subtract).then_inc(gap_ready, 1)
                        nc.vector.tensor_tensor(chosen_bf[:, :, :], sel1, sel2[:, :, :], ALU.add).then_inc(chosen_ready, 1)
                        nc.vector.tensor_tensor(chosen, sel1, sel2[:, :, :], ALU.add)
                    if n == T_LOGIT + 2:
                        dve.wait_ge(gap_exped, b + 1)
                        chain.step(nc.vector.tensor_scalar(gap_sum[:, :], gap_exp[:, :], 1.0, None, ALU.add))
                        chain.step(nc.vector.reciprocal(rec[:, :, 2 * E], gap_sum[:, :]))
                        nc.vector.tensor_tensor(rec[:, :, 2 * E + 1], rec[:, :, 2 * E], gap_exp[:, :], ALU.mult)
                    if n == T_RANK:
                        whole = [P, NT, E]
                        old, new = running[:, par, :], running[:, 1 - par, :]
                        dve.wait_ge(ranks_ps, b + 1)
                        nc.vector.tensor_tensor(new, TA[:, NT * E:(NT + 1) * E], old, ALU.add)
                        nc.vector.tensor_tensor(pos[:, :, :], TA[:, 0:NT * E].rearrange("p (t e) -> p t e", t=NT),
                                                over_tiles(old, whole), ALU.add).then_inc(ranks_sb, 1)
                        dve.wait_ge(ranks_sb, b + 1)
                        chain.step(nc.vector.tensor_scalar(late[:, :, :], pos[:, :, :], float(CAP), OUT_OF_BOUNDS,
                                                           ALU.is_ge, ALU.mult))
                        chain.step(nc.vector.tensor_tensor(pos[:, :, :], pos[:, :, :], late[:, :, :], ALU.add))
                        chain.step(nc.vector.tensor_tensor(pos[:, :, :], pos[:, :, :],
                                                           over_tiles(expert_base[:, :], whole), ALU.add))
                        for k, sel in enumerate((rec[:, :, 0:E], sel2[:, :, :])):
                            chain.step(nc.vector.tensor_tensor(picked[:, :, :], pos[:, :, :], sel, ALU.mult))
                            chain.step(nc.vector.tensor_reduce(rec[:, :, 2 * E + 2 + k:2 * E + 3 + k], picked[:, :, :],
                                                               AX, ALU.add))
                        nc.vector.tensor_copy(slot_idx[par][:, :, :], rec[:, :, 2 * E + 2:REC]).then_inc(slots_ready, 1)
                        chain.step(nc.vector.tensor_copy(record[:, bass.ds(NT * b, NT), :], rec[:, :, :]))
                    if n == UNITS - 1:
                        assert chain.n == TAIL_STEPS, chain.n

                run(dve, unit, front, tail)
                norm_pair(B - 1, PAIRS - 1)
                copy_OT(B - 1, PAIRS - 1)
                for n in range(UNITS):
                    tail(B - 1, 1, n)
                nc.vector.tensor_reduce(most[:, :], running[:, B % 2, :], AX, ALU.max).then_inc(totals_ready, 1)
                dve.wait_ge(totals_ready, 1)

            @block.tensor
            def _(pe):
                pe.wait_ge(weights_in, 16)
                pe.wait_ge(split, 5)
                pe.wait_ge(consts, 5)
                pe.wait_ge(zero_ready, 2)

                def transposes(dst, src, lo, hi):
                    for t in range(NT):
                        ins = nc.tensor.transpose(dst[0:hi - lo, t * P:t * P + P], src[:, t, lo:hi], ident[:, :])
                    return ins

                def transposes16(dst, src, k):
                    for t in range(NT):
                        ins = nc.tensor.transpose(dst[:, t * P:t * P + P], src[:, t, k * P:k * P + P], ident16[:, :])
                    return ins

                def front(b, par, n):
                    if n == F_XT:
                        if isinstance(b, int):
                            pe.wait_ge(x_in[par], 32 * (b // 2 + 1))
                        else:
                            pe.wait_ge(x_in[par], 16 * (b - par) + 32)
                        after(pe, v_sb[0], NT * b)
                        after(pe, v_sb[1], NT * b)
                        transposes(FA, xin[par], 0, P)
                        transposes(FB, xin[par], P, D).then_inc(xsT_ps, 1)
                    if n == F_SCORE:
                        pe.wait_ge(xsT_first_sb, b + 1)
                        pe.wait_ge(xsT_last_sb, b + 1)
                        for t in range(NT):
                            c = slice(t * P, t * P + P)
                            nc.tensor.matmul(FA[:, c], xsT_first[:, c], xsT_first[:, c], start=True, stop=False)
                            ins = nc.tensor.matmul(FA[:, c], xsT_last[:, c], xsT_last[:, c], start=False, stop=True)
                        ins.then_inc(tok_scores, 1)
                    if n == F_PT:
                        pe.wait_ge(tok_exp, NT * (b + 1))
                        transposes(FB, tok_p, 0, P).then_inc(tok_pT_ps, 1)
                    if n == F_MIX:
                        pe.wait_ge(tok_pT_sb, b + 1)
                        for t in range(NT):
                            dst = FA[:, t * D:t * D + D] if t < 2 else FB[:, 0:D]
                            ins = nc.tensor.matmul(dst, tok_pT[:, t, :], xin[par][:, t, :], start=True, stop=True)
                        ins.then_inc(tok_mixed, 1)
                    if n == F_XNT:
                        pe.wait_ge(xn_ready, b + 1)
                        for k in range(2):
                            transposes16(FA[:, k * S // 2:(k + 1) * S // 2].bitcast(FP16), xs, k)
                        transposes16(FB[:, 0:S // 2].bitcast(FP16), xs, 2).then_inc(xnT_ps, 1)
                    q = n - F_PROJ
                    if q >= 0:
                        dst = (FA, FB)[q % 2]
                        if q < 2:
                            pe.wait_ge(xT_sb[0], b + 1)
                            pe.wait_ge(xT_sb[1], b + 1)
                        elif q < 2 * PAIRS + 2:
                            pe.wait_ge(qk_sb, 2 * PAIRS * b + q - 1)
                        else:
                            pe.wait_ge(v_sb[q % 2], NT * b + (q - 2 * PAIRS) // 2)
                        if q < 2 * PAIRS:
                            m = q % PAIRS
                            ins = product((w_q, w_k)[q // PAIRS], slice(m * P, m * P + P), xT, slice(0, S), dst[:, 0:S],
                                          False)
                        else:
                            t, half = divmod(q - 2 * PAIRS, 2)
                            ins = product(w_v, slice(half * VH, half * VH + VH), xT, slice(t * P, t * P + P), dst[:, 0:VH],
                                          True)
                        ins.then_inc(proj_ps, 1)

                def score_unit(b, par, n):
                    h, t = divmod(n, NT)
                    m, rows = h // 2, slice(DK * (h % 2), DK * (h % 2) + DK)
                    g = UNITS * b + n
                    if n % PAIR == 0:
                        pe.wait_ge(qk_sb, 2 * PAIRS * b + PAIRS + m + 1)
                    after(pe, exp_done, g - 1)
                    dst = S_ps[n % 2]
                    for i, (q, k) in enumerate(((0, 0), (0, 1), (1, 0))):
                        nc.tensor.matmul(dst[:, 0:P * (t + 1)], QT[par][q][rows, m, t * P:t * P + P],
                                         KT[par][k][rows, m, 0:P * (t + 1)], start=(i == 0), stop=False)
                    nc.tensor.matmul(dst[:, t * P:t * P + P], ident_bf[:, :], causal[:, :], start=False,
                                     stop=True).then_inc(scores, 1)

                def attend_unit(b, par, n):
                    h, t = divmod(n, NT)
                    g = UNITS * b + n
                    if n == 0:
                        for k in range(2):
                            pe.wait_ge(v_sb[k], NT * (b + 1))
                    if n % PAIR == 0:
                        after(pe, normed, PAIRS * b + n // PAIR)
                    pe.wait_ge(probT_sb[n % 2], UNITS // 2 * b + n // 2 + 1)
                    for j in range(t + 1):
                        ins = nc.tensor.matmul(O_view[:, t, DK * (h % 2):DK * (h % 2) + DK],
                                               probT[:, n % NR, j * P:j * P + P], V[par][:, j, h * DK:h * DK + DK],
                                               start=(j == 0), stop=(j == t))
                    ins.then_inc(attended, 1)

                def transpose_O(b, m):
                    k = PAIRS * b + m
                    pe.wait_ge(normed, k + 1)
                    after(pe, OT_sb, k)
                    if m == 0:
                        after(pe, wo_added, 2 * b)
                    if m == 1:
                        after(pe, logits_sb, b)
                    if m == 2:
                        after(pe, ranks_sb, b)
                    for t in range(NT):
                        ins = nc.tensor.transpose(TA[:, t * P:t * P + P], O_sb[:, m % 2, t, :], ident[:, :])
                    ins.then_inc(OT_ps, 1)

                def unit(b, par, n, first, last):
                    g = UNITS * b + n
                    t = n % NT
                    if first and n == 0:
                        score_unit(b, par, 0)
                        score_unit(b, par, 1)
                    pe.wait_ge(exp_done, g + 1)
                    if n >= 2 or not first:
                        pe.wait_ge(probT_sb[n % 2], UNITS // 2 * b + n // 2)
                    for j in range(t + 1):
                        ins = nc.tensor.transpose(T_ps[n % 2][:, j * P:j * P + P], prob[:, n % NR, j * P:j * P + P],
                                                  ident[:, :])
                    ins.then_inc(probT_ps, 1)
                    if n + 2 < UNITS:
                        score_unit(b, par, n + 2)
                    elif not last:
                        score_unit(b + 1, 1 - par, n + 2 - UNITS)
                    if n:
                        attend_unit(b, par, n - 1)
                    elif not first:
                        attend_unit(b - 1, 1 - par, UNITS - 1)
                    if n % PAIR == 1:
                        if n > 1:
                            transpose_O(b, n // PAIR - 1)
                        elif not first:
                            transpose_O(b - 1, PAIRS - 1)

                def tail(b, par, n, final=False):
                    for use, tiles in enumerate((range(0, 2), range(2, NT))):
                        if n == T_WO + use:
                            pe.wait_ge(OT_sb, PAIRS * (b + 1))
                            if use:
                                pe.wait_ge(wo_added, 2 * b + use)
                            for i, t in enumerate(tiles):
                                for m in range(PAIRS):
                                    ins = nc.tensor.matmul(TA[:, i * D:i * D + D], OT[:, m, t * P:t * P + P],
                                                           wo_sb[:, m, :], start=(m == 0), stop=(m == PAIRS - 1))
                            ins.then_inc(wo_ps, 1)
                    if n == T_X2T:
                        pe.wait_ge(xn2_ready, b + 1)
                        if not final:
                            pe.wait_ge(OT_sb, PAIRS * (b + 1) + 1)
                        for k in range(2):
                            ins = transposes16(TA[:, k * S // 2:(k + 1) * S // 2].bitcast(FP16), xs2[par], k)
                        ins.then_inc(x2T_ps, 1)
                    if n == T_X2T + 1:
                        pe.wait_ge(x2T_sb, 2 * b + 1)
                        transposes16(TA[:, 0:S // 2].bitcast(FP16), xs2[par], 2).then_inc(x2T_ps, 1)
                    if n == T_LOGIT:
                        pe.wait_ge(x2T_sb, 2 * b + 2)
                        for t in range(NT):
                            c = slice(t * P, t * P + P)
                            ins = product(w_g, slice(0, E), x2T, c, TA[:, t * E:t * E + E], True)
                        ins.then_inc(logits_ps, 1)
                    if n == T_RANK:
                        pe.wait_ge(chosen_ready, b + 1)
                        if not final:
                            pe.wait_ge(OT_sb, PAIRS * (b + 1) + 2)
                        for t in range(NT + 1):
                            dst = TA[:, t * E:t * E + E]
                            for k in range(t):
                                ins = nc.tensor.matmul(dst, ones_bf[:, :], chosen_bf[:, k, :], start=(k == 0),
                                                       stop=(t == NT and k == t - 1))
                            if t < NT:
                                ins = nc.tensor.matmul(dst, before[:, :], chosen_bf[:, t, :], start=(t == 0), stop=True)
                        ins.then_inc(ranks_ps, 1)

                run(pe, unit, front, tail)
                attend_unit(B - 1, 1, UNITS - 1)
                transpose_O(B - 1, PAIRS - 1)
                for n in range(UNITS):
                    tail(B - 1, 1, n, final=True)

        part = ExitStack()
        with part:
            def sa(name, shape, dt=FP32):
                return sb(name, shape, dt, part)

            def ps(name, shape, dt=FP32):
                return part.enter_context(nc.psum_tensor(name, shape, dt))

            HALF = TILES // 2
            assert HALF * E <= 512 and TILES <= 256
            priority = sa("priority", [P, TILES])
            threshold, candidate = sa("threshold", [P, E]), sa("candidate", [P, E])
            step_size = sa("step_size", [P, 1])
            hits = sa("hits", [P, TILES, E])
            hits_f = sa("hits_f", [P, E])
            hits_bf = sa("hits_bf", [P, E], BF16)
            raised = sa("raised", [P, E])
            above, ties = sa("above", [P, TILES, E]), sa("ties", [P, TILES, E])
            marked = sa("marked", [P, TILES, E], BF16)
            column, rank = sa("column", [P, TILES, E]), sa("rank", [P, TILES, E])
            ones_row = sa("ones_row", [P, TILES])
            places = sa("places", [P, TILES])
            second = sa("second", [P, TILES, E])
            scatter_to = sa("scatter_to", [P, TILES, 2])
            r_st, r_mv = sa("r_st", [P, 1, 6]), sa("r_mv", [P, 1, 2])
            r_h, r_y, r_yy = sa("r_h", [P, 1]), sa("r_y", [P, 1]), sa("r_yy", [P, 1])
            r_tok, r_x, r_rows = sa("r_tok", [P, 1, D]), sa("r_x", [P, 1, D]), sa("r_rows", [P, 1, 2 * D], FP16)
            r_idx = sa("r_idx", [P, 1, 2], U32)
            total_ps = ps("total_ps", [P, 512])
            before_ps = [ps(f"before_ps{i}", [P, 512]) for i in range(2)]
            column_ps = [ps(f"column_ps{i}", [P, 512]) for i in range(2)]
            r_chain, l_chain = sem("r_chain"), sem("l_chain")
            counted, totals, marks, ranked = sem("counted"), sem("totals"), sem("marks"), sem("ranked")
            r_ready, r_free, rescattered = sem("r_ready"), sem("r_free"), sem("rescattered")
            LOOP_CHAIN = 8
            TILE_CHAIN = 3 + 6 + 3 * NEWTON_STEPS

            block = part.enter_context(nc.Block())

            @block.vector
            def _(dve):
                with dve.If(dve.value_load(most[0:1, 0:1], min_val=0, max_val=T) > CAP):
                    whole = [P, TILES, E]
                    sel1, chosen = record[:, :, 0:E], record[:, :, E:2 * E]
                    chain = Chain(dve, r_chain, 0)
                    nc.vector.memset(threshold[:, :], 0.0)
                    nc.vector.memset(ones_row[:, :], 1.0)
                    chain.step(nc.vector.memset(step_size[:, :], float(1 << 24)))
                    chain.step(nc.vector.tensor_scalar(priority[:, :], record[:, :, 2 * E], float(1 << 24), None, ALU.mult))
                    with dve.Fori(0, SEARCH_STEPS) as k:
                        loop = Chain(dve, l_chain, LOOP_CHAIN * k)
                        loop.step(nc.vector.tensor_scalar(candidate[:, :], threshold[:, :], step_size[:, 0:1], None, ALU.add))
                        loop.step(nc.vector.tensor_tensor(hits[:, :, :], over_rows(priority[:, :], whole),
                                                          over_tiles(candidate[:, :], whole), ALU.is_ge))
                        loop.step(nc.vector.tensor_tensor(hits[:, :, :], hits[:, :, :], chosen, ALU.mult))
                        loop.step(nc.vector.tensor_reduce(hits_f[:, :], hits[:, :, :].rearrange("p t e -> p e t"), AX,
                                                          ALU.add))
                        nc.vector.tensor_copy(hits_bf[:, :], hits_f[:, :]).then_inc(counted, 1)
                        dve.wait_ge(totals, k + 1)
                        loop.step(nc.vector.tensor_scalar(raised[:, :], total_ps[:, 0:E], float(CAP), None, ALU.is_ge))
                        loop.step(nc.vector.tensor_scalar(raised[:, :], raised[:, :], step_size[:, 0:1], None, ALU.mult))
                        loop.step(nc.vector.tensor_tensor(threshold[:, :], threshold[:, :], raised[:, :], ALU.add))
                        loop.step(nc.vector.tensor_scalar(step_size[:, :], step_size[:, :], 0.5, None, ALU.mult))
                        assert loop.n == LOOP_CHAIN
                    for dst, op in ((above, ALU.is_gt), (ties, ALU.is_equal)):
                        chain.step(nc.vector.tensor_tensor(dst[:, :, :], over_rows(priority[:, :], whole),
                                                           over_tiles(threshold[:, :], whole), op))
                        chain.step(nc.vector.tensor_tensor(dst[:, :, :], dst[:, :, :], chosen, ALU.mult))
                    chain.step(nc.vector.tensor_reduce(hits_f[:, :], above[:, :, :].rearrange("p t e -> p e t"), AX, ALU.add))
                    nc.vector.tensor_copy(hits_bf[:, :], hits_f[:, :]).then_inc(counted, 1)
                    dve.wait_ge(totals, SEARCH_STEPS + 1)
                    chain.step(nc.vector.tensor_scalar(candidate[:, :], total_ps[:, 0:E], -1.0, float(CAP), ALU.mult, ALU.add))

                    def rank_of(marks_f, n):
                        nc.vector.tensor_copy(marked[:, :, :], marks_f).then_inc(marks, 1)
                        dve.wait_ge(ranked, n)
                        for i in range(2):
                            c = slice(i * HALF, (i + 1) * HALF)
                            nc.vector.tensor_copy(column[:, c, :], column_ps[i][:, 0:HALF * E]
                                                  .rearrange("p (t e) -> p t e", e=E))
                            ins = nc.vector.tensor_copy(rank[:, c, :], before_ps[i][:, 0:HALF * E]
                                                        .rearrange("p (t e) -> p t e", e=E))
                        chain.step(ins)
                        chain.step(nc.vector.tensor_tensor(rank[:, :, :], rank[:, :, :], column[:, :, :], ALU.subtract))
                        for e in range(E):
                            ins = nc.vector.tensor_tensor_scan(hits[:, :, e], ones_row[:, :], column[:, :, e], 0.0,
                                                               ALU.mult, ALU.add)
                        chain.step(ins)
                        chain.step(nc.vector.tensor_tensor(rank[:, :, :], rank[:, :, :], hits[:, :, :], ALU.add))

                    rank_of(ties[:, :, :], 1)
                    chain.step(nc.vector.tensor_tensor(rank[:, :, :], rank[:, :, :], over_tiles(candidate[:, :], whole),
                                                       ALU.is_lt))
                    chain.step(nc.vector.tensor_tensor(ties[:, :, :], ties[:, :, :], rank[:, :, :], ALU.mult))
                    chain.step(nc.vector.tensor_tensor(above[:, :, :], above[:, :, :], ties[:, :, :], ALU.add))
                    rank_of(above[:, :, :], 2)
                    chain.step(nc.vector.tensor_tensor(rank[:, :, :], rank[:, :, :], over_tiles(expert_base[:, :], whole),
                                                       ALU.add))
                    chain.step(nc.vector.tensor_tensor(second[:, :, :], chosen, sel1, ALU.subtract))
                    for k, sel in enumerate((sel1, second[:, :, :])):
                        slot, weight = record[:, :, 2 * E + 2 + k], record[:, :, 2 * E + k]
                        chain.step(nc.vector.tensor_tensor(hits[:, :, :], sel, above[:, :, :], ALU.mult))
                        chain.step(nc.vector.tensor_reduce(places[:, :], hits[:, :, :], AX, ALU.add))
                        chain.step(nc.vector.tensor_tensor(weight, weight, places[:, :], ALU.mult))
                        chain.step(nc.vector.tensor_tensor(hits[:, :, :], hits[:, :, :], rank[:, :, :], ALU.mult))
                        chain.step(nc.vector.tensor_reduce(slot, hits[:, :, :], AX, ALU.add))
                        chain.step(nc.vector.tensor_scalar(places[:, :], places[:, :], -OUT_OF_BOUNDS, OUT_OF_BOUNDS,
                                                           ALU.mult, ALU.add))
                        chain.step(nc.vector.tensor_tensor(scatter_to[:, :, k], slot, places[:, :], ALU.add))
                    with dve.Fori(0, TILES) as c:
                        tile_chain = Chain(dve, l_chain, LOOP_CHAIN * SEARCH_STEPS + TILE_CHAIN * c)
                        dve.wait_ge(r_free, c + 1)
                        tile_chain.step(nc.vector.tensor_copy(r_tok[:, :, :], tokens[:, bass.ds(c, 1), :]))
                        nc.vector.tensor_copy(r_idx[:, :, :], scatter_to[:, bass.ds(c, 1), :])
                        tile_chain.step(layer_norm(tile_chain, r_tok, r_x, r_st, r_mv, r_h, r_y, r_yy, 1))
                        split_tokens(tile_chain, r_x, r_rows).then_inc(r_ready, 1)
                        assert tile_chain.n == TILE_CHAIN

            @block.tensor
            def _(pe):
                with pe.If(pe.value_load(most[0:1, 0:1], min_val=0, max_val=T) > CAP):
                    with pe.Fori(0, SEARCH_STEPS + 1) as k:
                        pe.wait_ge(counted, k + 1)
                        nc.tensor.matmul(total_ps[:, 0:E], ones_bf[:, :], hits_bf[:, :], start=True, stop=True
                                         ).then_inc(totals, 1)
                    with pe.Fori(0, 2) as n:
                        pe.wait_ge(marks, n + 1)
                        for i in range(2):
                            src = marked[:, i * HALF:(i + 1) * HALF, :].rearrange("p t e -> p (t e)")
                            nc.tensor.matmul(before_ps[i][:, 0:HALF * E], before[:, :], src, start=True, stop=True)
                            ins = nc.tensor.matmul(column_ps[i][:, 0:HALF * E], ones_bf[:, :], src, start=True, stop=True)
                        ins.then_inc(ranked, 1)

            @block.gpsimd
            def _(pool):
                with pool.If(pool.value_load(most[0:1, 0:1], min_val=0, max_val=T) > CAP):
                    pool.sem_inc(r_free, 1)
                    with pool.Fori(0, TILES) as c:
                        pool.wait_ge(r_ready, c + 1)
                        alone(pool, spare)
                        for k in range(2):
                            pool.indirect_dma_start(slots_dram[:, :], bass.IndirectOffsetOnAxis(r_idx[:, 0, k:k + 1], 0),
                                                    r_rows[:, 0, :], None, bounds_check=E * CAPP - 1, oob_is_err=False
                                                    ).then_inc(rescattered, 16)
                        pool.wait_ge(rescattered, 32 * c + 32)
                        pool.sem_inc(r_free, 1)

        part = ExitStack()
        with part:
            def sa(name, shape, dt=FP32):
                return sb(name, shape, dt, part)

            def ps(name, shape, dt=FP32):
                return part.enter_context(nc.psum_tensor(name, shape, dt))

            raw1, raw2 = sa("raw1", [P, 2, HID]), sa("raw2", [P, HT, D])
            w1_sb = [(sa(f"w1_hi{i}", [P, HID], FP16), sa(f"w1_lo{i}", [P, HID], FP16),
                      sa(f"w1_twice{i}", [P, HID], FP16), sa(f"w1_last{i}", [D1, HID], FP16)) for i in range(2)]
            w2_sb = [[sa(f"w2_{k}{i}", [P, HT, D], FP16) for k in ("hi", "lo")] for i in range(2)]
            b1_all, b2_all = sa("b1_all", [P, E, HT]), sa("b2_all", [P, E, D])
            b1_sb = [sa(f"b1_sb{i}", [P, HT]) for i in range(2)]
            b2_sb = [sa(f"b2_sb{i}", [P, D]) for i in range(2)]
            rows = [sa(f"rows{i}", [P, NT, 2 * D], FP16) for i in range(2)]
            rT = [sa(f"rT{i}", [P, 3, GROUP], FP16) for i in range(2)]
            hidden = sa("hidden", [P, HT, GROUP])
            hT = [sa(f"hT_{k}", [P, HT, GROUP], FP16) for k in ("hi", "lo")]
            ex_out = [sa(f"ex_out{i}", [P, NT, D]) for i in range(2)]
            RG = 4
            assert TILES % RG == 0
            pick_w = sa("pick_w", [P, RG, 2])
            picks = [[sa(f"pick{k}_{i}", [P, D]) for i in range(RG)] for k in range(2)]
            pick_idx = sa("pick_idx", [P, RG, 2], U32)
            half = sa("half", [P, RG, D])
            result = [sa(f"result{i}", [P, D]) for i in range(RG)]

            HB = 3
            h_ps = [ps(f"h_ps{i}", [P, 512]) for i in range(HB)]
            rT_ps = [ps(f"rT_ps{i}", [P, 512]) for i in range(2)]
            ex_ps = [ps(f"ex_ps{i}", [P, 512]) for i in range(2)]

            raw_in2, b_in, w_ready, w_chain = sem("raw_in2"), sem("b_in"), sem("w_ready"), sem("w_chain")
            hidden_hi, hidden_split = sem("hidden_hi"), sem("hidden_split")
            rows_in = [sem("rows_in0"), sem("rows_in1")]
            rT_ready, rT_sb = sem("rT_ready"), [sem("rT_sb_dve"), sem("rT_sb_act")]
            hidden_ps, hidden_sb = sem("hidden_ps"), sem("hidden_sb")
            ex_ready, ex_added = sem("ex_ready"), sem("ex_added")
            stored = [sem("stored0"), sem("stored1")]
            idx_ready = sem("idx_ready")
            pick_in = [sem(f"pick_in{i}") for i in range(RG)]
            half_sum, result_ready = sem("half_sum"), sem("result_ready")
            out_stored = [sem(f"out_stored{i}") for i in range(RG)]

            def each_step(eng, step, at_expert=None):
                def expert(e, ep, last):
                    if at_expert:
                        at_expert(e, ep, last)
                    with eng.Fori(0, GPE // 2) as j:
                        for par in range(2):
                            step(GPE * e + 2 * j + par, par, ep)

                with eng.Fori(0, E // 2 - 1) as pair:
                    for ep in range(2):
                        expert(2 * pair + ep, ep, False)
                expert(E - 2, 0, False)
                expert(E - 1, 1, True)

            block = part.enter_context(nc.Block())

            def slot_rows(table, g):
                return table[bass.ds(g * GROUP, GROUP), :].rearrange("(p r) d -> p r d", p=P)

            @block.sync
            def _(sp):
                for s in stored + out_stored:
                    sp.sem_inc(s, 1)
                sp.dma_start(rows[0][:, :, :], slot_rows(slots_dram, 0)).then_inc(rows_in[0], 16)

                def step(g, par, ep):
                    sp.wait_ge(rT_ready, g + 1)
                    sp.dma_start(rows[1 - par][:, :, :], slot_rows(slots_dram, g + 1)).then_inc(rows_in[1 - par], 16)
                    sp.wait_ge(ex_added, g + 2)
                    sp.dma_start(slot_rows(expert_dram, g), ex_out[par][:, :, :]).then_inc(stored[par], 16)

                each_step(sp, step)
                sp.wait_ge(rows_in[0], 16 * (E * GPE // 2 + 1))
                out_rows = out.rearrange("b s d -> (b s) d")
                with sp.Fori(0, TILES // RG) as k:
                    for i in range(RG):
                        sp.wait_ge(result_ready, RG * k + i + 1)
                        sp.dma_start(out_rows[bass.ds((RG * k + i) * P, P), :], result[i][:, :]
                                     ).then_inc(out_stored[i], 16)
                for i in range(RG):
                    sp.wait_ge(out_stored[i], 16 * (TILES // RG) + 1)

            @block.gpsimd
            def _(pool):
                def weights(e):
                    first = w1[bass.ds(e, 1), 0:P, :].rearrange("o m k -> (o m) k")
                    last = w1[bass.ds(e, 1), P:D, :].rearrange("o m k -> (o m) k")
                    for dst, src in (
                        (raw1[:, 0, :], first), (raw1[0:D1, 1, :], last), (raw1[D1:P, 1, :], last),
                        (raw2[:, :, :], w2[bass.ds(e, 1), :, :].rearrange("o (c p) d -> (o p) c d", p=P)),
                    ):
                        pool.dma_start(dst, src, allow_slow_non_contiguous=True).then_inc(raw_in2, 16)

                weights(0)
                pool.dma_start(b1_all[:, :, :], b1.rearrange("e (c p) -> p e c", p=P), allow_slow_non_contiguous=True
                               ).then_inc(b_in, 16)
                pool.dma_start(b2_all[:, :, :].rearrange("p e d -> p (e d)"),
                               b2.rearrange("e d -> (e d)").rearrange("(o n) -> o n", o=1).to_broadcast([P, E * D]),
                               allow_slow_non_contiguous=True).then_inc(b_in, 16)
                with pool.Fori(1, E) as e:
                    pool.wait_ge(w_ready, e)
                    alone(pool, spare)
                    weights(e)
                for par in range(2):
                    pool.wait_ge(stored[par], 16 * (E * GPE // 2) + 1)
                with pool.Fori(0, TILES // RG) as k:
                    for i in range(RG):
                        pool.wait_ge(idx_ready, RG * k + i + 1)
                        alone(pool, spare)
                        for c in range(2):
                            pool.indirect_dma_start(picks[c][i][:, :], None, expert_dram[:, :],
                                                    bass.IndirectOffsetOnAxis(pick_idx[:, i, c:c + 1], 0),
                                                    bounds_check=E * CAPP - 1, oob_is_err=False
                                                    ).then_inc(pick_in[i], 16)

            @block.scalar
            def _(act):
                def move_last(par):
                    nc.scalar.activation(rT[par][:, 2, :], rT_ps[1][:, 0:GROUP // 2].bitcast(FP16), ACT.Copy
                                         ).then_inc(rT_sb[1], 1)

                act.wait_ge(rT_ready, 1)
                move_last(0)

                def at_expert(e, ep, last):
                    act.wait_ge(w_ready, e + 1)
                    alone(act, spare)

                def step(g, par, ep):
                    for m in range(HT):
                        act.wait_ge(hidden_ps, HT * g + m + 1)
                        nc.scalar.activation(hidden[:, m, :], h_ps[m % HB][:, 0:GROUP], ACT.Gelu,
                                             bias=b1_sb[ep][:, m:m + 1], scale=H_OUT).then_inc(hidden_sb, 1)
                    act.wait_ge(rT_ready, g + 2)
                    move_last(1 - par)

                each_step(act, step, at_expert)

            @block.vector
            def _(dve):
                dve.sem_inc(hidden_sb, HB)
                dve.sem_inc(ex_added, 1)

                def split_expert(e, ep):
                    dve.wait_ge(raw_in2, 64 * e + 64)
                    split = Chain(dve, w_chain, 2 * e)
                    last = split_weights(split, raw1[:, 0, :], raw1[:, 1, :], *(m[:, :] for m in w1_sb[ep]))
                    nc.vector.tensor_copy(b1_sb[ep][:, :], b1_all[:, bass.ds(e, 1), :].rearrange("p o c -> p (o c)"))
                    nc.vector.tensor_copy(b2_sb[ep][:, :], b2_all[:, bass.ds(e, 1), :].rearrange("p o c -> p (o c)"))
                    hi, lo = w2_sb[ep]
                    split.step(nc.vector.tensor_scalar(hi[:, :, :], raw2[:, :, :], W_SCALE, None, ALU.mult))
                    nc.vector.scalar_tensor_tensor(lo[:, :, :], raw2[:, :, :], W_SCALE, hi[:, :, :], ALU.mult,
                                                   ALU.subtract).then_inc(w_ready, 1)

                def move_first(par):
                    nc.vector.tensor_copy(rT[par][:, 0:2, :], rT_ps[0][:, 0:GROUP].bitcast(FP16)
                                          .rearrange("p (k n) -> p k n", k=2)).then_inc(rT_sb[0], 1)

                dve.wait_ge(b_in, 32)
                split_expert(0, 0)
                dve.wait_ge(rT_ready, 1)
                move_first(0)

                def at_expert(e, ep, last):
                    if not last:
                        dve.wait_ge(ex_added, GPE * e + 1)
                        alone(dve, spare)
                        split_expert(e + 1, 1 - ep)
                    else:
                        dve.wait_ge(w_ready, e + 1)
                        alone(dve, spare)

                def step(g, par, ep):
                    for m in range(HT):
                        dve.wait_ge(hidden_sb, HB + HT * g + m + 1)
                        nc.vector.tensor_scalar(hT[0][:, m, :], hidden[:, m, :], H_SCALE, None, ALU.mult
                                                ).then_inc(hidden_hi, 1)
                        dve.wait_ge(hidden_hi, HT * g + m + 1)
                        nc.vector.scalar_tensor_tensor(hT[1][:, m, :], hidden[:, m, :], H_SCALE, hT[0][:, m, :],
                                                       ALU.mult, ALU.subtract).then_inc(hidden_split, 1)
                    dve.wait_ge(rT_ready, g + 2)
                    move_first(1 - par)
                    dve.wait_ge(ex_ready, g + 1)
                    dve.wait_ge(stored[par], 8 * (g - par) + 1)
                    for lo, hi in ((0, 2), (2, NT)):
                        ins = nc.vector.scalar_tensor_tensor(
                            ex_out[par][:, lo:hi, :], ex_ps[lo // 2][:, 0:(hi - lo) * D].rearrange("p (t d) -> p t d", d=D),
                            EX_OUT, over_tiles(b2_sb[ep][:, :], [P, hi - lo, D]), ALU.mult, ALU.add)
                    ins.then_inc(ex_added, 1)

                each_step(dve, step, at_expert)

                def fetch(c, i):
                    nc.vector.tensor_copy(pick_w[:, i:i + 1, :], record[:, bass.ds(c, 1), 2 * E:2 * E + 2])
                    nc.vector.tensor_copy(pick_idx[:, i:i + 1, :], record[:, bass.ds(c, 1), 2 * E + 2:REC]
                                          ).then_inc(idx_ready, 1)

                def combine(k, i):
                    c = RG * k + i
                    dve.wait_ge(pick_in[i], 32 * k + 32)
                    dve.wait_ge(idx_ready, c + 1)
                    nc.vector.scalar_tensor_tensor(half[:, i:i + 1, :], picks[0][i][:, :].rearrange("p (o d) -> p o d", o=1),
                                                   pick_w[:, i, 0:1], tokens[:, bass.ds(c, 1), :], ALU.mult, ALU.add
                                                   ).then_inc(half_sum, 1)
                    dve.wait_ge(half_sum, c + 1)
                    dve.wait_ge(out_stored[i], 16 * k + 1)
                    nc.vector.scalar_tensor_tensor(result[i][:, :], picks[1][i][:, :], pick_w[:, i, 1:2], half[:, i, :],
                                                   ALU.mult, ALU.add).then_inc(result_ready, 1)

                for i in range(RG):
                    fetch(i, i)
                with dve.Fori(0, TILES // RG - 1) as k:
                    for i in range(RG):
                        combine(k, i)
                        dve.wait_ge(result_ready, RG * k + i + 1)
                        fetch(RG * k + i + RG, i)
                for i in range(RG):
                    combine(TILES // RG - 1, i)

            @block.tensor
            def _(pe):
                def transposes(par):
                    for k in range(3):
                        dst = rT_ps[k // 2][:, 0:GROUP].bitcast(FP16)
                        for r in range(NT):
                            c = (k % 2) * GROUP + r * P
                            ins = nc.tensor.transpose(dst[:, c:c + P], rows[par][:, r, k * P:k * P + P], ident16[:, :])
                    ins.then_inc(rT_ready, 1)

                pe.wait_ge(rows_in[0], 16)
                transposes(0)

                def at_expert(e, ep, last):
                    pe.wait_ge(w_ready, e + 1)
                    alone(pe, spare)

                def step(g, par, ep):
                    for k in range(2):
                        pe.wait_ge(rT_sb[k], g + 1)
                    for m in range(HT):
                        pe.wait_ge(hidden_sb, HT * g + m + 1)
                        product([w[:, :] for w in w1_sb[ep]], slice(m * P, m * P + P), rT[par], slice(0, GROUP),
                                h_ps[m % HB][:, 0:GROUP], False).then_inc(hidden_ps, 1)
                    pe.wait_ge(rows_in[1 - par], 8 * (g - par) + 16 + 16 * par)
                    transposes(1 - par)
                    pe.wait_ge(ex_added, g + 1)
                    w2_hi, w2_lo = w2_sb[ep]
                    for r in range(NT):
                        dst = ex_ps[r // 2][:, (r % 2) * D:(r % 2) * D + D]
                        for m in range(HT):
                            if r == 0:
                                pe.wait_ge(hidden_split, HT * g + m + 1)
                            h_hi, h_lo = (h[:, m, r * P:r * P + P] for h in hT)
                            nc.tensor.matmul(dst, h_hi, w2_hi[:, m, :], start=(m == 0), stop=False)
                            nc.tensor.matmul(dst, h_hi, w2_lo[:, m, :], start=False, stop=False)
                            ins = nc.tensor.matmul(dst, h_lo, w2_hi[:, m, :], start=False, stop=(m == HT - 1))
                    ins.then_inc(ex_ready, 1)

                each_step(pe, step, at_expert)


_INS = ["x", "L0_attn_W_Q", "L0_attn_W_K", "L0_attn_W_V", "L0_attn_W_O", "L0_ffn_Wg", "L0_ffn_W1", "L0_ffn_b1",
        "L0_ffn_W2", "L0_ffn_b2"]


def kernel(**inputs):
    import numpy as np
    import concourse.bacc as bacc
    from concourse.bass_utils import run_bass_kernel_spmd

    nc = bacc.Bacc("TRN2", target_bir_lowering=False, num_devices=1)
    arrays, args = {}, []
    for name in _INS:
        a = np.ascontiguousarray(inputs[name])
        arrays[f"in_{name}"] = a
        args.append(nc.dram_tensor(f"in_{name}", a.shape, mybir.dt.from_np(a.dtype), kind="ExternalInput").ap())
    batches, rows, width = inputs["x"].shape
    span = SEG * DILATION
    shape = (batches, -(-rows // span) * SEG, width)
    out = nc.dram_tensor("out_dram", shape, FP32, kind="ExternalOutput").ap()
    audio_tower_kernel(nc, *args, out)
    r = run_bass_kernel_spmd(nc, [arrays], core_ids=[0])
    return r.results[0]["out_dram"]
```

```python
import concourse.bass as bass
from concourse import mybir
from contextlib import ExitStack

FP32 = mybir.dt.float32
BF16 = mybir.dt.bfloat16
FP16 = mybir.dt.float16
U32 = mybir.dt.uint32
I32 = mybir.dt.int32
ALU = mybir.AluOpType
ACT = mybir.ActivationFunctionType
AX = mybir.AxisListType.X

P = 128
SEG = 64
DILATION = 2
LN_EPS = 1e-5
RSQRT_SEED = float(0x5F3759DF)
NEWTON_STEPS = 3
MASKED = -1e30
X_SCALE = 2.0 ** 8
W_SCALE = 2.0 ** 8
QK_SCALE = 2.0 ** 5
O_SCALE = 2.0 ** 6
H_SCALE = 2.0 ** 6
OUT_OF_BOUNDS = float(1 << 20)
CAPACITY_RATIO = 1.25
TOP_K = 2
SEARCH_STEPS = 26


def after(eng, sem, count):
    if not (isinstance(count, int) and count <= 0):
        eng.wait_ge(sem, count)


def alone(eng, sem):
    eng.sem_inc(sem, 1)


def over_rows(ap, shape):
    return ap.rearrange("p (t o) -> p t o", o=1).to_broadcast(shape)


def over_tiles(ap, shape):
    return ap.rearrange("p (o n) -> p o n", o=1).to_broadcast(shape)


class Chain:

    def __init__(self, eng, sem, base):
        self.eng, self.sem, self.base, self.n = eng, sem, base, 0

    def pause(self, ins):
        self.n += 1
        ins.then_inc(self.sem, 1)

    def resume(self):
        self.eng.wait_ge(self.sem, self.base + self.n)

    def step(self, ins):
        self.pause(ins)
        self.resume()


def audio_tower_kernel(nc, x, wq, wk, wv, wo, wg, w1, b1, w2, b2, out):
    B, S_IN, D = x.shape
    H, _, DK = wq.shape
    E, _, HID = w1.shape
    S = -(-S_IN // (SEG * DILATION)) * SEG
    REAL = -(-S_IN // DILATION)
    NT = S // P
    TILES = B * NT
    T = B * S
    CAP = int(CAPACITY_RATIO * T * TOP_K / E)
    GROUP = NT * P
    GPE = -(-CAP // (2 * GROUP)) * 2
    CAPP = GPE * GROUP
    D1 = D - P
    PAIRS = H // 2
    HT = HID // P
    UNITS = H * NT
    PROJ = 2 * PAIRS + 2 * NT
    VH = H * DK // 2
    TOK_SCALE = float(D) ** -0.5
    QK_OUT = QK_SCALE / (X_SCALE * W_SCALE)
    V_OUT = 1 / (X_SCALE * W_SCALE)
    S_OUT = float(DK) ** -0.5 / QK_SCALE ** 2
    WO_OUT = 1 / (O_SCALE * W_SCALE)
    H_OUT = 1 / (X_SCALE * W_SCALE)
    EX_OUT = 1 / (H_SCALE * W_SCALE)
    REC = 2 * E + 4
    assert S == NT * P and D1 == 64 and DK == 64 and B % 2 == 0 and UNITS % 4 == 0

    slots_dram = nc.dram_tensor("slots_dram", (E * CAPP + GROUP, 2 * D), FP16).ap()
    expert_dram = nc.dram_tensor("expert_dram", (E * CAPP, D), FP32).ap()

    top = ExitStack()
    with top:
        def sb(name, shape, dt=FP32, ctx=top):
            return ctx.enter_context(nc.sbuf_tensor(name, shape, dt))

        def sem(name):
            return top.enter_context(nc.semaphore(name))

        tokens = sb("tokens", [P, TILES, D])
        record = sb("record", [P, TILES, REC])
        ident = sb("ident", [P, P])
        ident_bf = sb("ident_bf", [P, P], BF16)
        ident16 = sb("ident16", [P, P], FP16)
        before = sb("before", [P, P], BF16)
        ones_bf = sb("ones_bf", [P, P], BF16)
        running = sb("running", [P, 2, E])
        expert_base = sb("expert_base", [P, E])
        first_wins = sb("first_wins", [P, E])
        most = sb("most", [P, 1], I32)
        spare = sem("spare")

        LN_PARTS = 4
        LN_STEPS = 6 + 2 * NEWTON_STEPS

        def layer_norm(chain, src, dst, st, mv, v, yw, t, n, parts=range(LN_PARTS)):
            y, w = yw[:, 0, 0:n], yw[:, 1, 0:n]

            def newton(chain_end=None):
                chain.step(nc.vector.tensor_tensor(t[:, 0:n], w, y, ALU.mult))
                (chain_end or chain.step)(nc.vector.scalar_tensor_tensor(
                    yw[:, :, 0:n], over_tiles(t[:, 0:n], [P, 2, n]), 1.5, yw[:, :, 0:n], ALU.add, ALU.mult))

            if 0 in parts:
                alone(chain.eng, spare)
                for i in range(n):
                    ins = nc.vector.bn_stats(st[:, i, :], src[:, i, :])
                chain.step(ins)
                alone(chain.eng, spare)
                for i in range(n):
                    ins = nc.vector.bn_aggr(mv[:, i, :], st[:, i, :])
                chain.pause(ins)
            if 1 in parts:
                chain.resume()
                chain.step(nc.vector.tensor_scalar(v[:, 0:n], mv[:, 0:n, 1], LN_EPS, X_SCALE ** -2, ALU.add, ALU.mult))
                chain.step(nc.vector.tensor_scalar(t[:, 0:n].bitcast(I32), v[:, 0:n].bitcast(I32), 1, None,
                                                   ALU.logical_shift_right))
                chain.step(nc.vector.tensor_scalar(y.bitcast(I32), t[:, 0:n].bitcast(I32), -1.0, RSQRT_SEED,
                                                   ALU.mult, ALU.add))
                chain.pause(nc.vector.scalar_tensor_tensor(w, v[:, 0:n], -0.5, y, ALU.mult, ALU.mult))
            if 2 in parts:
                chain.resume()
                for _ in range(NEWTON_STEPS - 2):
                    newton()
                newton(chain.pause)
            if 3 in parts:
                chain.resume()
                newton()
                for i in range(n):
                    ins = nc.vector.tensor_scalar(dst[:, i, :], src[:, i, :], mv[:, i, 0:1], yw[:, 0, i:i + 1],
                                                  ALU.subtract, ALU.mult)
                return ins

        def split_rest(src, dst):
            nc.vector.tensor_tensor(dst[:, :, D:2 * P], src[:, :, P:D], dst[:, :, P:D], ALU.subtract)
            return nc.vector.tensor_tensor(dst[:, :, 2 * P:2 * D], src[:, :, 0:P], dst[:, :, 0:P], ALU.subtract)

        def split_weights(chain, first, last, hi, lo, hi_twice, lo_last):
            nc.vector.tensor_scalar(hi_twice, last, W_SCALE, None, ALU.mult)
            chain.step(nc.vector.tensor_scalar(hi, first, W_SCALE, None, ALU.mult))
            nc.vector.scalar_tensor_tensor(lo, first, W_SCALE, hi, ALU.mult, ALU.subtract)
            return nc.vector.scalar_tensor_tensor(lo_last, last[0:D1], W_SCALE, hi_twice[0:D1], ALU.mult, ALU.subtract)

        def product(w, wc, xT, xc, dst, weights_move):
            w_hi, w_lo, w_twice, w_last = w
            terms = ((w_hi[:, wc], xT[:, 0, xc]), (w_lo[:, wc], xT[:, 0, xc]), (w_hi[:, wc], xT[:, 2, xc]),
                     (w_twice[:, wc], xT[:, 1, xc]), (w_last[:, wc], xT[0:D1, 1, xc]))
            for i, (a, b) in enumerate(terms):
                if weights_move:
                    a, b = b, a
                ins = nc.tensor.matmul(dst, a, b, start=(i == 0), stop=(i == len(terms) - 1))
            return ins

        part = ExitStack()
        with part:
            def sa(name, shape, dt=FP32):
                return sb(name, shape, dt, part)

            def ps(name, shape, dt=FP32):
                return part.enter_context(nc.psum_tensor(name, shape, dt))

            def w16(name, n, own_last=True):
                return [sa(name + "_hi", [P, n], FP16), sa(name + "_lo", [P, n], FP16),
                        sa(name + "_twice", [P, n], FP16), sa(name + "_last", [D1, n], FP16) if own_last else None]

            w_q, w_k, w_v, w_g = w16("w_q", H * DK, False), w16("w_k", H * DK), w16("w_v", H * DK), w16("w_g", E)
            wo_hi, wo_lo = sa("wo_hi", [P, PAIRS, D], FP16), sa("wo_lo", [P, PAIRS, D], FP16)
            wg_raw = sa("wg_raw", [P, 2, E])
            causal = sa("causal", [P, P], BF16)
            own_segment = sa("own_segment", [P, P])
            zeros = sa("zeros", [P, 2 * D], FP16)

            xin = [sa(f"xin{i}", [P, NT, D]) for i in range(2)]
            both_last = sa("both_last", [P, H * DK], FP16)
            xsT_first, xsT_last = sa("xsT_first", [P, S]), both_last[D1:P, :].bitcast(FP32)[:, 0:S]
            w_q[3] = both_last[0:D1, :]
            tok_max, tok_sum, tok_inv = sa("tok_max", [P, NT]), sa("tok_sum", [P, NT]), sa("tok_inv", [P, NT])
            st, mv = sa("st", [P, NT, 6]), sa("mv", [P, NT, 2])
            ln_v, ln_yw, ln_t = sa("ln_v", [P, NT]), sa("ln_yw", [P, 2, NT]), sa("ln_t", [P, NT])
            xn = sa("xn", [P, NT, D])
            xs = sa("xs", [P, NT, 2 * D], FP16)
            xT = sa("xT", [P, 3, S], FP16)
            QT = [[sa(f"QT_{k}{i}", [P, PAIRS, S], FP16) for k in ("hi", "lo")] for i in range(2)]
            KT = [[sa(f"KT_{k}{i}", [P, PAIRS, S], FP16) for k in ("hi", "lo")] for i in range(2)]
            V = [sa(f"V{i}", [P, NT, H * DK]) for i in range(2)]
            NR = 4
            neg_max = sa("neg_max", [P, NR])
            unread = sa("unread", [P, 2, S], BF16)
            prob = sa("prob", [P, NR, S])
            probT = sa("probT", [P, NR, S])
            row_sum = sa("row_sum", [P, H, NT])
            row_inv = sa("row_inv", [P, H, NT])
            O_sb = sa("O_sb", [P, 2, NT, P])
            OT_hi, OT_lo = sa("OT_hi", [P, PAIRS, S], FP16), sa("OT_lo", [P, PAIRS, S], FP16)
            st2, mv2 = sa("st2", [P, NT, 6]), sa("mv2", [P, NT, 2])
            ln_v2, ln_yw2, ln_t2 = sa("ln_v2", [P, NT]), sa("ln_yw2", [P, 2, NT]), sa("ln_t2", [P, NT])
            xs2 = [sa(f"xs2_{i}", [P, NT, 2 * D], FP16) for i in range(2)]
            x2T = sa("x2T", [P, 3, S], FP16)
            tok_s, tok_p, tok_pT = (big[:, :, :].rearrange("p k s -> p (k s)").bitcast(FP32)[:, 0:NT * P]
                                    .rearrange("p (t k) -> p t k", t=NT) for big in (xs, xT, x2T))
            lg, lg2 = sa("lg", [P, NT, E]), sa("lg2", [P, NT, E])
            key = sa("key", [P, NT, E])
            top1, top2, key_max = sa("top1", [P, NT]), sa("top2", [P, NT]), sa("key_max", [P, NT])
            gap, gap_exp, gap_sum = sa("gap", [P, NT]), sa("gap_exp", [P, NT]), sa("gap_sum", [P, NT])
            rec = sa("rec", [P, NT, REC])
            sel2 = sa("sel2", [P, NT, E])
            chosen_bf = sa("chosen_bf", [P, NT, E], BF16)
            pos, late = sa("pos", [P, NT, E]), sa("late", [P, NT, E])
            picked = sa("picked", [P, NT, E])
            slot_idx = [sa(f"slot_idx{i}", [P, NT, 2], U32) for i in range(2)]

            S_ps = [ps(f"S_ps{i}", [P, 512]) for i in range(2)]
            T_ps = [ps(f"T_ps{i}", [P, 512]) for i in range(2)]
            O_ps = ps("O_ps", [P, 512])
            FA, FB = ps("FA", [P, 512]), ps("FB", [P, 512])
            TA = ps("TA", [P, 512])
            wo_raw = OT_hi[:, :, :].rearrange("p m s -> p (m s)").bitcast(FP32).rearrange("p (m d) -> p m d", m=PAIRS)
            O_view = O_ps[:, 0:NT * P].rearrange("p (t c) -> p t c", t=NT)

            zero_ready, const_pool, consts = sem("zero_ready"), sem("const_pool"), sem("consts")
            x_in = [sem("x_in0"), sem("x_in1")]
            rows_zeroed = sem("rows_zeroed")
            xsT_ps, xsT_first_sb, xsT_last_sb = sem("xsT_ps"), sem("xsT_first_sb"), sem("xsT_last_sb")
            tok_scores, tok_max_ready, tok_exp = sem("tok_scores"), sem("tok_max_ready"), sem("tok_exp")
            tok_pT_ps, tok_pT_sb, tok_mixed = sem("tok_pT_ps"), sem("tok_pT_sb"), sem("tok_mixed")
            raw_in, split = [sem(f"raw_{k}_in") for k in ("q", "k", "v", "rest")], sem("split")
            xn_there, xn_hi, xn2_there, xn2_hi = sem("xn_there"), sem("xn_hi"), sem("xn2_there"), sem("xn2_hi")
            xn_ready, xnT_ps, xT_sb = sem("xn_ready"), sem("xnT_ps"), [sem("xT_sb_act"), sem("xT_sb_dve")]
            proj_ps, qk_hi, qk_sb = sem("proj_ps"), sem("qk_hi"), sem("qk_sb")
            v_sb = [sem("v_sb_act"), sem("v_sb_dve")]
            scores, max_ready, exp_done = sem("scores"), sem("max_ready"), sem("exp_done")
            probT_ps = sem("probT_ps")
            probT_sb = sem("probT_sb")
            attended, normed = sem("attended"), sem("normed")
            OT_ps, OT_hi_sb, OT_sb = sem("OT_ps"), sem("OT_hi_sb"), sem("OT_sb")
            wo_ps, wo_added = sem("wo_ps"), sem("wo_added")
            xn2_ready, x2T_ps, x2T_sb = sem("xn2_ready"), sem("x2T_ps"), sem("x2T_sb")
            totals_ready = sem("totals_ready")
            logits_ps, logits_sb, ranks_sb = sem("logits_ps"), sem("logits_sb"), sem("ranks_sb")
            gap_ready, gap_exped = sem("gap_ready"), sem("gap_exped")
            chosen_ready, ranks_ps, slots_ready = sem("chosen_ready"), sem("ranks_ps"), sem("slots_ready")
            xn2_free = sem("xn2_free")
            scattered = [sem("scattered0"), sem("scattered1")]
            front_chain, tail_chain, norm_chain = sem("front_chain"), sem("tail_chain"), sem("norm_chain")

            SPLIT_STEPS = 10
            FRONT_STEPS = 3 + LN_STEPS
            TAIL_STEPS = LN_STEPS + 5 + 1 + 5 + 2 + 4 + 4

            F_XT, F_SCORE, F_PT, F_MIX, F_HI, F_XNT, F_PROJ = 1, 3, 5, 7, 13, 16, UNITS - PROJ
            T_WO, T_HI, T_X2T, T_LOGIT, T_RANK = 4, 19, 22, 25, 30
            F_NORM, T_NORM = (8, 10, 11, 12), (14, 16, 17, 18)
            PAIR = 2 * NT

            def pairs_copied(n):
                return (n - 3) // PAIR


            def alternate(b, par, first, last, unit, front, tail):
                for n in range(UNITS):
                    unit(b, par, n, first, last)
                    if not first:
                        tail(b - 1, 1 - par, n)
                    if not last:
                        front(b + 1, 1 - par, n)

            def run(eng, unit, front, tail):
                for n in range(UNITS):
                    front(0, 0, n)
                alternate(0, 0, True, False, unit, front, tail)
                if B > 2:
                    with eng.Fori(0, B // 2 - 1) as j:
                        for u in range(2):
                            alternate(2 * j + 1 + u, (1 + u) % 2, False, False, unit, front, tail)
                alternate(B - 1, 1, False, True, unit, front, tail)

            block = part.enter_context(nc.Block())

            @block.sync
            def _(sp):
                LAST = REAL - (NT - 1) * P

                def load(b, par):
                    xb = x[bass.ds(b, 1), :, :].rearrange("o (s two) d -> (o s) two d", two=DILATION)
                    full = (NT - 1) * P
                    sp.dma_start(xin[par][:, 0:NT - 1, :],
                                 xb[0:full, 0, :].rearrange("(t p) d -> p t d", p=P)).then_inc(x_in[par], 16)
                    sp.dma_start(xin[par][0:LAST, NT - 1, :], xb[full:REAL, 0, :]).then_inc(x_in[par], 16)

                def zero_rows(k):
                    for e in range(E):
                        sp.dma_start(slots_dram[bass.ds(k * GROUP + e * CAPP, GROUP), :]
                                     .rearrange("(p r) d -> p r d", p=P), over_tiles(zeros[:, :], [P, NT, 2 * D])
                                     ).then_inc(rows_zeroed, 16)

                sp.wait_ge(zero_ready, 1)
                load(0, 0)
                load(1, 1)
                for i, w in enumerate((wq, wk, wv)):
                    for k, (lo, hi, rows) in enumerate(((0, P, slice(0, P)), (P, D, slice(0, D1)), (P, D, slice(D1, P)))):
                        n = (2 * i + min(k, 1))
                        sp.dma_start((V[0], V[1])[n // 3][rows, n % 3, :].rearrange("p (h k) -> p h k", h=H),
                                     w[:, lo:hi, :].rearrange("h m k -> m h k")).then_inc(raw_in[i], 16)
                for k, (lo, hi, rows) in enumerate(((0, P, slice(0, P)), (P, D, slice(0, D1)), (P, D, slice(D1, P)))):
                    sp.dma_start(wg_raw[rows, min(k, 1), :], wg[lo:hi, :]).then_inc(raw_in[3], 16)
                sp.dma_start(wo_raw, wo.rearrange("(c p) d -> p c d", p=P)).then_inc(raw_in[3], 16)
                sp.dma_start(slots_dram[E * CAPP:E * CAPP + GROUP, :].rearrange("(p r) d -> p r d", p=P),
                             over_tiles(zeros[:, :], [P, NT, 2 * D])).then_inc(rows_zeroed, 16)
                for turns, fill in ((range(1, GPE // 2 + 1), True), (range(GPE // 2 + 1, B // 2), False)):
                    if not len(turns):
                        continue
                    with sp.Fori(turns.start, turns.stop) as j:
                        for par in range(2):
                            if fill:
                                zero_rows(2 * j - 2 + par)
                            sp.wait_ge(tok_mixed, 2 * j - 1 + par)
                            load(2 * j + par, par)

            @block.gpsimd
            def _(pool):
                nc.gpsimd.memset(ident[:, :], 0.0).then_inc(const_pool, 1)
                nc.gpsimd.memset(ident_bf[:, :], 0.0).then_inc(const_pool, 1)
                nc.gpsimd.memset(ident16[:, :], 0.0).then_inc(const_pool, 1)
                nc.gpsimd.memset(before[:, :], 1.0).then_inc(const_pool, 1)
                nc.gpsimd.memset(causal[:, :], 0.0).then_inc(const_pool, 1)
                pool.wait_ge(const_pool, 5)
                for m in (ident, ident_bf, ident16):
                    nc.gpsimd.affine_select(out=m[:, :], in_=m[:, :], compare_op=ALU.not_equal, fill=1.0, base=0,
                                            pattern=[[-1, P]], channel_multiplier=1).then_inc(consts, 1)
                nc.gpsimd.affine_select(out=before[:, :], in_=before[:, :], compare_op=ALU.is_gt, fill=0.0, base=0,
                                        pattern=[[1, P]], channel_multiplier=-1).then_inc(consts, 1)
                nc.gpsimd.affine_select(out=causal[:, :], in_=causal[:, :], compare_op=ALU.is_ge, fill=MASKED, base=0,
                                        pattern=[[-1, P]], channel_multiplier=1).then_inc(consts, 1)

                pool.sem_inc(xn2_free, 2)

                def scatter(b, par, zeroed):
                    pool.wait_ge(slots_ready, b + 1)
                    if zeroed is not None:
                        pool.wait_ge(rows_zeroed, zeroed)
                    alone(pool, spare)
                    for t in range(NT):
                        for k in range(2):
                            pool.indirect_dma_start(
                                slots_dram[:, :], bass.IndirectOffsetOnAxis(slot_idx[par][:, t, k:k + 1], 0),
                                xs2[par][:, t, :], None, bounds_check=E * CAPP - 1, oob_is_err=False
                            ).then_inc(scattered[par], 16)
                    pool.wait_ge(scattered[par], NT * 16 * (b - par) + 2 * NT * 16)
                    pool.sem_inc(xn2_free, 1)

                with pool.Fori(0, GPE // 2) as j:
                    for par in range(2):
                        scatter(2 * j + par, par, 16 + 16 * E * (2 * j + par + 1))
                if B > GPE:
                    with pool.Fori(GPE // 2, B // 2) as j:
                        for par in range(2):
                            scatter(2 * j + par, par, None)
                pool.wait_ge(rows_zeroed, 16 + 16 * E * GPE)

            @block.scalar
            def _(act):
                def front(b, par, n):
                    if n == F_XT:
                        act.wait_ge(xsT_ps, b + 1)
                        nc.scalar.activation(xsT_first[:, :], FA[:, 0:S], ACT.Copy).then_inc(xsT_first_sb, 1)
                    if n == F_SCORE:
                        act.wait_ge(tok_max_ready, b + 1)
                        for t in range(NT):
                            nc.scalar.activation(tok_p[:, t, :], tok_s[:, t, :], ACT.Exp, bias=tok_max[:, t:t + 1],
                                                 accum_out=tok_sum[:, t:t + 1]).then_inc(tok_exp, 1)
                    if n == F_HI:
                        act.wait_ge(xn_there, b + 1)
                        nc.scalar.activation(xs[:, :, 0:D], xn[:, :, :], ACT.Copy).then_inc(xn_hi, 1)
                    if n == F_XNT:
                        act.wait_ge(xnT_ps, b + 1)
                        nc.scalar.activation(xT[:, 0:2, :], FA[:, 0:S].bitcast(FP16).rearrange("p (k s) -> p k s", k=2),
                                             ACT.Copy).then_inc(xT_sb[0], 1)
                    q = n - F_PROJ
                    if 0 <= q and (q < 2 * PAIRS or q % 2 == 0):
                        act.wait_ge(proj_ps, PROJ * b + q + 1)
                        if q == 0:
                            after(act, attended, UNITS * (b - 1))
                        src = (FA, FB)[q % 2]
                        if q < 2 * PAIRS:
                            dst = (QT, KT)[q // PAIRS][par][0][:, q % PAIRS, :]
                            nc.scalar.activation(dst, src[:, 0:S], ACT.Copy, scale=QK_OUT).then_inc(qk_hi, 1)
                        else:
                            t, half = divmod(q - 2 * PAIRS, 2)
                            nc.scalar.activation(V[par][:, t, half * VH:half * VH + VH], src[:, 0:VH], ACT.Copy,
                                                 scale=V_OUT).then_inc(v_sb[0], 1)

                def exp_unit(b, par, n):
                    g = UNITS * b + n
                    h, t = divmod(n, NT)
                    w = P * (t + 1)
                    act.wait_ge(max_ready, g + 1)
                    after(act, probT_ps, g - NR + 1)
                    nc.scalar.activation(prob[:, n % NR, 0:w], S_ps[n % 2][:, 0:w], ACT.Exp,
                                         bias=neg_max[:, n % NR:n % NR + 1], scale=S_OUT,
                                         accum_out=row_sum[:, h, t:t + 1]).then_inc(exp_done, 1)

                def copy_OT(b, m):
                    k = PAIRS * b + m
                    act.wait_ge(OT_ps, k + 1)
                    if m == 0:
                        after(act, wo_ps, 2 * b)
                    nc.scalar.activation(OT_hi[:, m, :], TA[:, 0:S], ACT.Copy, scale=O_SCALE).then_inc(OT_hi_sb, 1)

                def unit(b, par, n, first, last):
                    g = UNITS * b + n
                    w = P * (n % NT + 1)
                    if first and n == 0:
                        exp_unit(b, par, 0)
                        exp_unit(b, par, 1)
                    act.wait_ge(probT_ps, g + 1)
                    after(act, attended, g - NR + 1)
                    nc.scalar.activation(probT[:, n % NR, 0:w], T_ps[n % 2][:, 0:w], ACT.Copy).then_inc(probT_sb, 1)
                    if n + 2 < UNITS:
                        exp_unit(b, par, n + 2)
                    elif not last:
                        exp_unit(b + 1, 1 - par, n + 2 - UNITS)
                    if n % PAIR == 2:
                        if n > 2:
                            copy_OT(b, n // PAIR - 1)
                        elif not first:
                            copy_OT(b - 1, PAIRS - 1)

                def tail(b, par, n):
                    if n == T_HI:
                        act.wait_ge(xn2_there, b + 1)
                        act.wait_ge(xn2_free, b + 1)
                        nc.scalar.activation(xs2[par][:, :, 0:D], xn[:, :, :], ACT.Copy).then_inc(xn2_hi, 1)
                    if n == T_LOGIT + 3:
                        act.wait_ge(gap_ready, b + 1)
                        nc.scalar.activation(gap_exp[:, :], gap[:, :], ACT.Exp).then_inc(gap_exped, 1)

                run(act, unit, front, tail)
                copy_OT(B - 1, PAIRS - 1)
                for n in range(UNITS):
                    tail(B - 1, 1, n)

            @block.vector
            def _(dve):
                nc.vector.memset(zeros[:, :], 0.0)
                nc.vector.memset(running[:, :, :], 0.0)
                nc.vector.memset(ones_bf[:, :], 1.0)
                nc.vector.memset(own_segment[:, :], 0.0)
                nc.vector.memset(xin[0][:, :, :], 0.0)
                nc.vector.memset(xin[1][:, :, :], 0.0).then_inc(zero_ready, 1)
                for e in range(E):
                    nc.vector.memset(expert_base[:, e:e + 1], float(e * CAPP))
                    nc.vector.memset(first_wins[:, e:e + 1], float(E - e))
                dve.wait_ge(zero_ready, 1)
                nc.vector.memset(own_segment[0:SEG, SEG:P], MASKED)
                nc.vector.memset(own_segment[SEG:P, 0:SEG], MASKED).then_inc(zero_ready, 1)
                dve.wait_ge(zero_ready, 2)

                split_chain = Chain(dve, split, 0)

                def split_qkv(i):
                    dve.wait_ge(raw_in[i], 16 * 3)
                    raw = [(V[0], V[1])[n // 3][:, n % 3, :] for n in (2 * i, 2 * i + 1)]
                    split_chain.step(split_weights(split_chain, raw[0], raw[1], *(t[:, :] for t in (w_q, w_k, w_v)[i])))

                def split_last():
                    dve.wait_ge(raw_in[3], 16 * 4)
                    split_chain.step(split_weights(split_chain, wg_raw[:, 0, :], wg_raw[:, 1, :], *(t[:, :] for t in w_g)))
                    split_chain.step(nc.vector.tensor_scalar(wo_hi[:, :, :], wo_raw, W_SCALE, None, ALU.mult))
                    split_chain.step(nc.vector.scalar_tensor_tensor(wo_lo[:, :, :], wo_raw, W_SCALE, wo_hi[:, :, :],
                                                                    ALU.mult, ALU.subtract))
                    assert split_chain.n == SPLIT_STEPS

                chains = {}

                def front(b, par, n):
                    if n == 0:
                        chains["front"] = Chain(dve, front_chain, FRONT_STEPS * b)
                    chain = chains["front"]
                    if n == F_XT:
                        dve.wait_ge(xsT_ps, b + 1)
                        nc.vector.tensor_copy(xsT_last[:, :], FB[0:D1, 0:S]).then_inc(xsT_last_sb, 1)
                    if n == F_SCORE:
                        dve.wait_ge(tok_scores, b + 1)
                        chain.step(nc.vector.scalar_tensor_tensor(
                            tok_s[:, :, :], FA[:, 0:S].rearrange("p (t k) -> p t k", t=NT), TOK_SCALE,
                            over_tiles(own_segment[:, :], [P, NT, P]), ALU.mult, ALU.add))
                        nc.vector.tensor_reduce(tok_max[:, :], tok_s[:, :, :], AX, ALU.max,
                                                negate=True).then_inc(tok_max_ready, 1)
                    if n == F_PT:
                        dve.wait_ge(tok_pT_ps, b + 1)
                        nc.vector.tensor_copy(tok_pT[:, :, :], FB[:, 0:S].rearrange("p (t k) -> p t k", t=NT)
                                              ).then_inc(tok_pT_sb, 1)
                        dve.wait_ge(tok_exp, NT * (b + 1))
                        chain.step(nc.vector.reciprocal(tok_inv[:, :], tok_sum[:, :]))
                    if n == F_MIX:
                        dve.wait_ge(tok_mixed, b + 1)
                        for t in range(NT):
                            src = FA[:, t * D:t * D + D] if t < 2 else FB[:, 0:D]
                            ins = nc.vector.tensor_scalar(tokens[:, bass.ds(NT * b + t, 1), :],
                                                          src.rearrange("p (o d) -> p o d", o=1),
                                                          tok_inv[:, t:t + 1], None, ALU.mult)
                        chain.pause(ins)
                    if n in F_NORM:
                        part = F_NORM.index(n)
                        if part == 0:
                            chain.resume()
                        ins = layer_norm(chain, tokens[:, bass.ds(NT * b, NT), :], xn, st, mv, ln_v, ln_yw, ln_t, NT, (part,))
                        if part == LN_PARTS - 1:
                            ins.then_inc(xn_there, 1)
                    if n == F_HI + 1:
                        dve.wait_ge(xn_hi, b + 1)
                        split_rest(xn, xs).then_inc(xn_ready, 1)
                        dve.wait_ge(xn_ready, b + 1)
                    if n == F_XNT:
                        dve.wait_ge(xnT_ps, b + 1)
                        nc.vector.tensor_copy(xT[:, 2, :], FB[:, 0:S // 2].bitcast(FP16)).then_inc(xT_sb[1], 1)
                    q = n - F_PROJ
                    if isinstance(b, int) and b == 0:
                        if q == -1:
                            split_qkv(0)
                        if q == 2:
                            split_qkv(1)
                        if q == PAIRS + 2:
                            split_qkv(2)
                            split_last()
                    if 0 <= q < 2 * PAIRS:
                        src = (FA, FB)[q % 2]
                        hi, lo = ((QT, KT)[q // PAIRS][par][k][:, q % PAIRS, :] for k in range(2))
                        dve.wait_ge(qk_hi, 2 * PAIRS * b + q + 1)
                        nc.vector.scalar_tensor_tensor(lo, src[:, 0:S], QK_OUT, hi, ALU.mult, ALU.subtract
                                                       ).then_inc(qk_sb, 1)
                    elif q >= 0 and q % 2:
                        t, half = divmod(q - 2 * PAIRS, 2)
                        dve.wait_ge(proj_ps, PROJ * b + q + 1)
                        nc.vector.tensor_scalar(V[par][:, t, half * VH:half * VH + VH], FB[:, 0:VH], V_OUT, None, ALU.mult
                                                ).then_inc(v_sb[1], 1)
                    if n == UNITS - 1:
                        assert chain.n == FRONT_STEPS, chain.n

                def max_unit(b, par, n):
                    g = UNITS * b + n
                    w = P * (n % NT + 1)
                    dve.wait_ge(scores, g + 1)
                    after(dve, exp_done, g - NR + 1)
                    nc.vector.tensor_scalar(unread[:, n % 2, 0:w], S_ps[n % 2][:, 0:w], -S_OUT, None, ALU.mult, ALU.min,
                                            accum_out=neg_max[:, n % NR:n % NR + 1]).then_inc(max_ready, 1)

                def norm_pair(b, m):
                    k = PAIRS * b + m
                    dve.wait_ge(exp_done, UNITS * b + 2 * NT * (m + 1))
                    nc.vector.reciprocal(row_inv[:, 2 * m:2 * m + 2, :], row_sum[:, 2 * m:2 * m + 2, :]
                                         ).then_inc(norm_chain, 1)
                    dve.wait_ge(norm_chain, k + 1)
                    dve.wait_ge(attended, UNITS * b + 2 * NT * (m + 1))
                    after(dve, OT_ps, k - 1)
                    ins = nc.vector.tensor_tensor(
                        O_sb[:, m % 2, :, :].rearrange("p t (h c) -> p t h c", h=2),
                        O_view.rearrange("p t (h c) -> p t h c", h=2),
                        row_inv[:, 2 * m:2 * m + 2, :].rearrange("p h (t o) -> p t h o", o=1).to_broadcast([P, NT, 2, DK]),
                        ALU.mult)
                    ins.then_inc(normed, 1)

                def rest_of_OT(b, m):
                    dve.wait_ge(OT_hi_sb, PAIRS * b + m + 1)
                    nc.vector.scalar_tensor_tensor(OT_lo[:, m, :], TA[:, 0:S], O_SCALE, OT_hi[:, m, :], ALU.mult,
                                                   ALU.subtract).then_inc(OT_sb, 1)

                def unit(b, par, n, first, last):
                    if first and n == 0:
                        max_unit(b, par, 0)
                        max_unit(b, par, 1)
                    if n + 2 < UNITS:
                        max_unit(b, par, n + 2)
                    elif not last:
                        max_unit(b + 1, 1 - par, n + 2 - UNITS)
                    if n % PAIR == 0:
                        if n:
                            norm_pair(b, n // PAIR - 1)
                        elif not first:
                            norm_pair(b - 1, PAIRS - 1)
                    if n % PAIR == 3:
                        if n > 3:
                            rest_of_OT(b, n // PAIR - 1)
                        elif not first:
                            rest_of_OT(b - 1, PAIRS - 1)

                def tail(b, par, n):
                    if n == 0:
                        chains["tail"] = Chain(dve, tail_chain, TAIL_STEPS * b)
                    chain = chains["tail"]
                    for use, (lo, hi) in enumerate(((0, 2), (2, NT))):
                        if n == T_WO + use:
                            dve.wait_ge(wo_ps, 2 * b + use + 1)
                            h = tokens[:, bass.ds(NT * b + lo, hi - lo), :]
                            nc.vector.scalar_tensor_tensor(h, TA[:, 0:(hi - lo) * D].rearrange("p (t d) -> p t d", d=D),
                                                           WO_OUT, h, ALU.mult, ALU.add).then_inc(wo_added, 1)
                    if n in T_NORM:
                        part = T_NORM.index(n)
                        if part == 0:
                            dve.wait_ge(wo_added, 2 * b + 2)
                        ins = layer_norm(chain, tokens[:, bass.ds(NT * b, NT), :], xn, st2, mv2, ln_v2, ln_yw2, ln_t2, NT,
                                         (part,))
                        if part == LN_PARTS - 1:
                            ins.then_inc(xn2_there, 1)
                    if n == T_HI + 1:
                        dve.wait_ge(xn2_hi, b + 1)
                        split_rest(xn, xs2[par]).then_inc(xn2_ready, 1)
                        dve.wait_ge(xn2_ready, b + 1)
                    if n == T_X2T:
                        dve.wait_ge(x2T_ps, 2 * b + 1)
                        nc.vector.tensor_copy(x2T[:, 0:2, :], TA[:, 0:S].bitcast(FP16).rearrange("p (k s) -> p k s", k=2)
                                              ).then_inc(x2T_sb, 1)
                    if n == T_X2T + 2:
                        dve.wait_ge(x2T_ps, 2 * b + 2)
                        nc.vector.tensor_copy(x2T[:, 2, :], TA[:, 0:S // 2].bitcast(FP16)).then_inc(x2T_sb, 1)
                    if T_LOGIT <= n < T_LOGIT + 3:
                        whole = [P, NT, E]
                        sel1, chosen = rec[:, :, 0:E], rec[:, :, E:2 * E]

                        def pick_best(src, best):
                            chain.step(nc.vector.tensor_reduce(best[:, :], src, AX, ALU.max))
                            chain.step(nc.vector.tensor_tensor(key[:, :, :], src, over_rows(best[:, :], whole), ALU.is_equal))
                            chain.pause(nc.vector.tensor_tensor(key[:, :, :], key[:, :, :], over_tiles(first_wins[:, :], whole),
                                                                ALU.mult))

                        def pick_first(sel):
                            chain.resume()
                            chain.step(nc.vector.tensor_reduce(key_max[:, :], key[:, :, :], AX, ALU.max))
                            chain.pause(nc.vector.tensor_tensor(sel, key[:, :, :], over_rows(key_max[:, :], whole),
                                                                ALU.is_equal))

                    if n == T_LOGIT:
                        dve.wait_ge(logits_ps, b + 1)
                        nc.vector.tensor_scalar(lg[:, :, :], TA[:, 0:NT * E].rearrange("p (t e) -> p t e", t=NT),
                                                V_OUT, None, ALU.mult).then_inc(logits_sb, 1)
                        dve.wait_ge(logits_sb, b + 1)
                        pick_best(lg[:, :, :], top1)
                    if n == T_LOGIT + 1:
                        pick_first(sel1)
                        chain.resume()
                        chain.step(nc.vector.scalar_tensor_tensor(lg2[:, :, :], sel1, MASKED, lg[:, :, :], ALU.mult, ALU.add))
                        pick_best(lg2[:, :, :], top2)
                    if n == T_LOGIT + 2:
                        pick_first(sel2[:, :, :])
                        nc.vector.tensor_tensor(gap[:, :], top2[:, :], top1[:, :], ALU.subtract).then_inc(gap_ready, 1)
                        chain.resume()
                        nc.vector.tensor_tensor(chosen_bf[:, :, :], sel1, sel2[:, :, :], ALU.add).then_inc(chosen_ready, 1)
                        nc.vector.tensor_tensor(chosen, sel1, sel2[:, :, :], ALU.add)
                    if n == T_LOGIT + 4:
                        dve.wait_ge(gap_exped, b + 1)
                        chain.step(nc.vector.tensor_scalar(gap_sum[:, :], gap_exp[:, :], 1.0, None, ALU.add))
                        chain.step(nc.vector.reciprocal(rec[:, :, 2 * E], gap_sum[:, :]))
                        nc.vector.tensor_tensor(rec[:, :, 2 * E + 1], rec[:, :, 2 * E], gap_exp[:, :], ALU.mult)
                    if n == T_RANK:
                        whole = [P, NT, E]
                        old, new = running[:, par, :], running[:, 1 - par, :]
                        dve.wait_ge(ranks_ps, b + 1)
                        nc.vector.tensor_tensor(new, TA[:, NT * E:(NT + 1) * E], old, ALU.add)
                        nc.vector.tensor_tensor(pos[:, :, :], TA[:, 0:NT * E].rearrange("p (t e) -> p t e", t=NT),
                                                over_tiles(old, whole), ALU.add).then_inc(ranks_sb, 1)
                        dve.wait_ge(ranks_sb, b + 1)
                    if n == T_RANK + 1:
                        whole = [P, NT, E]
                        chain.step(nc.vector.tensor_scalar(late[:, :, :], pos[:, :, :], float(CAP), OUT_OF_BOUNDS,
                                                           ALU.is_ge, ALU.mult))
                        chain.step(nc.vector.tensor_tensor(pos[:, :, :], pos[:, :, :], late[:, :, :], ALU.add))
                        chain.pause(nc.vector.tensor_tensor(pos[:, :, :], pos[:, :, :],
                                                            over_tiles(expert_base[:, :], whole), ALU.add))
                    if n == T_RANK + 2:
                        chain.resume()
                        for k, sel in enumerate((rec[:, :, 0:E], sel2[:, :, :])):
                            chain.step(nc.vector.tensor_tensor(picked[:, :, :], pos[:, :, :], sel, ALU.mult))
                            chain.step(nc.vector.tensor_reduce(rec[:, :, 2 * E + 2 + k:2 * E + 3 + k], picked[:, :, :],
                                                               AX, ALU.add))
                        nc.vector.tensor_copy(slot_idx[par][:, :, :], rec[:, :, 2 * E + 2:REC]).then_inc(slots_ready, 1)
                        chain.step(nc.vector.tensor_copy(record[:, bass.ds(NT * b, NT), :], rec[:, :, :]))
                    if n == UNITS - 1:
                        assert chain.n == TAIL_STEPS, chain.n

                run(dve, unit, front, tail)
                norm_pair(B - 1, PAIRS - 1)
                rest_of_OT(B - 1, PAIRS - 1)
                for n in range(UNITS):
                    tail(B - 1, 1, n)
                nc.vector.tensor_reduce(most[:, :], running[:, B % 2, :], AX, ALU.max).then_inc(totals_ready, 1)
                dve.wait_ge(totals_ready, 1)

            @block.tensor
            def _(pe):
                pe.wait_ge(consts, 5)
                pe.wait_ge(zero_ready, 2)

                def transposes(dst, src, lo, hi):
                    for t in range(NT):
                        ins = nc.tensor.transpose(dst[0:hi - lo, t * P:t * P + P], src[:, t, lo:hi], ident[:, :])
                    return ins

                def transposes16(dst, src, k):
                    for t in range(NT):
                        ins = nc.tensor.transpose(dst[:, t * P:t * P + P], src[:, t, k * P:k * P + P], ident16[:, :])
                    return ins

                def front(b, par, n):
                    if n == F_XT:
                        if isinstance(b, int):
                            pe.wait_ge(x_in[par], 32 * (b // 2 + 1))
                        else:
                            pe.wait_ge(x_in[par], 16 * (b - par) + 32)
                        after(pe, v_sb[0], NT * b)
                        after(pe, v_sb[1], NT * b)
                        transposes(FA, xin[par], 0, P)
                        transposes(FB, xin[par], P, D).then_inc(xsT_ps, 1)
                    if n == F_SCORE:
                        pe.wait_ge(xsT_first_sb, b + 1)
                        pe.wait_ge(xsT_last_sb, b + 1)
                        for t in range(NT):
                            c = slice(t * P, t * P + P)
                            nc.tensor.matmul(FA[:, c], xsT_first[:, c], xsT_first[:, c], start=True, stop=False)
                            ins = nc.tensor.matmul(FA[:, c], xsT_last[:, c], xsT_last[:, c], start=False, stop=True)
                        ins.then_inc(tok_scores, 1)
                    if n == F_PT:
                        pe.wait_ge(tok_exp, NT * (b + 1))
                        transposes(FB, tok_p, 0, P).then_inc(tok_pT_ps, 1)
                    if n == F_MIX:
                        pe.wait_ge(tok_pT_sb, b + 1)
                        for t in range(NT):
                            dst = FA[:, t * D:t * D + D] if t < 2 else FB[:, 0:D]
                            ins = nc.tensor.matmul(dst, tok_pT[:, t, :], xin[par][:, t, :], start=True, stop=True)
                        ins.then_inc(tok_mixed, 1)
                    if n == F_XNT:
                        pe.wait_ge(xn_ready, b + 1)
                        for k in range(2):
                            transposes16(FA[:, k * S // 2:(k + 1) * S // 2].bitcast(FP16), xs, k)
                        transposes16(FB[:, 0:S // 2].bitcast(FP16), xs, 2).then_inc(xnT_ps, 1)
                    q = n - F_PROJ
                    if q >= 0:
                        dst = (FA, FB)[q % 2]
                        if isinstance(b, int) and b == 0 and q in (0, PAIRS, 2 * PAIRS):
                            pe.wait_ge(split, {0: 2, PAIRS: 4, 2 * PAIRS: SPLIT_STEPS}[q])
                        if q < 2:
                            pe.wait_ge(xT_sb[0], b + 1)
                            pe.wait_ge(xT_sb[1], b + 1)
                        elif q < 2 * PAIRS + 2:
                            pe.wait_ge(qk_sb, 2 * PAIRS * b + q - 1)
                        else:
                            pe.wait_ge(v_sb[q % 2], NT * b + (q - 2 * PAIRS) // 2)
                        if q < 2 * PAIRS:
                            m = q % PAIRS
                            ins = product((w_q, w_k)[q // PAIRS], slice(m * P, m * P + P), xT, slice(0, S), dst[:, 0:S],
                                          False)
                        else:
                            t, half = divmod(q - 2 * PAIRS, 2)
                            ins = product(w_v, slice(half * VH, half * VH + VH), xT, slice(t * P, t * P + P), dst[:, 0:VH],
                                          True)
                        ins.then_inc(proj_ps, 1)

                def score_unit(b, par, n):
                    h, t = divmod(n, NT)
                    m, rows = h // 2, slice(DK * (h % 2), DK * (h % 2) + DK)
                    g = UNITS * b + n
                    if n % PAIR == 0:
                        pe.wait_ge(qk_sb, 2 * PAIRS * b + PAIRS + m + 1)
                    after(pe, exp_done, g - 1)
                    dst = S_ps[n % 2]
                    for i, (q, k) in enumerate(((0, 0), (0, 1), (1, 0))):
                        nc.tensor.matmul(dst[:, 0:P * (t + 1)], QT[par][q][rows, m, t * P:t * P + P],
                                         KT[par][k][rows, m, 0:P * (t + 1)], start=(i == 0), stop=False)
                    nc.tensor.matmul(dst[:, t * P:t * P + P], ident_bf[:, :], causal[:, :], start=False,
                                     stop=True).then_inc(scores, 1)

                def attend_unit(b, par, n):
                    h, t = divmod(n, NT)
                    g = UNITS * b + n
                    if n == 0:
                        for k in range(2):
                            pe.wait_ge(v_sb[k], NT * (b + 1))
                    if n % PAIR == 0:
                        after(pe, normed, PAIRS * b + n // PAIR)
                    pe.wait_ge(probT_sb, g + 1)
                    for j in range(t + 1):
                        ins = nc.tensor.matmul(O_view[:, t, DK * (h % 2):DK * (h % 2) + DK],
                                               probT[:, n % NR, j * P:j * P + P], V[par][:, j, h * DK:h * DK + DK],
                                               start=(j == 0), stop=(j == t))
                    ins.then_inc(attended, 1)

                def transpose_O(b, m):
                    k = PAIRS * b + m
                    pe.wait_ge(normed, k + 1)
                    after(pe, OT_sb, k)
                    if m == 0:
                        after(pe, wo_added, 2 * b)
                    for n, used, count in ((T_X2T, x2T_sb, 2 * b), (T_LOGIT, logits_sb, b), (T_RANK, ranks_sb, b)):
                        if m == pairs_copied(n):
                            after(pe, used, count)
                    for t in range(NT):
                        ins = nc.tensor.transpose(TA[:, t * P:t * P + P], O_sb[:, m % 2, t, :], ident[:, :])
                    ins.then_inc(OT_ps, 1)

                def unit(b, par, n, first, last):
                    g = UNITS * b + n
                    t = n % NT
                    if first and n == 0:
                        score_unit(b, par, 0)
                        score_unit(b, par, 1)
                    pe.wait_ge(exp_done, g + 1)
                    if n >= 2 or not first:
                        pe.wait_ge(probT_sb, g - 1)
                    for j in range(t + 1):
                        ins = nc.tensor.transpose(T_ps[n % 2][:, j * P:j * P + P], prob[:, n % NR, j * P:j * P + P],
                                                  ident[:, :])
                    ins.then_inc(probT_ps, 1)
                    if n + 2 < UNITS:
                        score_unit(b, par, n + 2)
                    elif not last:
                        score_unit(b + 1, 1 - par, n + 2 - UNITS)
                    if n % PAIR == 2:
                        attend_unit(b, par, n - 2)
                    if n == 0 and not first:
                        attend_unit(b - 1, 1 - par, UNITS - 1)
                    if n and n % PAIR != 1:
                        attend_unit(b, par, n - 1)
                    if n % PAIR == 2:
                        if n > 2:
                            transpose_O(b, n // PAIR - 1)
                        elif not first:
                            transpose_O(b - 1, PAIRS - 1)

                def tail(b, par, n, final=False):
                    for use, tiles in enumerate((range(0, 2), range(2, NT))):
                        if n == T_WO + use:
                            pe.wait_ge(OT_sb, PAIRS * (b + 1))
                            if use:
                                pe.wait_ge(wo_added, 2 * b + use)
                            for i, t in enumerate(tiles):
                                dst = TA[:, i * D:i * D + D]
                                for m in range(PAIRS):
                                    o_hi, o_lo = (o[:, m, t * P:t * P + P] for o in (OT_hi, OT_lo))
                                    nc.tensor.matmul(dst, o_hi, wo_hi[:, m, :], start=(m == 0), stop=False)
                                    nc.tensor.matmul(dst, o_hi, wo_lo[:, m, :], start=False, stop=False)
                                    ins = nc.tensor.matmul(dst, o_lo, wo_hi[:, m, :], start=False, stop=(m == PAIRS - 1))
                            ins.then_inc(wo_ps, 1)
                    if n == T_X2T:
                        pe.wait_ge(xn2_ready, b + 1)
                        if not final:
                            pe.wait_ge(OT_sb, PAIRS * (b + 1) + pairs_copied(T_X2T))
                        for k in range(2):
                            ins = transposes16(TA[:, k * S // 2:(k + 1) * S // 2].bitcast(FP16), xs2[par], k)
                        ins.then_inc(x2T_ps, 1)
                    if n == T_X2T + 2:
                        pe.wait_ge(x2T_sb, 2 * b + 1)
                        transposes16(TA[:, 0:S // 2].bitcast(FP16), xs2[par], 2).then_inc(x2T_ps, 1)
                    if n == T_LOGIT:
                        pe.wait_ge(x2T_sb, 2 * b + 2)
                        if not final:
                            pe.wait_ge(OT_sb, PAIRS * (b + 1) + pairs_copied(T_LOGIT))
                        for t in range(NT):
                            c = slice(t * P, t * P + P)
                            ins = product(w_g, slice(0, E), x2T, c, TA[:, t * E:t * E + E], True)
                        ins.then_inc(logits_ps, 1)
                    if n == T_RANK:
                        pe.wait_ge(chosen_ready, b + 1)
                        if not final:
                            pe.wait_ge(OT_sb, PAIRS * (b + 1) + pairs_copied(T_RANK))
                        for t in range(NT + 1):
                            dst = TA[:, t * E:t * E + E]
                            for k in range(t):
                                ins = nc.tensor.matmul(dst, ones_bf[:, :], chosen_bf[:, k, :], start=(k == 0),
                                                       stop=(t == NT and k == t - 1))
                            if t < NT:
                                ins = nc.tensor.matmul(dst, before[:, :], chosen_bf[:, t, :], start=(t == 0), stop=True)
                        ins.then_inc(ranks_ps, 1)

                run(pe, unit, front, tail)
                attend_unit(B - 1, 1, UNITS - 1)
                transpose_O(B - 1, PAIRS - 1)
                for n in range(UNITS):
                    tail(B - 1, 1, n, final=True)

        part = ExitStack()
        with part:
            def sa(name, shape, dt=FP32):
                return sb(name, shape, dt, part)

            def ps(name, shape, dt=FP32):
                return part.enter_context(nc.psum_tensor(name, shape, dt))

            HALF = TILES // 2
            assert HALF * E <= 512 and TILES <= 256
            priority = sa("priority", [P, TILES])
            threshold, candidate = sa("threshold", [P, E]), sa("candidate", [P, E])
            step_size = sa("step_size", [P, 1])
            hits = sa("hits", [P, TILES, E])
            hits_f = sa("hits_f", [P, E])
            hits_bf = sa("hits_bf", [P, E], BF16)
            raised = sa("raised", [P, E])
            above, ties = sa("above", [P, TILES, E]), sa("ties", [P, TILES, E])
            marked = sa("marked", [P, TILES, E], BF16)
            column, rank = sa("column", [P, TILES, E]), sa("rank", [P, TILES, E])
            ones_row = sa("ones_row", [P, TILES])
            places = sa("places", [P, TILES])
            second = sa("second", [P, TILES, E])
            scatter_to = sa("scatter_to", [P, TILES, 2])
            r_st, r_mv = sa("r_st", [P, 1, 6]), sa("r_mv", [P, 1, 2])
            r_v, r_yw, r_t = sa("r_v", [P, 1]), sa("r_yw", [P, 2, 1]), sa("r_t", [P, 1])
            r_tok, r_x, r_rows = sa("r_tok", [P, 1, D]), sa("r_x", [P, 1, D]), sa("r_rows", [P, 1, 2 * D], FP16)
            r_idx = sa("r_idx", [P, 1, 2], U32)
            total_ps = ps("total_ps", [P, 512])
            before_ps = [ps(f"before_ps{i}", [P, 512]) for i in range(2)]
            column_ps = [ps(f"column_ps{i}", [P, 512]) for i in range(2)]
            r_chain, l_chain = sem("r_chain"), sem("l_chain")
            counted, totals, marks, ranked = sem("counted"), sem("totals"), sem("marks"), sem("ranked")
            r_ready, r_free, rescattered = sem("r_ready"), sem("r_free"), sem("rescattered")
            LOOP_CHAIN = 8
            TILE_CHAIN = 3 + LN_STEPS

            block = part.enter_context(nc.Block())

            @block.vector
            def _(dve):
                with dve.If(dve.value_load(most[0:1, 0:1], min_val=0, max_val=T) > CAP):
                    whole = [P, TILES, E]
                    sel1, chosen = record[:, :, 0:E], record[:, :, E:2 * E]
                    chain = Chain(dve, r_chain, 0)
                    nc.vector.memset(threshold[:, :], 0.0)
                    nc.vector.memset(ones_row[:, :], 1.0)
                    chain.step(nc.vector.memset(step_size[:, :], float(1 << 24)))
                    chain.step(nc.vector.tensor_scalar(priority[:, :], record[:, :, 2 * E], float(1 << 24), None, ALU.mult))
                    with dve.Fori(0, SEARCH_STEPS) as k:
                        loop = Chain(dve, l_chain, LOOP_CHAIN * k)
                        loop.step(nc.vector.tensor_scalar(candidate[:, :], threshold[:, :], step_size[:, 0:1], None, ALU.add))
                        loop.step(nc.vector.tensor_tensor(hits[:, :, :], over_rows(priority[:, :], whole),
                                                          over_tiles(candidate[:, :], whole), ALU.is_ge))
                        loop.step(nc.vector.tensor_tensor(hits[:, :, :], hits[:, :, :], chosen, ALU.mult))
                        loop.step(nc.vector.tensor_reduce(hits_f[:, :], hits[:, :, :].rearrange("p t e -> p e t"), AX,
                                                          ALU.add))
                        nc.vector.tensor_copy(hits_bf[:, :], hits_f[:, :]).then_inc(counted, 1)
                        dve.wait_ge(totals, k + 1)
                        loop.step(nc.vector.tensor_scalar(raised[:, :], total_ps[:, 0:E], float(CAP), None, ALU.is_ge))
                        loop.step(nc.vector.tensor_scalar(raised[:, :], raised[:, :], step_size[:, 0:1], None, ALU.mult))
                        loop.step(nc.vector.tensor_tensor(threshold[:, :], threshold[:, :], raised[:, :], ALU.add))
                        loop.step(nc.vector.tensor_scalar(step_size[:, :], step_size[:, :], 0.5, None, ALU.mult))
                        assert loop.n == LOOP_CHAIN
                    for dst, op in ((above, ALU.is_gt), (ties, ALU.is_equal)):
                        chain.step(nc.vector.tensor_tensor(dst[:, :, :], over_rows(priority[:, :], whole),
                                                           over_tiles(threshold[:, :], whole), op))
                        chain.step(nc.vector.tensor_tensor(dst[:, :, :], dst[:, :, :], chosen, ALU.mult))
                    chain.step(nc.vector.tensor_reduce(hits_f[:, :], above[:, :, :].rearrange("p t e -> p e t"), AX, ALU.add))
                    nc.vector.tensor_copy(hits_bf[:, :], hits_f[:, :]).then_inc(counted, 1)
                    dve.wait_ge(totals, SEARCH_STEPS + 1)
                    chain.step(nc.vector.tensor_scalar(candidate[:, :], total_ps[:, 0:E], -1.0, float(CAP), ALU.mult, ALU.add))

                    def rank_of(marks_f, n):
                        nc.vector.tensor_copy(marked[:, :, :], marks_f).then_inc(marks, 1)
                        dve.wait_ge(ranked, n)
                        for i in range(2):
                            c = slice(i * HALF, (i + 1) * HALF)
                            nc.vector.tensor_copy(column[:, c, :], column_ps[i][:, 0:HALF * E]
                                                  .rearrange("p (t e) -> p t e", e=E))
                            ins = nc.vector.tensor_copy(rank[:, c, :], before_ps[i][:, 0:HALF * E]
                                                        .rearrange("p (t e) -> p t e", e=E))
                        chain.step(ins)
                        chain.step(nc.vector.tensor_tensor(rank[:, :, :], rank[:, :, :], column[:, :, :], ALU.subtract))
                        for e in range(E):
                            ins = nc.vector.tensor_tensor_scan(hits[:, :, e], ones_row[:, :], column[:, :, e], 0.0,
                                                               ALU.mult, ALU.add)
                        chain.step(ins)
                        chain.step(nc.vector.tensor_tensor(rank[:, :, :], rank[:, :, :], hits[:, :, :], ALU.add))

                    rank_of(ties[:, :, :], 1)
                    chain.step(nc.vector.tensor_tensor(rank[:, :, :], rank[:, :, :], over_tiles(candidate[:, :], whole),
                                                       ALU.is_lt))
                    chain.step(nc.vector.tensor_tensor(ties[:, :, :], ties[:, :, :], rank[:, :, :], ALU.mult))
                    chain.step(nc.vector.tensor_tensor(above[:, :, :], above[:, :, :], ties[:, :, :], ALU.add))
                    rank_of(above[:, :, :], 2)
                    chain.step(nc.vector.tensor_tensor(rank[:, :, :], rank[:, :, :], over_tiles(expert_base[:, :], whole),
                                                       ALU.add))
                    chain.step(nc.vector.tensor_tensor(second[:, :, :], chosen, sel1, ALU.subtract))
                    for k, sel in enumerate((sel1, second[:, :, :])):
                        slot, weight = record[:, :, 2 * E + 2 + k], record[:, :, 2 * E + k]
                        chain.step(nc.vector.tensor_tensor(hits[:, :, :], sel, above[:, :, :], ALU.mult))
                        chain.step(nc.vector.tensor_reduce(places[:, :], hits[:, :, :], AX, ALU.add))
                        chain.step(nc.vector.tensor_tensor(weight, weight, places[:, :], ALU.mult))
                        chain.step(nc.vector.tensor_tensor(hits[:, :, :], hits[:, :, :], rank[:, :, :], ALU.mult))
                        chain.step(nc.vector.tensor_reduce(slot, hits[:, :, :], AX, ALU.add))
                        chain.step(nc.vector.tensor_scalar(places[:, :], places[:, :], -OUT_OF_BOUNDS, OUT_OF_BOUNDS,
                                                           ALU.mult, ALU.add))
                        chain.step(nc.vector.tensor_tensor(scatter_to[:, :, k], slot, places[:, :], ALU.add))
                    with dve.Fori(0, TILES) as c:
                        tile_chain = Chain(dve, l_chain, LOOP_CHAIN * SEARCH_STEPS + TILE_CHAIN * c)
                        dve.wait_ge(r_free, c + 1)
                        tile_chain.step(nc.vector.tensor_copy(r_tok[:, :, :], tokens[:, bass.ds(c, 1), :]))
                        nc.vector.tensor_copy(r_idx[:, :, :], scatter_to[:, bass.ds(c, 1), :])
                        tile_chain.step(layer_norm(tile_chain, r_tok, r_x, r_st, r_mv, r_v, r_yw, r_t, 1))
                        tile_chain.step(nc.vector.tensor_copy(r_rows[:, :, 0:D], r_x[:, :, :]))
                        split_rest(r_x, r_rows).then_inc(r_ready, 1)
                        assert tile_chain.n == TILE_CHAIN

            @block.tensor
            def _(pe):
                with pe.If(pe.value_load(most[0:1, 0:1], min_val=0, max_val=T) > CAP):
                    with pe.Fori(0, SEARCH_STEPS + 1) as k:
                        pe.wait_ge(counted, k + 1)
                        nc.tensor.matmul(total_ps[:, 0:E], ones_bf[:, :], hits_bf[:, :], start=True, stop=True
                                         ).then_inc(totals, 1)
                    with pe.Fori(0, 2) as n:
                        pe.wait_ge(marks, n + 1)
                        for i in range(2):
                            src = marked[:, i * HALF:(i + 1) * HALF, :].rearrange("p t e -> p (t e)")
                            nc.tensor.matmul(before_ps[i][:, 0:HALF * E], before[:, :], src, start=True, stop=True)
                            ins = nc.tensor.matmul(column_ps[i][:, 0:HALF * E], ones_bf[:, :], src, start=True, stop=True)
                        ins.then_inc(ranked, 1)

            @block.gpsimd
            def _(pool):
                with pool.If(pool.value_load(most[0:1, 0:1], min_val=0, max_val=T) > CAP):
                    pool.sem_inc(r_free, 1)
                    with pool.Fori(0, TILES) as c:
                        pool.wait_ge(r_ready, c + 1)
                        alone(pool, spare)
                        for k in range(2):
                            pool.indirect_dma_start(slots_dram[:, :], bass.IndirectOffsetOnAxis(r_idx[:, 0, k:k + 1], 0),
                                                    r_rows[:, 0, :], None, bounds_check=E * CAPP - 1, oob_is_err=False
                                                    ).then_inc(rescattered, 16)
                        pool.wait_ge(rescattered, 32 * c + 32)
                        pool.sem_inc(r_free, 1)

        part = ExitStack()
        with part:
            def sa(name, shape, dt=FP32):
                return sb(name, shape, dt, part)

            def ps(name, shape, dt=FP32):
                return part.enter_context(nc.psum_tensor(name, shape, dt))

            raw1, raw2 = sa("raw1", [P, 2, HID]), sa("raw2", [P, HT, D])
            w1_sb = [(sa(f"w1_hi{i}", [P, HID], FP16), sa(f"w1_lo{i}", [P, HID], FP16),
                      sa(f"w1_twice{i}", [P, HID], FP16), sa(f"w1_last{i}", [D1, HID], FP16)) for i in range(2)]
            w2_sb = [[sa(f"w2_{k}{i}", [P, HT, D], FP16) for k in ("hi", "lo")] for i in range(2)]
            b1_all, b2_all = sa("b1_all", [P, E, HT]), sa("b2_all", [P, E, D])
            b1_sb = [sa(f"b1_sb{i}", [P, HT]) for i in range(2)]
            b2_sb = [sa(f"b2_sb{i}", [P, D]) for i in range(2)]
            rows = [sa(f"rows{i}", [P, NT, 2 * D], FP16) for i in range(2)]
            rT = [sa(f"rT{i}", [P, 3, GROUP], FP16) for i in range(2)]
            hidden = sa("hidden", [P, HT, GROUP])
            hT = [sa(f"hT_{k}", [P, HT, GROUP], FP16) for k in ("hi", "lo")]
            ex_out = [sa(f"ex_out{i}", [P, NT, D]) for i in range(2)]
            RG = 4
            assert TILES % RG == 0
            pick_w = sa("pick_w", [P, RG, 2])
            picks = [[sa(f"pick{k}_{i}", [P, D]) for i in range(RG)] for k in range(2)]
            pick_idx = sa("pick_idx", [P, RG, 2], U32)
            half = sa("half", [P, RG, D])
            result = [sa(f"result{i}", [P, D]) for i in range(RG)]

            HB = 3
            ACT_HI = HT // 2
            h_ps = [ps(f"h_ps{i}", [P, 512]) for i in range(HB)]
            rT_ps = [ps(f"rT_ps{i}", [P, 512]) for i in range(2)]
            ex_ps = [ps(f"ex_ps{i}", [P, 512]) for i in range(2)]

            raw_in1, raw_in2, b_in, w_ready, w_chain = sem("raw_in1"), sem("raw_in2"), sem("b_in"), sem("w_ready"), sem("w_chain")
            hidden_hi, hidden_split = [sem("hidden_hi_act"), sem("hidden_hi_dve")], sem("hidden_split")
            rows_in = [sem("rows_in0"), sem("rows_in1")]
            rT_ready, rT_sb = sem("rT_ready"), [sem("rT_sb_dve"), sem("rT_sb_act")]
            hidden_ps, hidden_sb = sem("hidden_ps"), sem("hidden_sb")
            ex_ready, ex_added = sem("ex_ready"), sem("ex_added")
            stored = [sem("stored0"), sem("stored1")]
            idx_ready = sem("idx_ready")
            pick_in = [sem(f"pick_in{i}") for i in range(RG)]
            half_sum, result_ready = sem("half_sum"), sem("result_ready")
            out_stored = [sem(f"out_stored{i}") for i in range(RG)]

            def each_step(eng, step, at_expert=None):
                def expert(e, ep):
                    if at_expert:
                        at_expert(e, ep)
                    with eng.Fori(0, GPE // 2) as j:
                        for par in range(2):
                            step(GPE * e + 2 * j + par, par, ep)

                with eng.Fori(0, E // 2) as pair:
                    for ep in range(2):
                        expert(2 * pair + ep, ep)

            def load_weights(eng, e, done):
                first = w1[bass.ds(e, 1), 0:P, :].rearrange("o m k -> (o m) k")
                last = w1[bass.ds(e, 1), P:D, :].rearrange("o m k -> (o m) k")
                for dst, src in (
                    (raw1[:, 0, :], first), (raw1[0:D1, 1, :], last), (raw1[D1:P, 1, :], last),
                    (raw2[:, :, :], w2[bass.ds(e, 1), :, :].rearrange("o (c p) d -> (o p) c d", p=P)),
                ):
                    eng.dma_start(dst, src, allow_slow_non_contiguous=True).then_inc(done, 16)

            def split_expert(eng, ops, e, ep):
                if isinstance(e, int) and e == 0:
                    eng.wait_ge(raw_in1, 64)
                else:
                    eng.wait_ge(raw_in2, 64 * e)
                chain = Chain(eng, w_chain, 2 * e)
                w_hi, w_lo, w_twice, w_last = (m[:, :] for m in w1_sb[ep])
                w2_hi, w2_lo = (m[:, :, :] for m in w2_sb[ep])
                first, last, second = raw1[:, 0, :], raw1[:, 1, :], raw2[:, :, :]
                alone(eng, spare)
                for raw in (first, last, second):
                    ins = ops.tensor_scalar(raw, raw, W_SCALE, None, ALU.mult)
                chain.step(ins)
                alone(eng, spare)
                for hi, raw in ((w_hi, first), (w_twice, last), (w2_hi, second)):
                    ins = ops.tensor_copy(hi, raw)
                chain.step(ins)
                for lo, raw, hi in ((w_lo, first, w_hi), (w_last, last[0:D1], w_twice[0:D1]), (w2_lo, second, w2_hi)):
                    ops.tensor_tensor(lo, raw, hi, ALU.subtract)
                eng.wait_ge(b_in, 32)
                alone(eng, spare)
                ops.tensor_copy(b1_sb[ep][:, :], b1_all[:, bass.ds(e, 1), :].rearrange("p o c -> p (o c)"))
                ops.tensor_copy(b2_sb[ep][:, :], b2_all[:, bass.ds(e, 1), :].rearrange("p o c -> p (o c)")
                                ).then_inc(w_ready, 1)

            block = part.enter_context(nc.Block())

            def slot_rows(table, g):
                return table[bass.ds(g * GROUP, GROUP), :].rearrange("(p r) d -> p r d", p=P)

            @block.sync
            def _(sp):
                for s in stored + out_stored:
                    sp.sem_inc(s, 1)
                load_weights(sp, 0, raw_in1)
                sp.dma_start(rows[0][:, :, :], slot_rows(slots_dram, 0)).then_inc(rows_in[0], 16)

                def step(g, par, ep):
                    sp.wait_ge(rT_ready, g + 1)
                    sp.dma_start(rows[1 - par][:, :, :], slot_rows(slots_dram, g + 1)).then_inc(rows_in[1 - par], 16)
                    sp.wait_ge(ex_added, g + 2)
                    sp.dma_start(slot_rows(expert_dram, g), ex_out[par][:, :, :]).then_inc(stored[par], 16)

                each_step(sp, step)
                sp.wait_ge(rows_in[0], 16 * (E * GPE // 2 + 1))
                out_rows = out.rearrange("b s d -> (b s) d")
                with sp.Fori(0, TILES // RG) as k:
                    for i in range(RG):
                        sp.wait_ge(result_ready, RG * k + i + 1)
                        sp.dma_start(out_rows[bass.ds((RG * k + i) * P, P), :], result[i][:, :]
                                     ).then_inc(out_stored[i], 16)
                for i in range(RG):
                    sp.wait_ge(out_stored[i], 16 * (TILES // RG) + 1)

            @block.gpsimd
            def _(pool):
                pool.dma_start(b1_all[:, :, :], b1.rearrange("e (c p) -> p e c", p=P), allow_slow_non_contiguous=True
                               ).then_inc(b_in, 16)
                pool.dma_start(b2_all[:, :, :].rearrange("p e d -> p (e d)"),
                               b2.rearrange("e d -> (e d)").rearrange("(o n) -> o n", o=1).to_broadcast([P, E * D]),
                               allow_slow_non_contiguous=True).then_inc(b_in, 16)
                pool.wait_ge(w_ready, 1)
                load_weights(pool, 1, raw_in2)
                split_expert(pool, nc.gpsimd, 1, 1)

                def next_weights(e, ep):
                    pool.wait_ge(w_ready, e)
                    alone(pool, spare)
                    load_weights(pool, e, raw_in2)
                    pool.wait_ge(ex_added, GPE * (e - 1) + 1)
                    split_expert(pool, nc.gpsimd, e, ep)

                with pool.Fori(1, E // 2) as pair:
                    for ep in range(2):
                        next_weights(2 * pair + ep, ep)
                for par in range(2):
                    pool.wait_ge(stored[par], 16 * (E * GPE // 2) + 1)
                with pool.Fori(0, TILES // RG) as k:
                    for i in range(RG):
                        pool.wait_ge(idx_ready, RG * k + i + 1)
                        alone(pool, spare)
                        for c in range(2):
                            pool.indirect_dma_start(picks[c][i][:, :], None, expert_dram[:, :],
                                                    bass.IndirectOffsetOnAxis(pick_idx[:, i, c:c + 1], 0),
                                                    bounds_check=E * CAPP - 1, oob_is_err=False
                                                    ).then_inc(pick_in[i], 16)

            @block.scalar
            def _(act):
                def move_last(par):
                    nc.scalar.activation(rT[par][:, 2, :], rT_ps[1][:, 0:GROUP // 2].bitcast(FP16), ACT.Copy
                                         ).then_inc(rT_sb[1], 1)

                act.wait_ge(rT_ready, 1)
                move_last(0)

                def at_expert(e, ep):
                    act.wait_ge(w_ready, e + 1)
                    alone(act, spare)

                def step(g, par, ep):
                    for m in range(HT):
                        act.wait_ge(hidden_ps, HT * g + m + 1)
                        nc.scalar.activation(hidden[:, m, :], h_ps[m % HB][:, 0:GROUP], ACT.Gelu,
                                             bias=b1_sb[ep][:, m:m + 1], scale=H_OUT).then_inc(hidden_sb, 1)
                        if 1 <= m <= ACT_HI:
                            act.wait_ge(hidden_sb, HB + HT * g + m)
                            nc.scalar.activation(hT[0][:, m - 1, :], hidden[:, m - 1, :], ACT.Copy, scale=H_SCALE
                                                 ).then_inc(hidden_hi[0], 1)
                    act.wait_ge(rT_ready, g + 2)
                    move_last(1 - par)

                each_step(act, step, at_expert)

            @block.vector
            def _(dve):
                dve.sem_inc(hidden_sb, HB)
                dve.sem_inc(ex_added, 1)

                def move_first(par):
                    nc.vector.tensor_copy(rT[par][:, 0:2, :], rT_ps[0][:, 0:GROUP].bitcast(FP16)
                                          .rearrange("p (k n) -> p k n", k=2)).then_inc(rT_sb[0], 1)

                split_expert(dve, nc.vector, 0, 0)
                dve.wait_ge(rT_ready, 1)
                move_first(0)

                def at_expert(e, ep):
                    dve.wait_ge(w_ready, e + 1)
                    alone(dve, spare)

                def step(g, par, ep):
                    for m in range(HT):
                        dve.wait_ge(hidden_sb, HB + HT * g + m + 1)
                        if m < ACT_HI:
                            dve.wait_ge(hidden_hi[0], ACT_HI * g + m + 1)
                        else:
                            nc.vector.tensor_scalar(hT[0][:, m, :], hidden[:, m, :], H_SCALE, None, ALU.mult
                                                    ).then_inc(hidden_hi[1], 1)
                            dve.wait_ge(hidden_hi[1], (HT - ACT_HI) * g + m - ACT_HI + 1)
                        nc.vector.scalar_tensor_tensor(hT[1][:, m, :], hidden[:, m, :], H_SCALE, hT[0][:, m, :],
                                                       ALU.mult, ALU.subtract).then_inc(hidden_split, 1)
                    dve.wait_ge(rT_ready, g + 2)
                    move_first(1 - par)
                    dve.wait_ge(ex_ready, g + 1)
                    dve.wait_ge(stored[par], 8 * (g - par) + 1)
                    for lo, hi in ((0, 2), (2, NT)):
                        ins = nc.vector.scalar_tensor_tensor(
                            ex_out[par][:, lo:hi, :], ex_ps[lo // 2][:, 0:(hi - lo) * D].rearrange("p (t d) -> p t d", d=D),
                            EX_OUT, over_tiles(b2_sb[ep][:, :], [P, hi - lo, D]), ALU.mult, ALU.add)
                    ins.then_inc(ex_added, 1)

                each_step(dve, step, at_expert)

                def fetch(c, i):
                    nc.vector.tensor_copy(pick_w[:, i:i + 1, :], record[:, bass.ds(c, 1), 2 * E:2 * E + 2])
                    nc.vector.tensor_copy(pick_idx[:, i:i + 1, :], record[:, bass.ds(c, 1), 2 * E + 2:REC]
                                          ).then_inc(idx_ready, 1)

                def combine(k, i):
                    c = RG * k + i
                    dve.wait_ge(pick_in[i], 32 * k + 32)
                    dve.wait_ge(idx_ready, c + 1)
                    nc.vector.scalar_tensor_tensor(half[:, i:i + 1, :], picks[0][i][:, :].rearrange("p (o d) -> p o d", o=1),
                                                   pick_w[:, i, 0:1], tokens[:, bass.ds(c, 1), :], ALU.mult, ALU.add
                                                   ).then_inc(half_sum, 1)
                    dve.wait_ge(half_sum, c + 1)
                    dve.wait_ge(out_stored[i], 16 * k + 1)
                    nc.vector.scalar_tensor_tensor(result[i][:, :], picks[1][i][:, :], pick_w[:, i, 1:2], half[:, i, :],
                                                   ALU.mult, ALU.add).then_inc(result_ready, 1)

                for i in range(RG):
                    fetch(i, i)
                with dve.Fori(0, TILES // RG - 1) as k:
                    for i in range(RG):
                        combine(k, i)
                        dve.wait_ge(result_ready, RG * k + i + 1)
                        fetch(RG * k + i + RG, i)
                for i in range(RG):
                    combine(TILES // RG - 1, i)

            @block.tensor
            def _(pe):
                def transposes(par):
                    for k in range(3):
                        dst = rT_ps[k // 2][:, 0:GROUP].bitcast(FP16)
                        for r in range(NT):
                            c = (k % 2) * GROUP + r * P
                            ins = nc.tensor.transpose(dst[:, c:c + P], rows[par][:, r, k * P:k * P + P], ident16[:, :])
                    ins.then_inc(rT_ready, 1)

                pe.wait_ge(rows_in[0], 16)
                transposes(0)

                def at_expert(e, ep):
                    pe.wait_ge(w_ready, e + 1)
                    alone(pe, spare)

                def step(g, par, ep):
                    for k in range(2):
                        pe.wait_ge(rT_sb[k], g + 1)
                    for m in range(HT):
                        pe.wait_ge(hidden_sb, HT * g + m + 1)
                        product([w[:, :] for w in w1_sb[ep]], slice(m * P, m * P + P), rT[par], slice(0, GROUP),
                                h_ps[m % HB][:, 0:GROUP], False).then_inc(hidden_ps, 1)
                    pe.wait_ge(rows_in[1 - par], 8 * (g - par) + 16 + 16 * par)
                    transposes(1 - par)
                    pe.wait_ge(ex_added, g + 1)
                    w2_hi, w2_lo = w2_sb[ep]
                    turns = [(r, m) for m in range(HT) for r in (0, NT - 1)] + [(1, m) for m in range(HT)]
                    for r, m in turns:
                        dst = ex_ps[r // 2][:, (r % 2) * D:(r % 2) * D + D]
                        if r == 0:
                            pe.wait_ge(hidden_split, HT * g + m + 1)
                        h_hi, h_lo = (h[:, m, r * P:r * P + P] for h in hT)
                        nc.tensor.matmul(dst, h_hi, w2_hi[:, m, :], start=(m == 0), stop=False)
                        nc.tensor.matmul(dst, h_hi, w2_lo[:, m, :], start=False, stop=False)
                        ins = nc.tensor.matmul(dst, h_lo, w2_hi[:, m, :], start=False, stop=(m == HT - 1))
                    ins.then_inc(ex_ready, 1)

                each_step(pe, step, at_expert)


_INS = ["x", "L0_attn_W_Q", "L0_attn_W_K", "L0_attn_W_V", "L0_attn_W_O", "L0_ffn_Wg", "L0_ffn_W1", "L0_ffn_b1",
        "L0_ffn_W2", "L0_ffn_b2"]


def kernel(**inputs):
    import numpy as np
    import concourse.bacc as bacc
    from concourse.bass_utils import run_bass_kernel_spmd

    nc = bacc.Bacc("TRN2", target_bir_lowering=False, num_devices=1)
    arrays, args = {}, []
    for name in _INS:
        a = np.ascontiguousarray(inputs[name])
        arrays[f"in_{name}"] = a
        args.append(nc.dram_tensor(f"in_{name}", a.shape, mybir.dt.from_np(a.dtype), kind="ExternalInput").ap())
    batches, rows, width = inputs["x"].shape
    span = SEG * DILATION
    shape = (batches, -(-rows // span) * SEG, width)
    out = nc.dram_tensor("out_dram", shape, FP32, kind="ExternalOutput").ap()
    audio_tower_kernel(nc, *args, out)
    r = run_bass_kernel_spmd(nc, [arrays], core_ids=[0])
    return r.results[0]["out_dram"]
```
